# Optimizing a Trainium2 kernel written in Bass

```python
import numpy as np
import jax
import jax.numpy as jnp

def _softmax(x, axis=-1):
    return jax.nn.softmax(x, axis=axis)

def _gelu(x):
    return jax.nn.gelu(x, approximate=True)

def _silu(x):
    return jax.nn.silu(x)

def _sigmoid(x):
    return jax.nn.sigmoid(x)

def _layernorm(x, axis=-1, eps=1e-05):
    m = jnp.mean(x, axis=axis, keepdims=True)
    v = jnp.var(x, axis=axis, keepdims=True)
    return (x - m) / jnp.sqrt(v + eps)

def _scatter_add(tgt, idx, src, axis=0):
    return tgt.at[idx].add(src)

def _segment_sum(src, seg, n):
    return jax.ops.segment_sum(src, seg, n)
kernel_name = 'mk_cond_seq_d2_seqx_r4_a5a04f'

def setup_inputs(seed: int=0):
    np.random.seed(seed)
    _w = jnp.asarray

    def _rec_inputs():
        import jax
        import jax.numpy as jnp
        _rk = jax.random.key(seed)
        x = -0.0002928 + 1 * jax.random.normal(jax.random.fold_in(_rk, 1), (4, 512, 256), jnp.float32)
        _lenS = 512 - jax.random.randint(jax.random.fold_in(_rk, 7), (4,), 0, max(1, 512 // 4) + 1, jnp.int32)
        _lenS2 = 512 - jax.random.randint(jax.random.fold_in(_rk, 8), (4,), 0, max(1, 512 // 4) + 1, jnp.int32)
        cond_1024 = 0.00786388 + 1.0143 * jax.random.normal(jax.random.fold_in(_rk, 11), (4, 256), jnp.float32)
        _validS = jnp.arange(512)[None, :] < _lenS[:, None]
        _validS2 = jnp.arange(512)[None, :] < _lenS2[:, None]
        _causal = jnp.tril(jnp.ones((512, 512), dtype=bool))
        mask_BxS_bf1 = jnp.ones((4, 512), dtype=bool)
        return (x, cond_1024, mask_BxS_bf1)
    x, cond_1024, mask_BxS_bf1 = _rec_inputs()

    def _L0_cond_setup():
        import jax, jax.numpy as jnp
        import numpy as np
        EPS = 1e-05
        NEG_INF = -1e+30

        def layer_norm(x, g, b):
            mu = jnp.mean(x, axis=-1, keepdims=True)
            var = jnp.var(x, axis=-1, keepdims=True)
            return (x - mu) * jax.lax.rsqrt(var + EPS) * g + b
        B, L, D, H, F = (2, 512, 256, 16, 1024)
        key = jax.random.key(seed)
        ks = jax.random.split(key, 12)
        s = 0.02
        return {'x': jax.random.normal(ks[0], (B, L, D), jnp.float32), 'torus_dist': jax.random.uniform(ks[1], (1, L, L), jnp.float32), 'time_emb': jax.random.normal(ks[2], (B, D), jnp.float32), 'mask': jnp.ones((B, L), dtype=bool), 'ln1_g': jnp.ones((D,), jnp.float32), 'ln1_b': jnp.zeros((D,), jnp.float32), 'Wqkv': jax.random.normal(ks[3], (D, 3 * D), jnp.float32) * s, 'Wout': jax.random.normal(ks[4], (D, D), jnp.float32) * s, 'torus_scale': jnp.full((H,), 0.1, jnp.float32), 'ln2_g': jnp.ones((D,), jnp.float32), 'ln2_b': jnp.zeros((D,), jnp.float32), 'W1': jax.random.normal(ks[5], (D, F), jnp.float32) * s, 'b1': jnp.zeros((F,), jnp.float32), 'W2': jax.random.normal(ks[6], (F, D), jnp.float32) * s, 'b2': jnp.zeros((D,), jnp.float32), 'Wt': jax.random.normal(ks[7], (D, 2 * D), jnp.float32) * s, 'bt': jnp.zeros((2 * D,), jnp.float32)}
    _L0_cond_all = _L0_cond_setup()
    _L0_cond_in = {k: v for k, v in _L0_cond_all.items() if k in ('torus_dist', 'ln1_g', 'ln1_b', 'Wqkv', 'Wout', 'torus_scale', 'ln2_g', 'ln2_b', 'W1', 'b1', 'W2', 'b2', 'Wt', 'bt')}
    del _L0_cond_all

    def _L1_cond_setup():
        import jax, jax.numpy as jnp
        import numpy as np
        B, N, D = (2, 512, 256)
        H, HD = (16, 64)
        E, DD = (8, 1024)
        EPS = 1e-05

        def _ln(x, g, b):
            m = jnp.mean(x, axis=-1, keepdims=True)
            v = jnp.var(x, axis=-1, keepdims=True)
            return (x - m) * jax.lax.rsqrt(v + EPS) * g + b
        key = jax.random.key(seed)
        ks = jax.random.split(key, 16)
        s = 0.02
        return {'x': jax.random.normal(ks[0], (B, N, D), jnp.float32), 't': jax.random.normal(ks[1], (B, 1, D), jnp.float32), 'W_ada': jax.random.normal(ks[2], (D, D), jnp.float32) * s, 'b_ada': jnp.zeros((D,), jnp.float32), 'ln1_g': jnp.ones((D,), jnp.float32), 'ln1_b': jnp.zeros((D,), jnp.float32), 'Wqkv': jax.random.normal(ks[3], (3 * H * HD, D), jnp.float32) * s, 'qn_g': jnp.ones((HD,), jnp.float32), 'qn_b': jnp.zeros((HD,), jnp.float32), 'kn_g': jnp.ones((HD,), jnp.float32), 'kn_b': jnp.zeros((HD,), jnp.float32), 'Wout': jax.random.normal(ks[4], (D, H * HD), jnp.float32) * s, 'mlp_g': jnp.ones((D,), jnp.float32), 'mlp_b': jnp.zeros((D,), jnp.float32), 'Wgate': jax.random.normal(ks[5], (E, D), jnp.float32) * s, 'fc1s': jax.random.normal(ks[6], (E, DD, D), jnp.float32) * s, 'b1s': jnp.zeros((E, DD), jnp.float32), 'fc2s': jax.random.normal(ks[7], (E, D, DD), jnp.float32) * s, 'b2s': jnp.zeros((E, D), jnp.float32)}
    _L1_cond_all = _L1_cond_setup()
    _L1_cond_in = {k: v for k, v in _L1_cond_all.items() if k in ('W_ada', 'b_ada', 'ln1_g', 'ln1_b', 'Wqkv', 'qn_g', 'qn_b', 'kn_g', 'kn_b', 'Wout', 'mlp_g', 'mlp_b', 'Wgate', 'fc1s', 'b1s', 'fc2s', 'b2s')}
    del _L1_cond_all
    return {'x': x, 'cond_1024': cond_1024, 'mask_BxS_bf1': mask_BxS_bf1, 'L0_cond_torus_dist': _L0_cond_in['torus_dist'], 'L0_cond_ln1_g': _L0_cond_in['ln1_g'], 'L0_cond_ln1_b': _L0_cond_in['ln1_b'], 'L0_cond_Wqkv': _L0_cond_in['Wqkv'], 'L0_cond_Wout': _L0_cond_in['Wout'], 'L0_cond_torus_scale': _L0_cond_in['torus_scale'], 'L0_cond_ln2_g': _L0_cond_in['ln2_g'], 'L0_cond_ln2_b': _L0_cond_in['ln2_b'], 'L0_cond_W1': _L0_cond_in['W1'], 'L0_cond_b1': _L0_cond_in['b1'], 'L0_cond_W2': _L0_cond_in['W2'], 'L0_cond_b2': _L0_cond_in['b2'], 'L0_cond_Wt': _L0_cond_in['Wt'], 'L0_cond_bt': _L0_cond_in['bt'], 'L1_cond_W_ada': _L1_cond_in['W_ada'], 'L1_cond_b_ada': _L1_cond_in['b_ada'], 'L1_cond_ln1_g': _L1_cond_in['ln1_g'], 'L1_cond_ln1_b': _L1_cond_in['ln1_b'], 'L1_cond_Wqkv': _L1_cond_in['Wqkv'], 'L1_cond_qn_g': _L1_cond_in['qn_g'], 'L1_cond_qn_b': _L1_cond_in['qn_b'], 'L1_cond_kn_g': _L1_cond_in['kn_g'], 'L1_cond_kn_b': _L1_cond_in['kn_b'], 'L1_cond_Wout': _L1_cond_in['Wout'], 'L1_cond_mlp_g': _L1_cond_in['mlp_g'], 'L1_cond_mlp_b': _L1_cond_in['mlp_b'], 'L1_cond_Wgate': _L1_cond_in['Wgate'], 'L1_cond_fc1s': _L1_cond_in['fc1s'], 'L1_cond_b1s': _L1_cond_in['b1s'], 'L1_cond_fc2s': _L1_cond_in['fc2s'], 'L1_cond_b2s': _L1_cond_in['b2s']}

def reference(x, cond_1024, mask_BxS_bf1, L0_cond_torus_dist, L0_cond_ln1_g, L0_cond_ln1_b, L0_cond_Wqkv, L0_cond_Wout, L0_cond_torus_scale, L0_cond_ln2_g, L0_cond_ln2_b, L0_cond_W1, L0_cond_b1, L0_cond_W2, L0_cond_b2, L0_cond_Wt, L0_cond_bt, L1_cond_W_ada, L1_cond_b_ada, L1_cond_ln1_g, L1_cond_ln1_b, L1_cond_Wqkv, L1_cond_qn_g, L1_cond_qn_b, L1_cond_kn_g, L1_cond_kn_b, L1_cond_Wout, L1_cond_mlp_g, L1_cond_mlp_b, L1_cond_Wgate, L1_cond_fc1s, L1_cond_b1s, L1_cond_fc2s, L1_cond_b2s):
    import jax
    import jax.numpy as jnp

    def _L0_cond_ref(x, torus_dist, time_emb, mask, ln1_g, ln1_b, Wqkv, Wout, torus_scale, ln2_g, ln2_b, W1, b1, W2, b2, Wt, bt):
        import jax, jax.numpy as jnp
        import numpy as np
        EPS = 1e-05
        NEG_INF = -1e+30

        def layer_norm(x, g, b):
            mu = jnp.mean(x, axis=-1, keepdims=True)
            var = jnp.var(x, axis=-1, keepdims=True)
            return (x - mu) * jax.lax.rsqrt(var + EPS) * g + b
        B, L, D = x.shape
        H = torus_scale.shape[0]
        hd = D // H
        tp = jax.nn.gelu(time_emb) @ Wt + bt
        scale, shift = jnp.split(tp, 2, axis=-1)
        h = layer_norm(x, ln1_g, ln1_b) * (1.0 + scale[:, None, :]) + shift[:, None, :]
        qkv = (h @ Wqkv).reshape(B, L, 3, H, hd)
        q = jnp.transpose(qkv[:, :, 0], (0, 2, 1, 3))
        k = jnp.transpose(qkv[:, :, 1], (0, 2, 1, 3))
        v = jnp.transpose(qkv[:, :, 2], (0, 2, 1, 3))
        scores = jnp.einsum('bhqd,bhkd->bhqk', q, k) / np.sqrt(hd).astype(np.float32)
        scores = scores - torus_dist[:, None, :, :] * torus_scale[None, :, None, None]
        pad = ~mask[:, None, None, :]
        scores = jnp.where(pad, NEG_INF, scores)
        attn = jax.nn.softmax(scores, axis=-1)
        attn = jnp.nan_to_num(attn, nan=0.0)
        out = jnp.einsum('bhqk,bhkd->bhqd', attn, v)
        out = jnp.transpose(out, (0, 2, 1, 3)).reshape(B, L, D)
        x = x + out @ Wout
        h2 = layer_norm(x, ln2_g, ln2_b)
        x = x + (jax.nn.gelu(h2 @ W1 + b1) @ W2 + b2)
        return x

    def _L1_cond_ref(x, t, W_ada, b_ada, ln1_g, ln1_b, Wqkv, qn_g, qn_b, kn_g, kn_b, Wout, mlp_g, mlp_b, Wgate, fc1s, b1s, fc2s, b2s):
        import jax, jax.numpy as jnp
        import numpy as np
        B, N, D = (2, 512, 256)
        H, HD = (16, 64)
        E, DD = (8, 1024)
        EPS = 1e-05

        def _ln(x, g, b):
            m = jnp.mean(x, axis=-1, keepdims=True)
            v = jnp.var(x, axis=-1, keepdims=True)
            return (x - m) * jax.lax.rsqrt(v + EPS) * g + b
        b, n, d = x.shape
        shift = jax.nn.silu(t) @ W_ada.T + b_ada
        h = _ln(x, ln1_g, ln1_b) + shift
        qkv = (h @ Wqkv.T).reshape(b, n, 3, H, HD)
        q = _ln(qkv[:, :, 0].transpose(0, 2, 1, 3), qn_g, qn_b)
        k = _ln(qkv[:, :, 1].transpose(0, 2, 1, 3), kn_g, kn_b)
        v = qkv[:, :, 2].transpose(0, 2, 1, 3)
        scores = jnp.einsum('bhnd,bhmd->bhnm', q, k) / jnp.sqrt(jnp.float32(HD))
        attn = jax.nn.softmax(scores, axis=-1)
        o = jnp.einsum('bhnm,bhmd->bhnd', attn, v)
        o = o.transpose(0, 2, 1, 3).reshape(b, n, H * HD)
        x = x + o @ Wout.T
        tok = x.reshape(-1, d)
        bs = tok.shape[0]
        gate = jax.nn.softmax(tok @ Wgate.T, axis=-1)
        k_cap = bs // E
        vals, idx = jax.lax.top_k(gate.T, k_cap)
        idx_flat = idx.T.reshape(-1)
        w = vals.T
        g = _ln(tok[idx_flat], mlp_g, mlp_b).reshape(k_cap, E, d)
        y = jnp.einsum('ked,ehd->keh', g, fc1s) + b1s
        y = jax.nn.gelu(y, approximate=True)
        y = jnp.einsum('keh,edh->ked', y, fc2s) + b2s
        y = y * w[..., None]
        tok = tok.at[idx_flat].add(y.reshape(-1, d))
        return tok.reshape(x.shape)
    x = _L0_cond_ref(x, L0_cond_torus_dist, cond_1024, mask_BxS_bf1, L0_cond_ln1_g, L0_cond_ln1_b, L0_cond_Wqkv, L0_cond_Wout, L0_cond_torus_scale, L0_cond_ln2_g, L0_cond_ln2_b, L0_cond_W1, L0_cond_b1, L0_cond_W2, L0_cond_b2, L0_cond_Wt, L0_cond_bt)
    x = _L1_cond_ref(x, cond_1024[:, None, :], L1_cond_W_ada, L1_cond_b_ada, L1_cond_ln1_g, L1_cond_ln1_b, L1_cond_Wqkv, L1_cond_qn_g, L1_cond_qn_b, L1_cond_kn_g, L1_cond_kn_b, L1_cond_Wout, L1_cond_mlp_g, L1_cond_mlp_b, L1_cond_Wgate, L1_cond_fc1s, L1_cond_b1s, L1_cond_fc2s, L1_cond_b2s)
    return x

_drawn_inputs = setup_inputs


def setup_inputs(seed=0):
    import zlib

    import numpy as np

    out = dict(_drawn_inputs(seed))
    spreads = {'L0_cond_ln1_g': (1.0, 0.6),
     'L0_cond_ln1_b': (0.0, 0.724),
     'L0_cond_torus_scale': (0.10000000149011612, 0.6),
     'L0_cond_ln2_g': (1.0, 0.6),
     'L0_cond_ln2_b': (0.0, 0.753),
     'L0_cond_b1': (0.0, 0.1),
     'L0_cond_b2': (0.0, 0.1),
     'L0_cond_bt': (0.0, 0.8),
     'L1_cond_b_ada': (0.0, 0.342),
     'L1_cond_ln1_g': (1.0, 0.6),
     'L1_cond_ln1_b': (0.0, 0.429),
     'L1_cond_qn_g': (1.0, 0.6),
     'L1_cond_qn_b': (0.0, 0.8),
     'L1_cond_kn_g': (1.0, 0.6),
     'L1_cond_kn_b': (0.0, 2.0),
     'L1_cond_mlp_g': (1.0, 0.6),
     'L1_cond_mlp_b': (0.0, 2.0),
     'L1_cond_b1s': (0.0, 0.8),
     'L1_cond_b2s': (0.0, 0.425)}
    factors = {'L0_cond_torus_dist': 57.549, 'L0_cond_Wt': 2.7}
    for name, (base, spread) in spreads.items():
        noise = np.random.default_rng([zlib.crc32(name.encode()), seed]).standard_normal(out[name].shape)
        drawn = base * np.exp(spread * noise) if base else spread * noise
        out[name] = jnp.asarray(drawn.astype(out[name].dtype))
    for name, factor in factors.items():
        out[name] = (out[name] * factor).astype(out[name].dtype)
    return out
```

```python
import concourse.bass as bass
from concourse import mybir
from contextlib import ExitStack


def cond_seq_kernel(nc, t, out, stop_after=None):
    fp32 = mybir.dt.float32
    fp16 = mybir.dt.float16
    bf16 = mybir.dt.bfloat16
    i32 = mybir.dt.int32
    u32 = mybir.dt.uint32
    u8 = mybir.dt.uint8
    ALU = mybir.AluOpType
    ACT = mybir.ActivationFunctionType
    AX = mybir.AxisListType

    B, L, D = t["x"].shape
    P = 128
    H = t["L0_cond_torus_scale"].shape[0]
    HD0 = D // H
    HD1 = 64
    C = D // P
    QT = L // P
    NT = B * QT
    F0 = t["L0_cond_W1"].shape[1]
    FT = F0 // P
    E, _, F1 = t["L1_cond_fc1s"].shape
    W1V = H * HD1
    JT = W1V // P
    EPS = 1e-5
    CAP = B * L // E
    HALVES = CAP // P
    PAIRS = H // 2
    CH = 512
    G8 = CH // HD1
    RW = D + E
    NEG = -1e30
    LANES = P // E

    ctx = ExitStack()
    with ctx:
        def sb(name, shape, dt=fp32):
            return ctx.enter_context(nc.sbuf_tensor(name, shape, dt))

        def sem(name):
            return ctx.enter_context(nc.semaphore(name))

        qk_parts = nc.dram_tensor("qk_parts", (3, 4 * P, L), bf16, kind="Internal").ap()
        rows = nc.dram_tensor("routed_rows", (B * L, RW), fp32, kind="Internal").ap()

        x = sb("x", [P, NT, D])
        ident = sb("ident", [P, P])
        wqkv0 = sb("wqkv0", [P, C, 3 * D])
        wout0 = sb("wout0", [P, C, D])
        w1 = sb("w1", [P, C, F0])
        w2 = sb("w2", [P, FT, D])
        wqkv1 = sb("wqkv1", [P, C, 3 * W1V])
        wout1 = sb("wout1", [P, JT, D])
        wgate = sb("wgate", [P, C, E])
        hT = sb("hT", [P, C, L])
        xn = sb("xn", [P, QT, RW])
        q_stack = sb("q_stack", [P, H, L], bf16)
        k_stack = sb("k_stack", [P, H, L], bf16)
        kl_stack = sb("kl_stack", [P, H, L], fp16)
        vals_flat = sb("vals", [P, QT * W1V])
        obuf = sb("obuf", [P, QT * W1V])
        RB = QT * L
        ring = sb("ring", [P, 4 * RB])
        pen = sb("pen", [1, B * L], bf16)

        q16 = q_stack[:, :, :].bitcast(fp16)
        k16 = k_stack[:, :, :].bitcast(fp16)
        vals = [vals_flat[:, 0:QT * w].rearrange("p (q w) -> p q w", q=QT) for w in (D, W1V)]
        dist = vals_flat[:, QT * W1V - QT * L:QT * W1V]
        xs = w1[:, 0, 0:QT * D].rearrange("p (q d) -> p q d", q=QT)
        mask_u8 = obuf[0:1, 0:B * L // 4].bitcast(u8)
        bias_ring = kl_stack[:, :, :].rearrange("p h l -> p (h l)").bitcast(fp32)
        probs = [ring[:, r * RB:(r + 1) * RB] for r in (0, 1)]
        probsT = [ring[:, r * RB:(r + 1) * RB] for r in (2, 3)]
        split0 = [ring[:, r * RB // 2:(r + 1) * RB // 2].bitcast(bf16)
                  .rearrange("p (m l) -> p m l", m=4) for r in range(3)]
        rest0 = ring[:, 2 * RB:3 * RB].rearrange("p (m l) -> p m l", m=4)
        hi1 = ring[:, 0:2 * RB].bitcast(fp16).rearrange("p (w c l) -> p w c l", w=2, c=PAIRS)
        lo1 = ring[:, 2 * RB:4 * RB].bitcast(fp16).rearrange("p (w c l) -> p w c l", w=2, c=PAIRS)
        sq1 = [obuf[:, r * CH:(r + 1) * CH] for r in (0, 1)]
        qn1 = [obuf[:, r * CH:(r + 1) * CH] for r in (2, 3)]
        f1b = [obuf[:, r * CH:(r + 1) * CH] for r in (4, 5)]
        oT = ring[:, 0:JT * L].rearrange("p (j l) -> p j l", j=JT)
        aT = obuf[:, 0:FT * L].rearrange("p (f l) -> p f l", f=FT)
        wt = ring[:, 0:C * 2 * D].rearrange("p (c n) -> p c n", c=C)
        wada = ring[:, C * 2 * D:C * 3 * D].rearrange("p (c n) -> p c n", c=C)

        negmax = sb("negmax", [P, 2, QT])
        rsum = sb("rsum", [P, 2, QT])
        rinv = sb("rinv", [P, 2, QT])
        scale_now = sb("scale_now", [P, 2])
        tscale = sb("tscale", [P, H])
        stats = sb("stats", [P, QT, 6])
        mv = sb("mv", [P, QT, 2])
        veps = sb("veps", [P, QT])
        rstd = sb("rstd", [P, QT])
        mhalf = sb("mhalf", [P, 16])
        ssum = sb("ssum", [P, 2, G8])
        v8 = sb("v8", [P, 2, G8])
        r8 = sb("r8", [P, 2, G8])
        condT = sb("condT", [P, C, B])
        gelT = sb("gelT", [P, C, B])
        silT = sb("silT", [P, C, B])
        cols = sb("cols", [P, t["cols"].shape[1]])
        col, at_col = {}, 0
        for n, k in FEATURE_COLS:
            col[n] = cols[:, at_col:at_col + k]
            at_col += k
        qkg = cols[:, at_col:at_col + 4]
        qkf = sb("qkf", [P, 4])
        b2b = sb("b2b", [P, D])
        gain = {0: sb("gain0", [P, C, B]), 1: sb("gain1", [P, C, B]), 2: sb("gain2", [P, C, B])}
        shift = {0: sb("shift0", [P, C, B]), 1: sb("shift1", [P, C, B]), 2: sb("shift2", [P, C, B])}
        tp = sb("tp", [P, 3 * C, B])
        wmean = sb("wmean", [P, C, 2 * H])
        gates = sb("gates", [P, NT, E])
        gmax = sb("gmax", [P, QT])
        gsum = sb("gsum", [P, QT])
        gexp = sb("gexp", [P, QT, E])

        ST = 32 // 4
        gate_rep = ring[:, 0:B * L]
        above = ring[:, B * L:3 * B * L // 2].bitcast(bf16)
        level = ring[:, 3 * B * L // 2:2 * B * L].bitcast(bf16)
        above_n = ring[:, 2 * B * L:3 * B * L]
        level_n = ring[:, 3 * B * L:4 * B * L]
        taken_n = obuf[:, 0:B * L // 2].bitcast(bf16)
        xg = obuf[:, B * L // 2:B * L // 2 + 2 * HALVES * RW].rearrange("p (r h w) -> p r h w", r=2, h=HALVES)
        b2all = vals_flat[:, 0:E * D]
        yout = vals_flat[:, E * D:E * D + 2 * HALVES * D].rearrange("p (r h d) -> p r h d", r=2, h=HALVES)
        gT = vals_flat[:, E * D + 2 * HALVES * D:E * D + 2 * HALVES * D + 2 * C * CAP]\
            .rearrange("p (r c s) -> p r c s", r=2, c=C)
        yT = kl_stack[:, :, :].rearrange("p h l -> p (h l)").bitcast(fp32)\
            .rearrange("p (r f s) -> p r f s", r=2, f=F1 // P)
        fc1, fc2 = [], []
        for buf in (q_stack, k_stack):
            flat = buf[:, :, :].rearrange("p h l -> p (h l)").bitcast(fp32)
            fc1.append(flat[:, 0:C * F1].rearrange("p (c f) -> p c f", c=C))
            fc2.append(flat[:, C * F1:2 * C * F1].rearrange("p (f d) -> p f d", d=D))
        pick_f = w2[:, :, :].rearrange("p f d -> p (f d)")[:, 0:E * P]
        pick = w2[:, :, :].rearrange("p f d -> p (f d)")[:, E * P:E * P + E * P // 2].bitcast(bf16)
        lanes = sb("lanes", [P, ST], i32)
        steps = sb("steps", [P, ST])
        same = sb("same", [P, P])
        slot = sb("slot", [P, HALVES])
        prefix = sb("prefix", [P, 1], i32)
        cand = sb("cand", [P, 1], i32)
        more = sb("more", [P, 1], i32)
        count = sb("count", [P, 1])
        enough = sb("enough", [P, 1])
        need = sb("need", [P, 1])
        idx_f = sb("idx_f", [P, 2, HALVES])
        idx = sb("idx", [P, 2, HALVES], u32)

        PS = ctx.enter_context(nc.psum_tensor("PS", [P, 8, CH], fp32))

        s_x = sem("s_x")
        s_vec = sem("s_vec")
        s_w0 = sem("s_w0")
        s_w1 = sem("s_w1")
        s_ident = sem("s_ident")
        s_const = sem("s_const")
        s_pen = sem("s_pen")
        turn = {e: sem(f"turn_{e}") for e in ("pe", "act", "dve", "pool", "sp")}
        cond_act = sem("cond_act")
        cond_mm = sem("cond_mm")
        cond_vec = sem("cond_vec")
        w_centred = sem("w_centred")
        s_mean = sem("s_mean")

        def hold(eng, key, s, val):
            eng.wait_ge(s, val)
            eng.sem_inc(turn[key], 1)

        class Norm:
            def __init__(self, name):
                self.stats = sem(name + "_stats")
                self.aggr = sem(name + "_aggr")
                self.veps = sem(name + "_veps")
                self.rstd = sem(name + "_rstd")
                self.xn = sem(name + "_xn")
                self.tr = sem(name + "_tr")
                self.hT = sem(name + "_hT")

        ln = [Norm("ln_a"), Norm("ln_b"), Norm("ln_c"), Norm("ln_d")]

        def norm_dve(n, b, src, width_off=0):
            s = ln[n]
            for q in range(QT):
                nc.vector.bn_stats(stats[:, q, :], src(b, q)).then_inc(s.stats, 1)
            for q in range(QT):
                hold(nc.vector, "dve", s.stats, b * QT + q + 1)
                nc.vector.bn_aggr(mv[:, q, :], stats[:, q, :]).then_inc(s.aggr, 1)
            nc.vector.wait_ge(s.aggr, b * QT + QT)
            nc.vector.tensor_scalar(veps[:, :], mv[:, :, 1], EPS, None, ALU.add).then_inc(s.veps, 1)
            nc.vector.wait_ge(s.rstd, b + 1)
            for q in range(QT):
                nc.vector.tensor_scalar(xn[:, q, 0:D], src(b, q), mv[:, q, 0:1], rstd[:, q:q + 1],
                                        ALU.subtract, ALU.mult).then_inc(s.xn, 1)

        def norm_pool(n, b):
            s = ln[n]
            nc.gpsimd.wait_ge(s.veps, b + 1)
            nc.gpsimd.tensor_tensor(rstd[:, :], veps[:, :], mhalf[:, 0:QT], ALU.pow).then_inc(s.rstd, 1)

        def norm_pe(n, b):
            s = ln[n]
            for c in range(C):
                for q in range(QT):
                    if c == 0:
                        nc.tensor.wait_ge(s.xn, b * QT + q + 1)
                    mm = nc.tensor.transpose(PS[:, c, q * P:(q + 1) * P], xn[:, q, c * P:(c + 1) * P], ident[:, :])
                mm.then_inc(s.tr, 1)

        def norm_act(n, b):
            s = ln[n]
            for c in range(C):
                hold(nc.scalar, "act", s.tr, b * C + c + 1)
                nc.scalar.activation(hT[:, c, :], PS[:, c, :], ACT.Identity, bias=shift[n][:, c, bass.ds(b, 1)],
                                     scale=gain[n][:, c, bass.ds(b, 1)]).then_inc(s.hT, 1)

        class Attn:
            def __init__(self, name):
                self.s = sem(name + "_scores")
                self.mx = sem(name + "_max")
                self.ex = sem(name + "_exp")
                self.t = sem(name + "_probsT")
                self.ea = sem(name + "_evac_act")
                self.ed = sem(name + "_evac_dve")
                self.pv = sem(name + "_pv")
                self.ri = sem(name + "_rinv")
                self.o = sem(name + "_out")
                self.bias = sem(name + "_bias")
                self.scl = sem(name + "_scale")
                self.stack = sem(name + "_stack")
                self.qk = sem(name + "_qk")
                self.v = sem(name + "_v")
                self.vs = sem(name + "_v_sbuf")
                self.ot = sem(name + "_oT")
                self.ota = sem(name + "_oT_act")
                self.otd = sem(name + "_oT_dve")
                self.pr = sem(name + "_proj")
                self.xa = sem(name + "_x_added")

        at = [Attn("at0"), Attn("at1")]
        CS, CE, CO = 2 * QT, 1, 2

        def credits(eng, which):
            for a in at:
                if which == "pe":
                    eng.sem_inc(a.t, CS)
                    eng.sem_inc(a.pv, CO)
                if which == "act":
                    eng.sem_inc(a.ex, CS)
                    eng.sem_inc(a.ea, CE)
                if which == "dve":
                    eng.sem_inc(a.mx, CS)
                    eng.sem_inc(a.ed, CE)
                    eng.sem_inc(a.o, CO)
                    eng.sem_inc(a.ri, CO)

        def heads(eng, step):
            step(0, 0, True, False, False)
            step(1, 1, True, True, False)
            with eng.Fori(1, H // 2) as pair:
                step(2 * pair, 0, True, True, True)
                step(2 * pair + 1, 1, True, True, True)
            step(H, 0, False, True, True)
            step(H + 1, 1, False, False, True)

        def attn_pe(k, b):
            a = at[k]
            hd = (HD0, HD1)[k]

            def step(i, par, scores, turned, values):
                n = b * H + i
                for q in range(QT):
                    if scores:
                        hold(nc.tensor, "pe", (a.mx, a.ex)[k], n * QT + q + 1 - QT + CS)
                        if k == 0:
                            R = 6 * HD0 + 1
                            nc.tensor.matmul(PS[:, q, :], q_stack[0:R, i, q * P:(q + 1) * P], k_stack[0:R, i, :],
                                             start=True, stop=True).then_inc(a.s, 1)
                        else:
                            nc.tensor.matmul(PS[:, q, :], q16[:, i, q * P:(q + 1) * P], k16[:, i, :],
                                             start=True, stop=False)
                            nc.tensor.matmul(PS[:, q, :], q16[:, i, q * P:(q + 1) * P], kl_stack[:, i, :],
                                             start=False, stop=True).then_inc(a.s, 1)
                    if turned:
                        m, kt = n - 1, q
                        if kt == 0:
                            nc.tensor.wait_ge(a.ex, m * QT + QT + CS)
                        nc.tensor.wait_ge((a.ea, a.ed)[kt % 2], m * (QT // 2) + kt // 2 + CE)
                        for qq in range(QT):
                            mm = nc.tensor.transpose(PS[:, 4 + kt % 2, qq * P:(qq + 1) * P],
                                                     probs[1 - par][:, qq * L + kt * P:qq * L + (kt + 1) * P],
                                                     ident[:, :])
                        mm.then_inc(a.t, 1)
                    if values:
                        m = n - 2
                        if q == 0:
                            nc.tensor.wait_ge(a.ea, m * (QT // 2) + QT // 2 + CE)
                            nc.tensor.wait_ge(a.ed, m * (QT // 2) + QT // 2 + CE)
                            nc.tensor.wait_ge(a.o, m - 1 + CO)
                        for kt in range(QT):
                            mm = nc.tensor.matmul(PS[:, 6 + par, q * hd:(q + 1) * hd],
                                                  probsT[par][:, kt * L + q * P:kt * L + (q + 1) * P],
                                                  vals[k][:, kt, bass.ds((i - 2) * hd, hd)],
                                                  start=(kt == 0), stop=(kt == QT - 1))
                        if q == QT - 1:
                            mm.then_inc(a.pv, 1)

            heads(nc.tensor, step)

        def evac_probsT(eng, a, m, kt, par):
            if kt < 2:
                eng.wait_ge(a.pv, m - 1 + CO)
            eng.wait_ge(a.t, m * QT + kt + 1 + CS)
            dst, src = probsT[par][:, kt * L:(kt + 1) * L], PS[:, 4 + kt % 2, :]
            if eng is nc.scalar:
                nc.scalar.activation(dst, src, ACT.Copy).then_inc(a.ea, 1)
            else:
                nc.vector.tensor_copy(dst, src).then_inc(a.ed, 1)

        def attn_act(k, b):
            a = at[k]

            def step(i, par, scores, turned, values):
                n = b * H + i
                for q in range(QT):
                    if scores:
                        if q == 0:
                            nc.scalar.wait_ge(a.ri, n - 1 + CO)
                            if k == 1:
                                nc.scalar.wait_ge(a.t, (n - 1) * QT + CS)
                        nc.scalar.wait_ge(a.mx, n * QT + q + 1 + CS)
                        p = probs[par][:, q * L:(q + 1) * L]
                        if k == 0:
                            nc.scalar.activation(p, p, ACT.Exp, bias=negmax[:, par, q:q + 1], scale=-1.0,
                                                 accum_out=rsum[:, par, q:q + 1]).then_inc(a.ex, 1)
                        else:
                            nc.scalar.activation(p, PS[:, q, :], ACT.Exp, bias=negmax[:, par, q:q + 1],
                                                 accum_out=rsum[:, par, q:q + 1]).then_inc(a.ex, 1)
                    if turned and q % 2 == 0:
                        evac_probsT(nc.scalar, a, n - 1, q, 1 - par)

            heads(nc.scalar, step)

        def attn_dve(k, b):
            a = at[k]
            hd = (HD0, HD1)[k]

            def step(i, par, scores, turned, values):
                n = b * H + i
                if values:
                    nc.vector.wait_ge(a.ex, (n - 2) * QT + QT + CS)
                    nc.vector.reciprocal(rinv[:, par, :], rsum[:, par, :]).then_inc(a.ri, 1)
                for q in range(QT):
                    if scores:
                        if k == 0:
                            if q == 0:
                                nc.vector.wait_ge(a.t, (n - 1) * QT + CS)
                                nc.vector.wait_ge(a.bias, n + 1)
                            nc.vector.wait_ge(a.ex, (n - 2) * QT + q + 1 + CS)
                            hold(nc.vector, "dve", a.s, n * QT + q + 1)
                            nc.vector.tensor_tensor_reduce(probs[par][:, q * L:(q + 1) * L], PS[:, q, :],
                                                           bias_ring[:, par * RB + q * L:par * RB + (q + 1) * L],
                                                           -1.0, 3e38, ALU.add, ALU.min,
                                                           negmax[:, par, q:q + 1]).then_inc(a.mx, 1)
                        else:
                            nc.vector.wait_ge(a.ex, (n - 2) * QT + q + 1 + CS)
                            nc.vector.wait_ge(a.s, n * QT + q + 1)
                            nc.vector.tensor_reduce(negmax[:, par, q:q + 1], PS[:, q, :], AX.X, ALU.max,
                                                    negate=True).then_inc(a.mx, 1)
                    if turned and q % 2 == 1:
                        evac_probsT(nc.vector, a, n - 1, q, 1 - par)
                if values:
                    m = n - 2
                    nc.vector.wait_ge(a.ri, m + 1 + CO)
                    nc.vector.wait_ge(a.pv, m + 1 + CO)
                    o = obuf[:, 0:QT * H * hd].rearrange("p (q w) -> p q w", q=QT)
                    nc.vector.tensor_tensor(o[:, :, bass.ds((i - 2) * hd, hd)],
                                            PS[:, 6 + par, 0:QT * hd].rearrange("p (q w) -> p q w", q=QT),
                                            rinv[:, par, :].unsqueeze(2).broadcast_to([P, QT, hd]),
                                            ALU.mult).then_inc(a.o, 1)

            heads(nc.vector, step)

        def bias_pool(b):
            a = at[0]
            with nc.gpsimd.Fori(0, H // 2) as pair:
                for par in range(2):
                    i = 2 * pair + par
                    n = b * H + i
                    hold(nc.gpsimd, "pool", a.mx, (n - 1) * QT + CS)
                    nc.gpsimd.tensor_copy(scale_now[:, par:par + 1], tscale[:, bass.ds(i, 1)])\
                        .then_inc(a.scl, 1)
                    hold(nc.gpsimd, "pool", a.scl, n + 1)
                    nc.gpsimd.tensor_scalar(bias_ring[:, par * RB:(par + 1) * RB], dist[:, :],
                                            scale_now[:, par:par + 1], -1.0, ALU.mult, ALU.mult)\
                        .then_inc(a.bias, 1)

        def out_pe(k, b):
            a = at[k]
            jt, w = ((C, wout0), (JT, wout1))[k]
            o = obuf[:, 0:QT * jt * P].rearrange("p (q w) -> p q w", q=QT)
            nc.tensor.wait_ge(a.o, (b + 1) * H + CO)
            for j in range(jt):
                if j >= 2:
                    nc.tensor.wait_ge((a.ota, a.otd)[j % 2], b * (jt // 2) + j // 2)
                for q in range(QT):
                    mm = nc.tensor.transpose(PS[:, j % 2, q * P:(q + 1) * P], o[:, q, j * P:(j + 1) * P], ident[:, :])
                mm.then_inc(a.ot, 1)
            nc.tensor.wait_ge(a.ota, (b + 1) * (jt // 2))
            nc.tensor.wait_ge(a.otd, (b + 1) * (jt // 2))
            for q in range(QT):
                for j in range(jt):
                    mm = nc.tensor.matmul(PS[:, 2 + q, 0:D], oT[:, j, q * P:(q + 1) * P], w[:, j, :],
                                          start=(j == 0), stop=(j == jt - 1))
                mm.then_inc(a.pr, 1)

        def out_act(k, b):
            a = at[k]
            jt = (C, JT)[k]
            for j in range(0, jt, 2):
                nc.scalar.wait_ge(a.ot, b * jt + j + 1)
                nc.scalar.activation(oT[:, j, :], PS[:, 0, :], ACT.Copy).then_inc(a.ota, 1)

        def out_dve(k, b):
            a = at[k]
            jt = (C, JT)[k]
            for j in range(1, jt, 2):
                nc.vector.wait_ge(a.ot, b * jt + j + 1)
                nc.vector.tensor_copy(oT[:, j, :], PS[:, 1, :]).then_inc(a.otd, 1)
            for q in range(QT):
                nc.vector.wait_ge(a.pr, b * QT + q + 1)
                old = x[:, bass.ds(b * QT + q, 1), :].rearrange("p a d -> p (a d)")
                new = old if k == 0 else xs[:, q, :]
                nc.vector.tensor_tensor(new, PS[:, 2 + q, 0:D], old, ALU.add).then_inc(a.xa, 1)

        f0 = {n: sem("p0_" + n) for n in ("hi", "f", "r", "mid", "lo", "stored")}

        def proj0_pe(b):
            a = at[0]
            nc.tensor.wait_ge(ln[0].hT, (b + 1) * C)
            for m in range(4):
                for c in range(C):
                    mm = nc.tensor.matmul(PS[:, m, :], wqkv0[:, c, m * P:(m + 1) * P], hT[:, c, :],
                                          start=(c == 0), stop=(c == C - 1))
                mm.then_inc(a.qk, 1)
            for q in range(QT):
                for c in range(C):
                    mm = nc.tensor.matmul(PS[:, 4 + q, 0:D], hT[:, c, q * P:(q + 1) * P],
                                          wqkv0[:, c, 2 * D:3 * D], start=(c == 0), stop=(c == C - 1))
                mm.then_inc(a.v, 1)

        def proj0_act(b):
            a = at[0]
            for m in range(4):
                nc.scalar.wait_ge(f0["f"], b * 4 + m + 1)
                nc.scalar.activation(split0[0][:, m, :], rest0[:, m, :], ACT.Copy).then_inc(f0["hi"], 1)
            for m in range(4):
                nc.scalar.wait_ge(f0["r"], b * 4 + m + 1)
                nc.scalar.activation(split0[1][:, m, :], rest0[:, m, :], ACT.Copy).then_inc(f0["mid"], 1)
            for q in range(QT):
                nc.scalar.wait_ge(a.v, b * QT + q + 1)
                nc.scalar.activation(vals[0][:, q, :], PS[:, 4 + q, 0:D], ACT.Copy).then_inc(a.vs, 1)

        def proj0_dve(b):
            a = at[0]
            for m in range(4):
                nc.vector.wait_ge(a.qk, b * 4 + m + 1)
                nc.vector.tensor_scalar(rest0[:, m, :], PS[:, m, :], (HD0 ** -0.5 if m < 2 else 1.0), None,
                                        ALU.mult).then_inc(f0["f"], 1)
                nc.vector.wait_ge(f0["hi"], b * 4 + m + 1)
                nc.vector.tensor_tensor(rest0[:, m, :], rest0[:, m, :], split0[0][:, m, :],
                                        ALU.subtract).then_inc(f0["r"], 1)

        def proj0_pool(b):
            for m in range(4):
                nc.gpsimd.wait_ge(f0["mid"], b * 4 + m + 1)
                nc.gpsimd.tensor_tensor(split0[2][:, m, :], rest0[:, m, :], split0[1][:, m, :],
                                        ALU.subtract).then_inc(f0["lo"], 1)

        Q_PARTS, K_PARTS = (0, 0, 1, 1, 0, 2), (0, 1, 0, 1, 2, 0)

        def stacks0_sp(b):
            a = at[0]
            for part, s in enumerate(("hi", "mid", "lo")):
                hold(nc.sync, "sp", f0[s], (b + 1) * 4)
                nc.sync.dma_start(qk_parts[part].rearrange("(m p) l -> p m l", p=P), split0[part])\
                    .then_inc(f0["stored"], 16)
            hold(nc.sync, "sp", f0["stored"], (b + 1) * 48)
            for r in range(6):
                for stack, parts, base in ((q_stack, Q_PARTS, 0), (k_stack, K_PARTS, 2 * P)):
                    nc.sync.dma_start(stack[r * HD0:(r + 1) * HD0, :, :],
                                      qk_parts[parts[r], base:base + 2 * P, :].rearrange("(h d) l -> d h l", d=HD0))\
                        .then_inc(a.stack, 16)
            nc.sync.dma_start(k_stack[6 * HD0:6 * HD0 + 1, :, :],
                              pen[:, bass.ds(b * L, L)].unsqueeze(1).broadcast_to([1, H, L])).then_inc(a.stack, 16)

        STACK0 = 13 * 16

        ff = {n: sem("ff_" + n) for n in ("h", "g", "y", "x", "b")}

        def ffn_pe(b):
            nc.tensor.wait_ge(ln[1].hT, (b + 1) * C)
            for f in range(FT):
                if f >= 4:
                    nc.tensor.wait_ge(ff["g"], b * FT + f - 3)
                for c in range(C):
                    mm = nc.tensor.matmul(PS[:, f % 4, :], w1[:, c, f * P:(f + 1) * P], hT[:, c, :],
                                          start=(c == 0), stop=(c == C - 1))
                mm.then_inc(ff["h"], 1)
            nc.tensor.wait_ge(ff["g"], (b + 1) * FT)
            for q in range(QT):
                for f in range(FT):
                    mm = nc.tensor.matmul(PS[:, 4 + q, 0:D], aT[:, f, q * P:(q + 1) * P], w2[:, f, :],
                                          start=(f == 0), stop=(f == FT - 1))
                mm.then_inc(ff["y"], 1)

        def ffn_act(b):
            for f in range(FT):
                nc.scalar.wait_ge(ff["h"], b * FT + f + 1)
                nc.scalar.activation(aT[:, f, :], PS[:, f % 4, :], ACT.Gelu_apprx_tanh,
                                     bias=col["L0_cond_b1"][:, f:f + 1]).then_inc(ff["g"], 1)

        def ffn_dve(b):
            for q in range(QT):
                xq = x[:, bass.ds(b * QT + q, 1), :].rearrange("p a d -> p (a d)")
                nc.vector.wait_ge(ff["y"], b * QT + q + 1)
                nc.vector.tensor_tensor(xq, PS[:, 4 + q, 0:D], xq, ALU.add).then_inc(ff["x"], 1)
                nc.vector.wait_ge(ff["x"], b * QT + q + 1)
                nc.vector.tensor_tensor(xq, xq, b2b[:, :], ALU.add).then_inc(ff["b"], 1)

        p1 = {n: sem("p1_" + n) for n in ("mm", "sq", "sum", "v8", "r8", "qn", "tr", "hi", "f", "lo")}
        NS = 4 * QT

        def where1(n):
            cc, q = n // QT, n % QT
            return cc // 2, (cc % 2) * (G8 // 2), q

        def proj1_pe(b):
            a = at[1]
            nc.tensor.wait_ge(ln[2].hT, (b + 1) * C)
            for n in range(NS + 2):
                if n < NS:
                    q = n % QT
                    if n >= 4:
                        nc.tensor.wait_ge(p1["qn"], b * NS + n - 3)
                    for c in range(C):
                        mm = nc.tensor.matmul(PS[:, n % 4, :], hT[:, c, q * P:(q + 1) * P],
                                              wqkv1[:, c, (n // QT) * CH:(n // QT + 1) * CH],
                                              start=(c == 0), stop=(c == C - 1))
                    mm.then_inc(p1["mm"], 1)
                if n >= 2:
                    m = n - 2
                    nc.tensor.wait_ge(p1["qn"], b * NS + m + 1)
                    if m >= 2:
                        nc.tensor.wait_ge(p1["f"], b * NS + m - 1)
                        nc.tensor.wait_ge(p1["hi"], b * NS + m - 1)
                    for pr in range(G8 // 2):
                        mm = nc.tensor.transpose(PS[:, 4 + m % 2, pr * P:(pr + 1) * P],
                                                 qn1[m % 2][:, pr * P:(pr + 1) * P], ident[:, :])
                    mm.then_inc(p1["tr"], 1)
            for n in range(2 * QT):
                q, half = n // 2, n % 2
                if n >= 2:
                    nc.tensor.wait_ge(a.vs, b * 2 * QT + n - 1)
                for c in range(C):
                    mm = nc.tensor.matmul(PS[:, 6 + half, :], hT[:, c, q * P:(q + 1) * P],
                                          wqkv1[:, c, 2 * W1V + half * CH:2 * W1V + (half + 1) * CH],
                                          start=(c == 0), stop=(c == C - 1))
                mm.then_inc(a.v, 1)

        def proj1_act(b):
            a = at[1]
            for n in range(NS + 3):
                if n < NS:
                    nc.scalar.wait_ge(p1["mm"], b * NS + n + 1)
                    if n >= 2:
                        nc.scalar.wait_ge(p1["sum"], b * NS + n - 1)
                    nc.scalar.activation(sq1[n % 2], PS[:, n % 4, :], ACT.Square).then_inc(p1["sq"], 1)
                if n >= 3:
                    m = n - 3
                    w, pair, q = where1(m)
                    nc.scalar.wait_ge(p1["f"], b * NS + m + 1)
                    nc.scalar.activation(hi1[:, w, pair:pair + G8 // 2, q * P:(q + 1) * P],
                                         f1b[m % 2].rearrange("p (c l) -> p c l", l=P), ACT.Copy)\
                        .then_inc(p1["hi"], 1)
            for n in range(2 * QT):
                q, half = n // 2, n % 2
                nc.scalar.wait_ge(a.v, b * 2 * QT + n + 1)
                nc.scalar.activation(vals[1][:, q, half * CH:(half + 1) * CH], PS[:, 6 + half, :], ACT.Copy)\
                    .then_inc(a.vs, 1)

        def proj1_dve(b):
            for n in range(NS + 3):
                if n < NS:
                    r = n % 2
                    nc.vector.wait_ge(p1["sq"], b * NS + n + 1)
                    nc.vector.tensor_reduce(ssum[:, r, :], sq1[r].rearrange("p (h d) -> p h d", d=HD1),
                                            AX.X, ALU.add).then_inc(p1["sum"], 1)
                    nc.vector.wait_ge(p1["sum"], b * NS + n + 1)
                    if n >= 2:
                        nc.vector.wait_ge(p1["r8"], b * NS + n - 1)
                    nc.vector.tensor_scalar(v8[:, r, :], ssum[:, r, :], 1.0 / HD1, EPS, ALU.mult, ALU.add)\
                        .then_inc(p1["v8"], 1)
                if 1 <= n <= NS:
                    m = n - 1
                    r = m % 2
                    nc.vector.wait_ge(p1["r8"], b * NS + m + 1)
                    if m >= 2:
                        nc.vector.wait_ge(p1["tr"], b * NS + m - 1)
                    nc.vector.tensor_tensor(qn1[r].rearrange("p (h d) -> p h d", d=HD1),
                                            PS[:, m % 4, :].rearrange("p (h d) -> p h d", d=HD1),
                                            r8[:, r, :].unsqueeze(2).broadcast_to([P, G8, HD1]), ALU.mult)\
                        .then_inc(p1["qn"], 1)
                if n >= 3:
                    m = n - 3
                    w = where1(m)[0]
                    nc.vector.wait_ge(p1["tr"], b * NS + m + 1)
                    if m >= 2:
                        nc.vector.wait_ge(p1["lo"], b * NS + m - 1)
                    nc.vector.tensor_scalar(f1b[m % 2], PS[:, 4 + m % 2, :], qkf[:, 2 * w:2 * w + 1],
                                            qkf[:, 2 * w + 1:2 * w + 2], ALU.mult, ALU.add).then_inc(p1["f"], 1)

        def proj1_pool(b):
            for n in range(NS + 3):
                if n < NS:
                    nc.gpsimd.wait_ge(p1["v8"], b * NS + n + 1)
                    if n >= 2:
                        nc.gpsimd.wait_ge(p1["qn"], b * NS + n - 1)
                    nc.gpsimd.tensor_tensor(r8[:, n % 2, :], v8[:, n % 2, :], mhalf[:, 0:G8], ALU.pow)\
                        .then_inc(p1["r8"], 1)
                if n >= 3:
                    m = n - 3
                    w, pair, q = where1(m)
                    nc.gpsimd.wait_ge(p1["hi"], b * NS + m + 1)
                    nc.gpsimd.wait_ge(p1["f"], b * NS + m + 1)
                    nc.gpsimd.tensor_tensor(lo1[:, w, pair:pair + G8 // 2, q * P:(q + 1) * P],
                                            f1b[m % 2].rearrange("p (c l) -> p c l", l=P),
                                            hi1[:, w, pair:pair + G8 // 2, q * P:(q + 1) * P], ALU.subtract)\
                        .then_inc(p1["lo"], 1)

        def stacks1_sp(b):
            a = at[1]

            def place(stack, row, src, w):
                for odd in range(2):
                    nc.sync.dma_start(stack[row:row + HD1, odd:H:2, :],
                                      src[odd * HD1:(odd + 1) * HD1, w, :, :]).then_inc(a.stack, 16)

            hold(nc.sync, "sp", p1["lo"], b * NS + NS // 2)
            place(q16, 0, hi1, 0)
            place(q16, HD1, lo1, 0)
            hold(nc.sync, "sp", p1["lo"], b * NS + NS)
            for row in (0, HD1):
                place(k16, row, hi1, 1)
                place(kl_stack, row, lo1, 1)

        STACK1 = 12 * 16

        g = {n: sem("gate_" + n) for n in ("xT", "xTs", "mm", "max", "sub", "exp", "sum", "inv", "gate", "row",
                                           "stored")}

        def gate_pe(b):
            nc.tensor.wait_ge(at[1].xa, (b + 1) * QT)
            for c in range(C):
                for q in range(QT):
                    mm = nc.tensor.transpose(PS[:, c, q * P:(q + 1) * P], xs[:, q, c * P:(c + 1) * P], ident[:, :])
                mm.then_inc(g["xT"], 1)
            nc.tensor.wait_ge(g["xTs"], (b + 1) * C)
            for q in range(QT):
                for c in range(C):
                    mm = nc.tensor.matmul(PS[:, 6, q * E:(q + 1) * E], hT[:, c, q * P:(q + 1) * P], wgate[:, c, :],
                                          start=(c == 0), stop=(c == C - 1))
            mm.then_inc(g["mm"], 1)

        def gate_act(b):
            for c in range(C):
                nc.scalar.wait_ge(g["xT"], b * C + c + 1)
                nc.scalar.activation(hT[:, c, :], PS[:, c, :], ACT.Copy).then_inc(g["xTs"], 1)
            nc.scalar.wait_ge(g["sub"], b + 1)
            nc.scalar.activation(gexp[:, :, :], gexp[:, :, :], ACT.Exp).then_inc(g["exp"], 1)

        def gate_dve(b):
            logits = PS[:, 6, 0:QT * E].rearrange("p (q e) -> p q e", e=E)
            nc.vector.wait_ge(g["mm"], b + 1)
            nc.vector.tensor_reduce(gmax[:, :], logits, AX.X, ALU.max).then_inc(g["max"], 1)
            nc.vector.wait_ge(g["max"], b + 1)
            nc.vector.tensor_tensor(gexp[:, :, :], logits, gmax[:, :].unsqueeze(2).broadcast_to([P, QT, E]),
                                    ALU.subtract).then_inc(g["sub"], 1)
            nc.vector.wait_ge(g["exp"], b + 1)
            nc.vector.tensor_reduce(gsum[:, :], gexp[:, :, :], AX.X, ALU.add).then_inc(g["sum"], 1)
            nc.vector.wait_ge(g["sum"], b + 1)
            nc.vector.reciprocal(gmax[:, :], gsum[:, :]).then_inc(g["inv"], 1)
            nc.vector.wait_ge(g["inv"], b + 1)
            nc.vector.tensor_tensor(gates[:, bass.ds(b * QT, QT), :], gexp[:, :, :],
                                    gmax[:, :].unsqueeze(2).broadcast_to([P, QT, E]), ALU.mult)\
                .then_inc(g["gate"], 1)
            nc.vector.tensor_tensor(xn[:, :, D:RW], gexp[:, :, :],
                                    gmax[:, :].unsqueeze(2).broadcast_to([P, QT, E]), ALU.mult)\
                .then_inc(g["row"], 1)

        def gate_sp(b):
            tiles = out.rearrange("b (q p) d -> p (b q) d", p=P)
            hold(nc.sync, "sp", at[1].xa, (b + 1) * QT)
            nc.sync.dma_start(tiles[:, bass.ds(b * QT, QT), :], xs[:, :, :]).then_inc(g["stored"], 16)
            hold(nc.sync, "sp", ln[3].xn, (b + 1) * QT)
            hold(nc.sync, "sp", g["row"], b + 1)
            nc.sync.dma_start(rows.rearrange("(n p) w -> p n w", p=P)[:, bass.ds(b * QT, QT), :], xn[:, :, :])\
                .then_inc(g["stored"], 16)
            hold(nc.sync, "sp", g["stored"], (b + 2) * 32)

        def xtile(b, q):
            return x[:, bass.ds(b * QT + q, 1), :].rearrange("p a d -> p (a d)")


        ro = {n: sem("route_" + n) for n in ("b2", "consts", "pick", "spread", "gates", "rep", "cand", "count", "ok", "n", "more",
                                            "prefix", "above", "level", "need", "above_n", "level_n", "taken")}
        R_CONSTS = 5 * 16

        def route_pe():
            nc.tensor.wait_ge(ro["spread"], 1)
            for n in range(NT):
                mm = nc.tensor.matmul(PS[:, n // QT, (n % QT) * P:(n % QT + 1) * P],
                                      above_n[:, n * P:(n + 1) * P], ident[:, :],
                                      start=True, stop=True)
            mm.then_inc(ro["gates"], 1)
            nc.tensor.wait_ge(ro["consts"], R_CONSTS)
            with nc.tensor.Fori(0, ST) as k:
                nc.tensor.wait_ge(ro["ok"], k + 1)
                nc.tensor.matmul(PS[:, 7, 0:1], same[:, :], enough[:, :], start=True, stop=True)\
                    .then_inc(ro["n"], 1)

        def route_act():
            nc.scalar.wait_ge(ro["gates"], 1)
            nc.scalar.activation(gate_rep, PS[:, 0:QT, :].rearrange("p a b -> p (a b)"), ACT.Copy)\
                .then_inc(ro["rep"], 1)

        def route_dve():
            v = nc.vector
            v.wait_ge(g["gate"], B)
            v.tensor_copy(above_n.rearrange("p (n e l) -> p (n e) l", n=NT, e=E),
                          gates[:, :, :].rearrange("p n e -> p (n e)").unsqueeze(2).broadcast_to([P, NT * E, LANES]))\
                .then_inc(ro["spread"], 1)
            v.wait_ge(ro["consts"], R_CONSTS)
            v.tensor_copy(pick, pick_f).then_inc(ro["pick"], 1)
            v.memset(prefix[:, :], 0).then_inc(ro["prefix"], 1)
            v.wait_ge(ro["rep"], 1)
            with v.Fori(0, ST) as k:
                v.wait_ge(ro["prefix"], k + 1)
                v.tensor_tensor(cand[:, :], prefix[:, :], lanes[:, bass.ds(k, 1)], ALU.bitwise_or)\
                    .then_inc(ro["cand"], 1)
                v.wait_ge(ro["cand"], k + 1)
                v.tensor_scalar(level, gate_rep, cand[:, :].bitcast(fp32), None, ALU.is_ge, ALU.add,
                                accum_out=count[:, :]).then_inc(ro["count"], 1)
                v.wait_ge(ro["count"], k + 1)
                v.tensor_scalar(enough[:, :], count[:, :], CAP - 0.5, None, ALU.is_ge).then_inc(ro["ok"], 1)
                v.wait_ge(ro["n"], k + 1)
                v.tensor_scalar(more[:, :], PS[:, 7, 0:1], -1.0, steps[:, bass.ds(k, 1)], ALU.add, ALU.mult)\
                    .then_inc(ro["more"], 1)
                v.wait_ge(ro["more"], k + 1)
                v.tensor_tensor(prefix[:, :], prefix[:, :], more[:, :], ALU.bitwise_or).then_inc(ro["prefix"], 1)
            least = prefix[:, :].bitcast(fp32)
            v.wait_ge(ro["prefix"], ST + 1)
            v.tensor_scalar(above, gate_rep, least, None, ALU.is_gt, ALU.add, accum_out=count[:, :])\
                .then_inc(ro["above"], 1)
            v.tensor_scalar(level, gate_rep, least, None, ALU.is_equal).then_inc(ro["level"], 1)
            v.wait_ge(ro["above"], 1)
            v.tensor_scalar(need[:, :], count[:, :], -1.0, float(CAP), ALU.mult, ALU.add).then_inc(ro["need"], 1)
            v.tensor_tensor_scan(above_n, above, above, 0.0, ALU.add, ALU.max).then_inc(ro["above_n"], 1)
            v.wait_ge(ro["level"], 1)
            v.tensor_tensor_scan(level_n, level, level, 0.0, ALU.add, ALU.max).then_inc(ro["level_n"], 1)
            v.wait_ge(ro["level_n"], 1)
            v.wait_ge(ro["above_n"], 1)
            v.wait_ge(ro["need"], 1)
            v.scalar_tensor_tensor(out=taken_n, in0=level_n, scalar=need[:, 0:1], in1=above_n,
                                   op0=ALU.min, op1=ALU.add).then_inc(ro["taken"], 1)

        mo = {n: sem("moe_" + n) for n in ("w0", "w1", "taken", "idx_f", "idx", "xg", "tr", "gT", "h", "act", "y", "b",
                                          "yw", "add", "added")}
        FE = F1 // P
        IDX0 = HALVES

        def index_pe(e):
            hold(nc.tensor, "pe", mo["idx_f"], e * HALVES + IDX0)
            for n in range(QT):
                mm = nc.tensor.matmul(PS[:, n, :], pick[:, bass.ds(e * P, P)], taken_n[:, n * CH:(n + 1) * CH],
                                      start=True, stop=True)
            mm.then_inc(mo["taken"], 1)

        def index_dve(e, ring_at):
            v = nc.vector
            v.wait_ge(mo["taken"], e + 1)
            v.wait_ge(mo["idx"], e + 1)
            for h in range(HALVES):
                v.tensor_scalar((above, level)[h], PS[:, 0:QT, :].rearrange("p a b -> p (a b)"), slot[:, h:h + 1], None,
                                ALU.is_le, ALU.add, accum_out=idx_f[:, ring_at, h:h + 1]).then_inc(mo["idx_f"], 1)
            v.wait_ge(mo["idx_f"], (e + 1) * HALVES + IDX0)
            v.wait_ge(mo["added"], e + 1)
            v.tensor_copy(idx[:, ring_at, :], idx_f[:, ring_at, :]).then_inc(mo["idx"], 1)

        def gather_pool(e, ring_at):
            hold(nc.gpsimd, "pool", mo["idx"], e + 2)
            hold(nc.gpsimd, "pool", mo["yw"], (e - 2) * HALVES + 3 * HALVES)
            for h in range(HALVES):
                nc.gpsimd.indirect_dma_start(
                    out=xg[:, ring_at, h, :], out_offset=None, in_=rows[:, :],
                    in_offset=bass.IndirectOffsetOnAxis(ap=idx[:, ring_at, h:h + 1], axis=0))\
                    .then_inc(mo["xg"], 16)

        def expert_pe(e, ring_at):
            of_ring = e // 2 if isinstance(e, int) else (e - ring_at) // 2
            nc.tensor.wait_ge(mo["xg"], (e + 1) * HALVES * 16)
            nc.tensor.wait_ge(mo["gT"], e * C + C)
            for c in range(C):
                for h in range(HALVES):
                    mm = nc.tensor.transpose(PS[:, 4, c * CAP + h * P:c * CAP + (h + 1) * P],
                                             xg[:, ring_at, h, c * P:(c + 1) * P], ident[:, :])
            mm.then_inc(mo["tr"], 1)
            nc.tensor.wait_ge(mo["gT"], (e + 1) * C + C)
            nc.tensor.wait_ge(mo[f"w{ring_at}"], (of_ring + 1) * 32)
            for f in range(FE):
                if f % 2 == 0:
                    nc.tensor.wait_ge(mo["act"], e * FE + f - 2 + 4)
                for c in range(C):
                    mm = nc.tensor.matmul(PS[:, 5 + f // 2 % 2, f % 2 * CAP:(f % 2 + 1) * CAP],
                                          fc1[ring_at][:, c, f * P:(f + 1) * P], gT[:, ring_at, c, :],
                                          start=(c == 0), stop=(c == C - 1))
                if f % 2 == 1:
                    mm.then_inc(mo["h"], 1)
            nc.tensor.wait_ge(mo["act"], (e + 1) * FE + 4)
            nc.tensor.wait_ge(mo["b"], (e - 1) * HALVES + 2 * HALVES)
            for h in range(HALVES):
                for f in range(FE):
                    mm = nc.tensor.matmul(PS[:, 7, h * D:(h + 1) * D], yT[:, ring_at, f, h * P:(h + 1) * P],
                                          fc2[ring_at][:, f, :], start=(f == 0), stop=(f == FE - 1))
            mm.then_inc(mo["y"], 1)

        def expert_act(e, ring_at):
            for c in range(C):
                nc.scalar.wait_ge(mo["tr"], e + 1)
                nc.scalar.activation(gT[:, ring_at, c, :], PS[:, 4, c * CAP:(c + 1) * CAP], ACT.Identity,
                                     bias=col["L1_cond_mlp_b"][:, c:c + 1], scale=col["L1_cond_mlp_g"][:, c:c + 1])\
                    .then_inc(mo["gT"], 1)
            for f in range(FE):
                hold(nc.scalar, "act", mo["h"], e * (FE // 2) + f // 2 + 1)
                nc.scalar.activation(yT[:, ring_at, f, :], PS[:, 5 + f // 2 % 2, f % 2 * CAP:(f % 2 + 1) * CAP],
                                     ACT.Gelu_apprx_tanh, bias=col["L1_cond_b1s"][:, bass.ds(e * FE + f, 1)])\
                    .then_inc(mo["act"], 1)

        def expert_dve(e, ring_at):
            v = nc.vector
            v.wait_ge(mo["y"], e + 1)
            v.wait_ge(mo["added"], e + 1)
            for h in range(HALVES):
                v.tensor_tensor(yout[:, ring_at, h, :], PS[:, 7, h * D:(h + 1) * D], b2all[:, bass.ds(e * D, D)],
                                ALU.add).then_inc(mo["b"], 1)
            for h in range(HALVES):
                v.wait_ge(mo["b"], e * HALVES + h + 1 + HALVES)
                v.tensor_scalar(yout[:, ring_at, h, :], yout[:, ring_at, h, :],
                                xg[:, ring_at, h, bass.ds(D + e, 1)], None, ALU.mult).then_inc(mo["yw"], 1)

        def scatter_pool(e, ring_at):
            hold(nc.gpsimd, "pool", mo["yw"], (e + 1) * HALVES + HALVES)
            for h in range(HALVES):
                nc.gpsimd.indirect_dma_start(
                    out=out.rearrange("b l d -> (b l) d"),
                    out_offset=bass.IndirectOffsetOnAxis(ap=idx[:, ring_at, h:h + 1], axis=0),
                    in_=yout[:, ring_at, h, :], in_offset=None, compute_op=ALU.add).then_inc(mo["add"], 16)
            nc.gpsimd.wait_ge(mo["add"], (e + 1) * 32)
            nc.gpsimd.sem_inc(mo["added"], 1)

        def experts(eng, index, expert):
            index(0, 0)
            with eng.Fori(0, E // 2 - 1) as pair:
                index(2 * pair + 1, 1)
                expert(2 * pair, 0)
                index(2 * pair + 2, 0)
                expert(2 * pair + 1, 1)
            index(E - 1, 1)
            expert(E - 2, 0)
            expert(E - 1, 1)

        def weights_sp(e, ring_at):
            nc.sync.dma_start(fc1[ring_at], t["L1_cond_fc1s"][bass.ds(e, 1)].rearrange("a (c p) f -> p (a c) f", p=P))\
                .then_inc(mo[f"w{ring_at}"], 16)
            nc.sync.dma_start(fc2[ring_at], t["L1_cond_fc2s"][bass.ds(e, 1)].rearrange("a (f p) d -> p (a f) d", p=P))\
                .then_inc(mo[f"w{ring_at}"], 16)

        def experts_sp():
            hold(nc.sync, "sp", at[1].s, B * H * QT)
            for e in range(2):
                weights_sp(e, e)
            with nc.sync.Fori(0, E // 2 - 1) as pair:
                for ring_at in range(2):
                    hold(nc.sync, "sp", mo["y"], 2 * pair + ring_at + 1)
                    weights_sp(2 * pair + ring_at + 2, ring_at)

        N_VEC = 7
        block = ctx.enter_context(nc.Block())

        @block.sync
        def _(sp):
            sp.sem_inc(g["stored"], 32)
            sp.dma_start(x[:, :, :], t["x"].rearrange("b (q p) d -> p (b q) d", p=P)).then_inc(s_x, 16)
            sp.dma_start(condT[:, :, :], t["condT"].rearrange("(c p) b -> p c b", p=P)).then_inc(s_vec, 16)
            sp.dma_start(wt, t["L0_cond_Wt"].rearrange("(c p) n -> p c n", p=P)).then_inc(s_vec, 16)
            sp.dma_start(wada, t["L1_cond_W_ada"].rearrange("(c p) n -> p c n", p=P)).then_inc(s_vec, 16)
            sp.dma_start(cols[:, :], t["cols"]).then_inc(s_vec, 16)
            sp.dma_start(b2b[:, :], t["L0_cond_b2"].partition_broadcast(P)).then_inc(s_vec, 16)
            sp.dma_start(tscale[:, :], t["L0_cond_torus_scale"].partition_broadcast(P)).then_inc(s_vec, 16)
            sp.dma_start(mask_u8[:, :], t["mask_BxS_bf1"].rearrange("(a b) l -> a (b l)", a=1)).then_inc(s_vec, 16)
            sp.dma_start(wqkv0[:, :, :], t["L0_cond_Wqkv"].rearrange("(c p) n -> p c n", p=P)).then_inc(s_w0, 16)
            sp.dma_start(dist[:, :].rearrange("p (q l) -> p q l", q=QT),
                         t["L0_cond_torus_dist"].rearrange("a (q p) l -> p (a q) l", p=P)).then_inc(s_w0, 16)
            sp.dma_start(wout0[:, :, :], t["L0_cond_Wout"].rearrange("(c p) n -> p c n", p=P)).then_inc(s_w0, 16)
            sp.dma_start(w1[:, :, :], t["L0_cond_W1"].rearrange("(c p) n -> p c n", p=P)).then_inc(s_w0, 16)
            sp.dma_start(w2[:, :, :], t["L0_cond_W2"].rearrange("(c p) n -> p c n", p=P)).then_inc(s_w0, 16)
            sp.wait_ge(s_pen, 1)
            sp.wait_ge(s_const, 2)
            with sp.Fori(0, B) as b:
                stacks0_sp(b)
            sp.wait_ge(ff["y"], B * QT)
            sp.dma_start(pick_f, t["pick"]).then_inc(ro["consts"], 16)
            for dst, name in ((lanes, "lanes"), (steps, "steps"), (same, "same"), (slot, "slot")):
                sp.dma_start(dst[:, :], t[name]).then_inc(ro["consts"], 16)
            with sp.Fori(0, B) as b:
                stacks1_sp(b)
                gate_sp(b)
            experts_sp()

        @block.gpsimd
        def _(pool):
            pool.memset(ident[:, :], 0.0).then_inc(s_ident, 1)
            pool.memset(mhalf[:, :], -0.5).then_inc(s_const, 1)
            pool.wait_ge(s_ident, 1)
            pool.affine_select(out=ident[:, :], in_=ident[:, :], compare_op=ALU.not_equal, fill=1.0,
                               base=0, pattern=[[-1, P]], channel_multiplier=1).then_inc(s_ident, 1)
            pool.dma_start(wgate[:, :, :], t["L1_cond_Wgate"].rearrange("(c p) n -> p c n", p=P)).then_inc(s_w1, 16)
            pool.dma_start(wqkv1[:, :, :], t["L1_cond_Wqkv"].rearrange("(c p) n -> p c n", p=P)).then_inc(s_w1, 16)
            pool.dma_start(wout1[:, :, :], t["L1_cond_Wout"].rearrange("(c p) n -> p c n", p=P)).then_inc(s_w1, 16)
            pool.wait_ge(s_w0, 80)
            with pool.Fori(0, B) as b:
                norm_pool(0, b)
                proj0_pool(b)
                bias_pool(b)
                norm_pool(1, b)
            with pool.Fori(0, B) as b:
                norm_pool(2, b)
                proj1_pool(b)
                norm_pool(3, b)
            pool.sem_inc(mo["added"], 2)
            pool.wait_ge(at[1].pv, B * H + CO)
            pool.dma_start(b2all, t["L1_cond_b2s"].rearrange("e d -> (e d)").partition_broadcast(P))\
                .then_inc(ro["b2"], 16)
            pool.wait_ge(g["stored"], (B + 1) * 32)
            experts(pool, gather_pool, scatter_pool)
            pool.wait_ge(mo["add"], E * 32)

        @block.scalar
        def _(act):
            credits(act, "act")
            act.wait_ge(s_vec, N_VEC * 16)
            act.activation(gelT[:, :, :], condT[:, :, :], ACT.Gelu_apprx_tanh).then_inc(cond_act, 1)
            act.activation(silT[:, :, :], condT[:, :, :], ACT.Silu).then_inc(cond_act, 1)
            act.wait_ge(cond_vec, 12)
            with act.Fori(0, B) as b:
                norm_act(0, b)
                proj0_act(b)
                attn_act(0, b)
                out_act(0, b)
                norm_act(1, b)
                ffn_act(b)
            with act.Fori(0, B) as b:
                norm_act(2, b)
                proj1_act(b)
                attn_act(1, b)
                out_act(1, b)
                gate_act(b)
            route_act()
            act.sem_inc(mo["gT"], C)
            act.sem_inc(mo["act"], 4)
            experts(act, lambda e, ring_at: None, expert_act)

        @block.tensor
        def _(pe):
            credits(pe, "pe")
            pe.wait_ge(s_ident, 2)
            pe.wait_ge(s_vec, N_VEC * 16)
            pe.wait_ge(cond_act, 2)
            for m in range(3 * C):
                w, act_in, off = (wt, gelT, m * P) if m < 2 * C else (wada, silT, (m - 2 * C) * P)
                for c in range(C):
                    mm = pe.matmul(PS[:, 7, m * B:(m + 1) * B], w[:, c, off:off + P], act_in[:, c, :],
                                   start=(c == 0), stop=(c == C - 1))
            mm.then_inc(cond_mm, 1)
            pe.wait_ge(s_w0, 80)
            pe.wait_ge(cond_vec, 12)
            with pe.Fori(0, B) as b:
                norm_pe(0, b)
                proj0_pe(b)
                pe.wait_ge(at[0].stack, (b + 1) * STACK0)
                pe.wait_ge(at[0].vs, (b + 1) * QT)
                attn_pe(0, b)
                out_pe(0, b)
                norm_pe(1, b)
                ffn_pe(b)
                pe.wait_ge(ff["x"], (b + 1) * QT)
            pe.wait_ge(s_w1, 3 * 16)
            pe.wait_ge(w_centred, 2 + 2 * C)
            with pe.Fori(0, B) as b:
                norm_pe(2, b)
                proj1_pe(b)
                pe.wait_ge(at[1].stack, (b + 1) * STACK1)
                pe.wait_ge(at[1].vs, (b + 1) * 2 * QT)
                attn_pe(1, b)
                out_pe(1, b)
                gate_pe(b)
            route_pe()
            pe.wait_ge(ro["taken"], 1)
            pe.wait_ge(ro["pick"], 1)
            pe.wait_ge(ro["rep"], 1)
            experts(pe, lambda e, ring_at: index_pe(e), expert_pe)

        @block.vector
        def _(dve):
            credits(dve, "dve")
            dve.memset(q_stack[6 * HD0:6 * HD0 + 1, :, :], 1.0).then_inc(s_const, 1)
            dve.wait_ge(s_vec, N_VEC * 16)
            dve.tensor_scalar(pen[:, :], mask_u8[:, :], 1.0, -NEG, ALU.subtract, ALU.mult).then_inc(s_pen, 1)
            dve.wait_ge(cond_mm, 1)
            modes = [(col["L0_cond_bt"][:, m:m + 1]) for m in range(2 * C)] + [col["L1_cond_b_ada"][:, c:c + 1] for c in range(C)]
            for m in range(3 * C):
                dve.tensor_scalar(tp[:, m, :], PS[:, 7, m * B:(m + 1) * B], modes[m],
                                  1.0 if m < C else 0.0, ALU.add, ALU.add).then_inc(cond_vec, 1)
            dve.wait_ge(cond_vec, 3 * C)
            for c in range(C):
                gc, bc = col["L0_cond_ln1_g"][:, c:c + 1], col["L0_cond_ln1_b"][:, c:c + 1]
                dve.tensor_scalar(gain[0][:, c, :], tp[:, c, :], gc, None, ALU.mult).then_inc(cond_vec, 1)
                dve.scalar_tensor_tensor(out=shift[0][:, c, :], in0=tp[:, c, :], scalar=bc, in1=tp[:, C + c, :],
                                         op0=ALU.mult, op1=ALU.add).then_inc(cond_vec, 1)
                dve.tensor_scalar(shift[2][:, c, :], tp[:, 2 * C + c, :], col["L1_cond_ln1_b"][:, c:c + 1], None,
                                  ALU.add).then_inc(cond_vec, 1)
            for c in range(C):
                for n, name in ((1, "L0_cond_ln2"), (2, "L1_cond_ln1")):
                    dve.tensor_scalar(gain[n][:, c, :], tp[:, c, :], 0.0, col[name + "_g"][:, c:c + 1],
                                      ALU.mult, ALU.add).then_inc(cond_vec, 1)
                dve.tensor_scalar(shift[1][:, c, :], tp[:, c, :], 0.0, col["L0_cond_ln2_b"][:, c:c + 1],
                                  ALU.mult, ALU.add).then_inc(cond_vec, 1)
            dve.wait_ge(s_x, 16)
            with dve.Fori(0, B) as b:
                norm_dve(0, b, xtile)
                proj0_dve(b)
                attn_dve(0, b)
                out_dve(0, b)
                hold(dve, "dve", at[0].xa, (b + 1) * QT)
                norm_dve(1, b, xtile)
                ffn_dve(b)
            dve.wait_ge(ff["b"], B * QT)
            dve.wait_ge(s_w1, 3 * 16)
            dve.tensor_scalar(qkf[:, 0:2], qkg[:, 0:2], 0.5, None, ALU.mult).then_inc(w_centred, 1)
            dve.tensor_scalar(qkf[:, 2:4], qkg[:, 2:4], 2.0 * HD1 ** -0.5, None, ALU.mult).then_inc(w_centred, 1)
            for c in range(C):
                wc = wqkv1[:, c, 0:2 * W1V].rearrange("p (h d) -> p h d", d=HD1)
                dve.tensor_reduce(wmean[:, c, :], wc, AX.X, ALU.add).then_inc(s_mean, 1)
                dve.wait_ge(s_mean, 2 * c + 1)
                dve.tensor_scalar(wmean[:, c, :], wmean[:, c, :], 1.0 / HD1, None, ALU.mult).then_inc(s_mean, 1)
                dve.wait_ge(s_mean, 2 * c + 2)
                dve.tensor_tensor(wc, wc, wmean[:, c, :].unsqueeze(2).broadcast_to([P, 2 * H, HD1]),
                                  ALU.subtract).then_inc(w_centred, 2)
            with dve.Fori(0, B) as b:
                hold(dve, "dve", g["stored"], (b + 1) * 32)
                norm_dve(2, b, xtile)
                proj1_dve(b)
                attn_dve(1, b)
                out_dve(1, b)
                hold(dve, "dve", at[1].xa, (b + 1) * QT)
                norm_dve(3, b, lambda b, q: xs[:, q, :])
                gate_dve(b)
            route_dve()
            dve.sem_inc(mo["idx_f"], IDX0)
            dve.sem_inc(mo["idx"], 1)
            dve.sem_inc(mo["b"], HALVES)
            dve.sem_inc(mo["yw"], HALVES)
            dve.wait_ge(ro["b2"], 16)
            experts(dve, index_dve, expert_dve)


FEATURE_COLS = [("L0_cond_ln1_g", 2), ("L0_cond_ln1_b", 2), ("L0_cond_ln2_g", 2), ("L0_cond_ln2_b", 2),
                ("L1_cond_ln1_g", 2), ("L1_cond_ln1_b", 2), ("L1_cond_mlp_g", 2), ("L1_cond_mlp_b", 2),
                ("L1_cond_b_ada", 2), ("L0_cond_bt", 4), ("L0_cond_b1", 8), ("L1_cond_b1s", 64)]
_PAIR_COLS = ["L1_cond_qn_g", "L1_cond_qn_b", "L1_cond_kn_g", "L1_cond_kn_b"]
_PLAIN = ["x", "mask_BxS_bf1", "L0_cond_torus_dist", "L0_cond_Wqkv", "L0_cond_Wout", "L0_cond_torus_scale",
          "L0_cond_W1", "L0_cond_W2", "L0_cond_b2", "L0_cond_Wt", "L1_cond_b2s"]
_TURNED = {"condT": "cond_1024", "L1_cond_W_ada": "L1_cond_W_ada", "L1_cond_Wqkv": "L1_cond_Wqkv",
           "L1_cond_Wout": "L1_cond_Wout", "L1_cond_Wgate": "L1_cond_Wgate", "L1_cond_fc1s": "L1_cond_fc1s",
           "L1_cond_fc2s": "L1_cond_fc2s"}


def kernel(**inputs):
    import numpy as _np
    import concourse.bacc as _bacc
    from concourse import mybir as _mybir
    from concourse.bass_utils import run_bass_kernel_spmd as _run

    nc = _bacc.Bacc("TRN2", target_bir_lowering=False, num_devices=1)
    laid = {n: _np.asarray(inputs[n]) for n in _PLAIN}
    laid.update({n: _np.swapaxes(_np.asarray(inputs[src]), -1, -2) for n, src in _TURNED.items()})
    laid["cols"] = _np.concatenate(
        [_np.asarray(inputs[n]).reshape(-1, 128).T for n, _ in FEATURE_COLS]
        + [_np.tile(_np.asarray(inputs[n]), 2)[:, None] for n in _PAIR_COLS], axis=1)
    part, ex = _np.arange(128), laid["L1_cond_b2s"].shape[0]
    lane, shifts = part % (128 // ex), 28 - 4 * _np.arange(8)
    laid["lanes"] = (_np.minimum(lane[:, None], _np.where(shifts == 28, 7, 15)) << shifts).astype(_np.int32)
    laid["steps"] = _np.broadcast_to((2.0 ** shifts).astype(_np.float32), (128, 8))
    laid["same"] = (part[:, None] // (128 // ex) == part // (128 // ex)).astype(_np.float32)
    laid["slot"] = (part[:, None] + 128 * _np.arange(2)).astype(_np.float32)
    laid["pick"] = _np.repeat((part[:, None] == (128 // ex) * _np.arange(ex)).astype(_np.float32), 128, axis=1)
    arrays, aps = {}, {}
    for name, a in laid.items():
        a = _np.ascontiguousarray(a)
        arrays[f"in_{name}"] = a
        aps[name] = nc.dram_tensor(f"in_{name}", a.shape, _mybir.dt.from_np(a.dtype), kind="ExternalInput").ap()
    out = nc.dram_tensor("out_0", laid["x"].shape, _mybir.dt.float32, kind="ExternalOutput").ap()
    cond_seq_kernel(nc, aps, out)
    r = _run(nc, [arrays], core_ids=[0])
    return r.results[0]["out_0"]
```

```python
import concourse.bass as bass
from concourse import mybir
from contextlib import ExitStack


def cond_seq_kernel(nc, t, out, stop_after=None):
    fp32 = mybir.dt.float32
    fp16 = mybir.dt.float16
    bf16 = mybir.dt.bfloat16
    i32 = mybir.dt.int32
    u32 = mybir.dt.uint32
    u8 = mybir.dt.uint8
    ALU = mybir.AluOpType
    ACT = mybir.ActivationFunctionType
    AX = mybir.AxisListType

    B, L, D = t["x"].shape
    P = 128
    H = t["L0_cond_torus_scale"].shape[0]
    HD0 = D // H
    HD1 = 64
    C = D // P
    QT = L // P
    NT = B * QT
    F0 = t["L0_cond_W1"].shape[1]
    FT = F0 // P
    E, _, F1 = t["L1_cond_fc1s"].shape
    W1V = H * HD1
    JT = W1V // P
    EPS = 1e-5
    CAP = B * L // E
    HALVES = CAP // P
    PAIRS = H // 2
    CH = 512
    G8 = CH // HD1
    RW = D + E
    NEG = -1e30
    LANES = P // E

    ctx = ExitStack()
    with ctx:
        def sb(name, shape, dt=fp32):
            return ctx.enter_context(nc.sbuf_tensor(name, shape, dt))

        def sem(name):
            return ctx.enter_context(nc.semaphore(name))

        qk_parts = nc.dram_tensor("qk_parts", (3, 4 * P, L), bf16, kind="Internal").ap()
        pen_rows = nc.dram_tensor("pen_rows", (1, B * L), bf16, kind="Internal").ap()
        rows = nc.dram_tensor("routed_rows", (B * L, RW), fp32, kind="Internal").ap()

        x = sb("x", [P, NT, D])
        ident = sb("ident", [P, P])
        JT0 = H // 4
        w_sizes = [C * 3 * D, JT0 * D, C * F0, FT * D]
        w0buf = sb("w0buf", [P, sum(w_sizes)])
        w_at = [sum(w_sizes[:k]) for k in range(5)]
        wqkv0, wout0, w1, w2 = [w0buf[:, w_at[k]:w_at[k + 1]].rearrange("p (c n) -> p c n", c=c)
                                for k, c in enumerate((C, JT0, C, FT))]
        wq1buf = sb("wq1buf", [P, C * 3 * W1V])
        wqkv1 = wq1buf[:, :].rearrange("p (c n) -> p c n", c=C)
        wout1 = sb("wout1", [P, JT, D])
        wgate = sb("wgate", [P, C, E])
        hT = sb("hT", [P, C, L])
        xn = sb("xn", [P, QT, RW])
        q_stack = sb("q_stack", [P, H, L], bf16)
        k_stack = sb("k_stack", [P, H, L], bf16)
        kl_stack = sb("kl_stack", [P, H, L], fp16)
        vals_flat = sb("vals", [P, QT * W1V])
        obuf = sb("obuf", [P, QT * W1V])
        RB = QT * L
        ring = sb("ring", [P, 4 * RB])
        v_now = sb("v_now", [P, 4 * QT * HD1])

        q16 = q_stack[:, :, :].bitcast(fp16)
        k16 = k_stack[:, :, :].bitcast(fp16)
        vals = [vals_flat[:, 0:QT * w].rearrange("p (q w) -> p q w", q=QT) for w in (D, W1V)]
        dist = vals_flat[:, QT * W1V - QT * L:QT * W1V]
        xs = w0buf[:, 2 * RB:2 * RB + QT * D].rearrange("p (q d) -> p q d", q=QT)
        mask_u8 = obuf[0:1, 0:B * L // 4].bitcast(u8)
        pen = obuf[0:1, B * L // 4:B * L // 4 + B * L // 2].bitcast(bf16)
        bias_ring = kl_stack[:, :, :].rearrange("p h l -> p (h l)").bitcast(fp32)
        probs = [ring[:, r * RB:(r + 1) * RB] for r in (0, 1)]
        probsT = [[ring[:, 2 * RB:3 * RB], ring[:, 3 * RB:4 * RB], far[:, 0:RB], far[:, RB:2 * RB]]
                  for far in (wq1buf, w0buf)]
        sum_rep, sum_T = [[far[:, at_:at_ + CH] for far, at_ in ((wq1buf, 2 * RB + d), (w0buf, 2 * RB + QT * D + d))]
                          for d in (0, CH)]
        OW = (2 * HD0, HD1)
        v_heads = [v_now[:, 0:4 * QT * w].rearrange("p (h q w) -> p h q w", h=4, q=QT) for w in OW]
        split0 = [ring[:, r * RB // 2:(r + 1) * RB // 2].bitcast(bf16)
                  .rearrange("p (m l) -> p m l", m=4) for r in range(3)]
        rest0 = ring[:, 2 * RB:3 * RB].rearrange("p (m l) -> p m l", m=4)
        hi1 = ring[:, 0:2 * RB].bitcast(fp16).rearrange("p (w c l) -> p w c l", w=2, c=PAIRS)
        lo1 = ring[:, 2 * RB:4 * RB].bitcast(fp16).rearrange("p (w c l) -> p w c l", w=2, c=PAIRS)
        sq1 = [obuf[:, r * CH:(r + 1) * CH] for r in (0, 1)]
        qn1 = [obuf[:, r * CH:(r + 1) * CH] for r in (2, 3)]
        f1b = [obuf[:, r * CH:(r + 1) * CH] for r in (4, 5)]
        oT = obuf[:, 0:JT * L].rearrange("p (j l) -> p j l", j=JT)
        aT = obuf[:, 0:FT * L].rearrange("p (f l) -> p f l", f=FT)
        wt = ring[:, 0:C * 2 * D].rearrange("p (c n) -> p c n", c=C)
        wada = ring[:, C * 2 * D:C * 3 * D].rearrange("p (c n) -> p c n", c=C)

        negmax = sb("negmax", [P, 2, QT])
        rsum = sb("rsum", [P, 4, QT])
        rinv = sb("rinv", [P, 4, QT])
        scale_now = sb("scale_now", [P, 2])
        tscale = sb("tscale", [P, H])
        stats = sb("stats", [P, QT, 6])
        mv = sb("mv", [P, QT, 2])
        veps = sb("veps", [P, QT])
        rstd = sb("rstd", [P, QT])
        mhalf = sb("mhalf", [P, 16])
        ssum = sb("ssum", [P, 2, G8])
        v8 = sb("v8", [P, 2, G8])
        r8 = sb("r8", [P, 2, G8])
        condT = sb("condT", [P, C, B])
        gelT = sb("gelT", [P, C, B])
        silT = sb("silT", [P, C, B])
        cols = sb("cols", [P, t["cols"].shape[1]])
        col, at_col = {}, 0
        for n, k in FEATURE_COLS:
            col[n] = cols[:, at_col:at_col + k]
            at_col += k
        qkg = cols[:, at_col:at_col + 4]
        qkf = sb("qkf", [P, 4])
        b2b = sb("b2b", [P, D])
        gain = {0: sb("gain0", [P, C, B]), 1: sb("gain1", [P, C, B]), 2: sb("gain2", [P, C, B])}
        shift = {0: sb("shift0", [P, C, B]), 1: sb("shift1", [P, C, B]), 2: sb("shift2", [P, C, B])}
        tp = sb("tp", [P, 3 * C, B])
        wmean = sb("wmean", [P, C, 2 * H])
        gates = sb("gates", [P, NT, E])
        gmax = sb("gmax", [P, QT])
        gsum = sb("gsum", [P, QT])
        gexp = sb("gexp", [P, QT, E])

        ST = 32 // 4
        gate_rep = ring[:, 0:B * L]
        above = ring[:, B * L:3 * B * L // 2].bitcast(bf16)
        level = ring[:, 3 * B * L // 2:2 * B * L].bitcast(bf16)
        above_n = ring[:, 2 * B * L:3 * B * L]
        level_n = ring[:, 3 * B * L:4 * B * L]
        taken_n = obuf[:, 0:B * L // 2].bitcast(bf16)
        xg = obuf[:, B * L // 2:B * L // 2 + 2 * HALVES * RW].rearrange("p (r h w) -> p r h w", r=2, h=HALVES)
        b2all = vals_flat[:, 0:E * D]
        yout = vals_flat[:, E * D:E * D + 2 * HALVES * D].rearrange("p (r h d) -> p r h d", r=2, h=HALVES)
        gT = vals_flat[:, E * D + 2 * HALVES * D:E * D + 2 * HALVES * D + 2 * C * CAP]\
            .rearrange("p (r c s) -> p r c s", r=2, c=C)
        yT = kl_stack[:, :, :].rearrange("p h l -> p (h l)").bitcast(fp32)\
            .rearrange("p (r f s) -> p r f s", r=2, f=F1 // P)
        fc1, fc2 = [], []
        for buf in (q_stack, k_stack):
            flat = buf[:, :, :].rearrange("p h l -> p (h l)").bitcast(fp32)
            fc1.append(flat[:, 0:C * F1].rearrange("p (c f) -> p c f", c=C))
            fc2.append(flat[:, C * F1:2 * C * F1].rearrange("p (f d) -> p f d", d=D))
        pick_f = w0buf[:, 0:E * P]
        pick = w0buf[:, E * P:E * P + E * P // 2].bitcast(bf16)
        lanes = sb("lanes", [P, ST], i32)
        steps = sb("steps", [P, ST])
        same = sb("same", [P, P])
        slot = sb("slot", [P, HALVES])
        prefix = sb("prefix", [P, 1], i32)
        cand = sb("cand", [P, 1], i32)
        more = sb("more", [P, 1], i32)
        count = sb("count", [P, 1])
        enough = sb("enough", [P, 1])
        need = sb("need", [P, 1])
        idx_f = sb("idx_f", [P, 2, HALVES])
        idx = sb("idx", [P, 2, HALVES], u32)

        PS = ctx.enter_context(nc.psum_tensor("PS", [P, 8, CH], fp32))

        s_x = sem("s_x")
        s_vec = sem("s_vec")
        s_w0 = sem("s_w0")
        s_w1 = sem("s_w1")
        s_ident = sem("s_ident")
        s_const = sem("s_const")
        s_pen = sem("s_pen")
        s_pen_row = sem("s_pen_row")
        s_wq1 = sem("s_wq1")
        turn = {e: sem(f"turn_{e}") for e in ("pe", "act", "dve", "pool", "sp")}
        cond_act = sem("cond_act")
        cond_mm = sem("cond_mm")
        cond_vec = sem("cond_vec")
        w_centred = sem("w_centred")
        s_mean = sem("s_mean")

        def hold(eng, key, s, val):
            eng.wait_ge(s, val)
            eng.sem_inc(turn[key], 1)

        class Norm:
            def __init__(self, name):
                self.stats = sem(name + "_stats")
                self.aggr = sem(name + "_aggr")
                self.veps = sem(name + "_veps")
                self.rstd = sem(name + "_rstd")
                self.xn = sem(name + "_xn")
                self.tr = sem(name + "_tr")
                self.hT = sem(name + "_hT")

        ln = [Norm("ln_a"), Norm("ln_b"), Norm("ln_c"), Norm("ln_d")]

        def norm_dve(n, b, src, width_off=0):
            s = ln[n]
            for q in range(QT):
                nc.vector.bn_stats(stats[:, q, :], src(b, q)).then_inc(s.stats, 1)
            for q in range(QT):
                hold(nc.vector, "dve", s.stats, b * QT + q + 1)
                nc.vector.bn_aggr(mv[:, q, :], stats[:, q, :]).then_inc(s.aggr, 1)
            nc.vector.wait_ge(s.aggr, b * QT + QT)
            nc.vector.tensor_scalar(veps[:, :], mv[:, :, 1], EPS, None, ALU.add).then_inc(s.veps, 1)
            nc.vector.wait_ge(s.rstd, b + 1)
            for q in range(QT):
                nc.vector.tensor_scalar(xn[:, q, 0:D], src(b, q), mv[:, q, 0:1], rstd[:, q:q + 1],
                                        ALU.subtract, ALU.mult).then_inc(s.xn, 1)

        def norm_pool(n, b):
            s = ln[n]
            nc.gpsimd.wait_ge(s.veps, b + 1)
            nc.gpsimd.tensor_tensor(rstd[:, :], veps[:, :], mhalf[:, 0:QT], ALU.pow).then_inc(s.rstd, 1)

        def norm_pe(n, b):
            s = ln[n]
            for c in range(C):
                for q in range(QT):
                    if c == 0:
                        nc.tensor.wait_ge(s.xn, b * QT + q + 1)
                    mm = nc.tensor.transpose(PS[:, c, q * P:(q + 1) * P], xn[:, q, c * P:(c + 1) * P], ident[:, :])
                mm.then_inc(s.tr, 1)

        def norm_act(n, b):
            s = ln[n]
            for c in range(C):
                hold(nc.scalar, "act", s.tr, b * C + c + 1)
                nc.scalar.activation(hT[:, c, :], PS[:, c, :], ACT.Identity, bias=shift[n][:, c, bass.ds(b, 1)],
                                     scale=gain[n][:, c, bass.ds(b, 1)]).then_inc(s.hT, 1)

        class Attn:
            def __init__(self, name):
                self.s = sem(name + "_scores")
                self.mx = sem(name + "_max")
                self.ex = sem(name + "_exp")
                self.t = sem(name + "_probsT")
                self.ea = sem(name + "_evac_act")
                self.ed = sem(name + "_evac_dve")
                self.pv = sem(name + "_pv")
                self.ri = sem(name + "_rinv")
                self.rep = sem(name + "_rep")
                self.reph = sem(name + "_rep_head")
                self.rt = sem(name + "_repT")
                self.re = sem(name + "_repT_sbuf")
                self.o = sem(name + "_out")
                self.vst = sem(name + "_v_head")
                self.bias = sem(name + "_bias")
                self.scl = sem(name + "_scale")
                self.stack = sem(name + "_stack")
                self.qk = sem(name + "_qk")
                self.v = sem(name + "_v")
                self.vs = sem(name + "_v_sbuf")
                self.pr = sem(name + "_proj")
                self.xa = sem(name + "_x_added")

        at = [Attn("at0"), Attn("at1")]
        CS = 2 * QT
        CE = 1
        C2 = 2
        C1 = 1

        def credits(eng, which):
            for a in at:
                if which == "pe":
                    eng.sem_inc(a.t, CS)
                    eng.sem_inc(a.pv, C2)
                    eng.sem_inc(a.rt, C1)
                if which == "act":
                    eng.sem_inc(a.ex, CS)
                    eng.sem_inc(a.ea, CE)
                    eng.sem_inc(a.re, C1)
                if which == "dve":
                    eng.sem_inc(a.mx, CS)
                    eng.sem_inc(a.ed, CE)
                    eng.sem_inc(a.o, C1)
                    eng.sem_inc(a.ri, C2)
                if which == "pool":
                    eng.sem_inc(a.rep, C2)

        class Step:
            def __init__(self, k, b, g, j):
                t_ = 4 * g + j
                self.k, self.b, self.j, self.t = k, b, j, t_
                peeled = isinstance(g, int)
                self.scores = not peeled or t_ < H
                self.turned = not peeled or 1 <= t_ <= H
                self.n = b * H + t_
                self.slot = j
                self.last_slot = (j - 1) % 4
                half = lambda back: 2 * g + (j - back) // 2
                self.pair = b * PAIRS + half(0)
                self.last_pair = b * PAIRS + half(1)
                self.pv = (not peeled or 0 <= half(3 + (j % 2 == 0)) < PAIRS)
                self.pv_local = half(3 if j % 2 else 4)
                if peeled:
                    self.pv = 0 <= self.pv_local < PAIRS
                self.pv_pair = b * PAIRS + self.pv_local
                self.pv_kts = (0, 1) if j % 2 else (2, 3)
                self.pv_odd = ((j - (3 if j % 2 else 4)) // 2) % 2
                self.inv = j % 2 == 0 and (not peeled or 0 <= half(2) < PAIRS)
                self.inv_pair = b * PAIRS + half(2)
                self.inv_slot = (j - 2) % 4
                per = (H // 4, PAIRS)[k]
                if k == 0:
                    rt_local, nm_local = g - 1, g - 1
                    rt_here, nm_here = j == 2, j == 3
                else:
                    rt_local, nm_local = half(4), half(5)
                    rt_here, nm_here = j % 2 == 0, j % 2 == 1
                self.rt = rt_here and (not peeled or 0 <= rt_local < per)
                self.norm = nm_here and (not peeled or 0 <= nm_local < per)
                self.inv_tile = b * (H // 4) + g + (j - 2) // 4
                self.rt_tile, self.norm_tile, self.norm_local = b * per + rt_local, b * per + nm_local, nm_local
                self.rt_pairs = b * PAIRS + ((g - 1) * 2 + 2 if k == 0 else half(4) + 1)
                self.norm_pairs = b * PAIRS + ((g - 1) * 2 + 2 if k == 0 else half(5) + 1)
                self.pv_tile = b * per + (self.pv_local if k == 1 else
                                          (g + ((j - (3 if j % 2 else 4)) // 4)))

        def heads(eng, k, b, work):
            for j in range(4):
                work(Step(k, b, 0, j))
            with eng.Fori(1, H // 4) as g:
                for j in range(4):
                    work(Step(k, b, g, j))
            for j in range(4):
                work(Step(k, b, H // 4, j))

        def attn_pe(k, b):
            a = at[k]

            def step(s):
                def score(q):
                    hold(nc.tensor, "pe", (a.mx, a.ex)[k], s.n * QT + q + 1 - QT + CS)
                    if k == 0:
                        R = 6 * HD0 + 1
                        nc.tensor.matmul(PS[:, q, :], q_stack[0:R, s.t, q * P:(q + 1) * P], k_stack[0:R, s.t, :],
                                         start=True, stop=True).then_inc(a.s, 1)
                    else:
                        nc.tensor.matmul(PS[:, q, :], q16[:, s.t, q * P:(q + 1) * P], k16[:, s.t, :],
                                         start=True, stop=False)
                        nc.tensor.matmul(PS[:, q, :], q16[:, s.t, q * P:(q + 1) * P], kl_stack[:, s.t, :],
                                         start=False, stop=True).then_inc(a.s, 1)

                def turn_probs(kt):
                    m = s.n - 1
                    if kt == 0:
                        nc.tensor.wait_ge(a.ex, m * QT + QT + CS)
                    nc.tensor.wait_ge((a.ea, a.ed)[kt % 2], m * (QT // 2) + kt // 2 + CE)
                    for qq in range(QT):
                        mm = nc.tensor.transpose(PS[:, 4 + kt % 2, qq * P:(qq + 1) * P],
                                                 probs[s.last_slot % 2][:, qq * L + kt * P:qq * L + (kt + 1) * P],
                                                 ident[:, :])
                    mm.then_inc(a.t, 1)

                def weigh_values(kt):
                    if kt == 0:
                        both = (s.pv_pair * 2 + 2) * (QT // 2) + CE
                        nc.tensor.wait_ge(a.ea, both)
                        nc.tensor.wait_ge(a.ed, both)
                        nc.tensor.wait_ge(a.vst, s.pv_pair * 2 + 2)
                        if k == 1 or not s.pv_odd:
                            nc.tensor.wait_ge(a.o, s.pv_tile + C1)
                    for h in range(2):
                        slot = 2 * s.pv_odd + h
                        row = (slot * OW[0], h * OW[1])[k]
                        mm = nc.tensor.matmul(PS[row:row + OW[k], 6, :], v_heads[k][:, slot, kt, :],
                                              probsT[k][slot][:, kt * L:(kt + 1) * L],
                                              start=(kt == 0), stop=(kt == QT - 1))
                    if kt == QT - 1:
                        mm.then_inc(a.pv, 1)

                for half in range(2):
                    for q in (2 * half, 2 * half + 1):
                        if s.scores:
                            score(q)
                    for kt in (2 * half, 2 * half + 1):
                        if s.turned:
                            turn_probs(kt)
                    if half == 1 and s.rt:
                        nc.tensor.wait_ge(a.rep, s.rt_pairs + C2)
                        nc.tensor.wait_ge(a.re, s.rt_tile + C1)
                        for q in range(QT):
                            mm = nc.tensor.transpose(PS[:, 7, q * P:(q + 1) * P],
                                                     sum_rep[k][:, q * P:(q + 1) * P], ident[:, :])
                        mm.then_inc(a.rt, 1)
                    if s.pv:
                        weigh_values(s.pv_kts[half])

            heads(nc.tensor, k, b, step)

        def evac_probsT(eng, k, s, kt):
            a = at[k]
            if kt < 2:
                eng.wait_ge(a.pv, s.last_pair - 1 + C2)
            eng.wait_ge(a.t, (s.n - 1) * QT + kt + 1 + CS)
            dst, src = probsT[k][s.last_slot][:, kt * L:(kt + 1) * L], PS[:, 4 + kt % 2, :]
            if eng is nc.scalar:
                nc.scalar.activation(dst, src, ACT.Copy).then_inc(a.ea, 1)
            else:
                nc.vector.tensor_copy(dst, src).then_inc(a.ed, 1)

        def attn_act(k, b):
            a = at[k]

            def step(s):
                for q in range(QT):
                    if s.turned and q % 2 == 0:
                        evac_probsT(nc.scalar, k, s, q)
                    if s.scores:
                        if q == 0:
                            nc.scalar.wait_ge(a.ri, s.pair - 1 + C2)
                            if k == 1:
                                nc.scalar.wait_ge(a.t, (s.n - 1) * QT + CS)
                        nc.scalar.wait_ge(a.mx, s.n * QT + q + 1 + CS)
                        p = probs[s.slot % 2][:, q * L:(q + 1) * L]
                        nc.scalar.activation(p, p if k == 0 else PS[:, q, :], ACT.Exp,
                                             bias=negmax[:, s.slot % 2, q:q + 1], scale=(-1.0, 1.0)[k],
                                             accum_out=rsum[:, s.slot, q:q + 1]).then_inc(a.ex, 1)
                if s.rt:
                    nc.scalar.wait_ge(a.rt, s.rt_tile + 1 + C1)
                    nc.scalar.wait_ge(a.o, s.rt_tile + C1)
                    nc.scalar.activation(sum_T[k], PS[:, 7, :], ACT.Copy).then_inc(a.re, 1)

            heads(nc.scalar, k, b, step)

        def attn_dve(k, b):
            a = at[k]

            def step(s):
                par = s.slot % 2

                def maximum(q):
                    if k == 0 and q == 0:
                        nc.vector.wait_ge(a.t, (s.n - 1) * QT + CS)
                        nc.vector.wait_ge(a.bias, s.n + 1)
                    nc.vector.wait_ge(a.ex, (s.n - 2) * QT + q + 1 + CS)
                    if k == 0:
                        hold(nc.vector, "dve", a.s, s.n * QT + q + 1)
                        nc.vector.tensor_tensor_reduce(probs[par][:, q * L:(q + 1) * L], PS[:, q, :],
                                                       bias_ring[:, par * RB + q * L:par * RB + (q + 1) * L],
                                                       -1.0, 3e38, ALU.add, ALU.min,
                                                       negmax[:, par, q:q + 1]).then_inc(a.mx, 1)
                    else:
                        nc.vector.wait_ge(a.s, s.n * QT + q + 1)
                        nc.vector.tensor_reduce(negmax[:, par, q:q + 1], PS[:, q, :], AX.X, ALU.max,
                                                negate=True).then_inc(a.mx, 1)

                for half in range(2):
                    for q in (2 * half, 2 * half + 1):
                        if s.scores:
                            maximum(q)
                    if half == 0 and s.inv:
                        nc.vector.wait_ge(a.ex, (s.inv_pair + 1) * 2 * QT + CS)
                        nc.vector.wait_ge(a.rep, s.inv_pair - 1 + C2)
                        two = slice(s.inv_slot, s.inv_slot + 2)
                        nc.vector.reciprocal(rinv[:, two, :], rsum[:, two, :]).then_inc(a.ri, 1)
                    if s.turned:
                        evac_probsT(nc.vector, k, s, 2 * half + 1)
                    if half == 0 and s.norm:
                        nc.vector.wait_ge(a.re, s.norm_tile + 1 + C1)
                        nc.vector.wait_ge(a.pv, s.norm_pairs + C2)
                        nc.vector.tensor_tensor(oT[:, s.norm_local, :], PS[:, 6, :], sum_T[k], ALU.mult)\
                            .then_inc(a.o, 1)

            heads(nc.vector, k, b, step)

        def attn_pool(k, b):
            a = at[k]
            w = (HD0, HD1)[k]

            def bias(i, par):
                n = b * H + i
                hold(nc.gpsimd, "pool", a.mx, (n - 1) * QT + CS)
                nc.gpsimd.tensor_copy(scale_now[:, par:par + 1], tscale[:, bass.ds(i, 1)]).then_inc(a.scl, 1)
                hold(nc.gpsimd, "pool", a.scl, n + 1)
                nc.gpsimd.tensor_scalar(bias_ring[:, par * RB:(par + 1) * RB], dist, scale_now[:, par:par + 1],
                                        -1.0, ALU.mult, ALU.mult).then_inc(a.bias, 1)

            def step(s):
                if k == 0 and s.scores:
                    if s.j == 0:
                        bias(s.t, 0)
                    if s.j < 3:
                        bias(s.t + 1, (s.j + 1) % 2)
                if s.turned:
                    hold(nc.gpsimd, "pool", a.pv, s.last_pair - 1 + C2)
                    nc.gpsimd.tensor_copy(v_heads[k][:, s.last_slot, :, 0:w],
                                          vals[k][:, :, bass.ds((s.t - 1) * w, w)]).then_inc(a.vst, 1)
                if s.inv:
                    hold(nc.gpsimd, "pool", a.ri, s.inv_pair + 1 + C2)
                    if k == 1:
                        hold(nc.gpsimd, "pool", a.rt, s.inv_pair + C1)
                    elif s.inv_slot == 0:
                        hold(nc.gpsimd, "pool", a.rt, s.inv_tile + C1)
                    per_tile = (4, 2)[k]
                    dst = sum_rep[k].rearrange("p (q h w) -> p q h w", q=QT, h=per_tile)
                    at_h = s.inv_slot if k == 0 else 0
                    for h in range(2):
                        nc.gpsimd.tensor_copy(dst[:, :, at_h + h, :],
                                              rinv[:, s.inv_slot + h, :].unsqueeze(2).broadcast_to([P, QT, OW[k]]))\
                            .then_inc(a.reph, 1)
                    hold(nc.gpsimd, "pool", a.reph, (s.inv_pair + 1) * 2)
                    nc.gpsimd.sem_inc(a.rep, 1)

            hold(nc.gpsimd, "pool", a.vs, (b + 1) * (QT, 2 * QT)[k])
            heads(nc.gpsimd, k, b, step)

        def out_pe(k, b):
            a = at[k]
            jt, w = ((JT0, wout0), (JT, wout1))[k]
            nc.tensor.wait_ge(a.o, (b + 1) * jt + C1)
            for q in range(QT):
                for j in range(jt):
                    mm = nc.tensor.matmul(PS[:, 2 + q, 0:D], oT[:, j, q * P:(q + 1) * P], w[:, j, :],
                                          start=(j == 0), stop=(j == jt - 1))
                mm.then_inc(a.pr, 1)

        def out_dve(k, b):
            a = at[k]
            for q in range(QT):
                nc.vector.wait_ge(a.pr, b * QT + q + 1)
                old = xtile(b, q)
                new = old if k == 0 else xs[:, q, :]
                nc.vector.tensor_tensor(new, PS[:, 2 + q, 0:D], old, ALU.add).then_inc(a.xa, 1)

        f0 = {n: sem("p0_" + n) for n in ("hi", "f", "r", "mid", "lo", "stored")}

        def proj0_pe(b):
            a = at[0]
            nc.tensor.wait_ge(ln[0].hT, (b + 1) * C)
            for m in range(4):
                for c in range(C):
                    mm = nc.tensor.matmul(PS[:, m, :], wqkv0[:, c, m * P:(m + 1) * P], hT[:, c, :],
                                          start=(c == 0), stop=(c == C - 1))
                mm.then_inc(a.qk, 1)
            for q in range(QT):
                for c in range(C):
                    mm = nc.tensor.matmul(PS[:, 4 + q, 0:D], hT[:, c, q * P:(q + 1) * P],
                                          wqkv0[:, c, 2 * D:3 * D], start=(c == 0), stop=(c == C - 1))
                mm.then_inc(a.v, 1)

        def proj0_act(b):
            a = at[0]
            for m in range(4):
                nc.scalar.wait_ge(f0["f"], b * 4 + m + 1)
                nc.scalar.activation(split0[0][:, m, :], rest0[:, m, :], ACT.Copy).then_inc(f0["hi"], 1)
            for m in range(4):
                nc.scalar.wait_ge(f0["r"], b * 4 + m + 1)
                nc.scalar.activation(split0[1][:, m, :], rest0[:, m, :], ACT.Copy).then_inc(f0["mid"], 1)
            for q in range(QT):
                nc.scalar.wait_ge(a.v, b * QT + q + 1)
                nc.scalar.activation(vals[0][:, q, :], PS[:, 4 + q, 0:D], ACT.Copy).then_inc(a.vs, 1)

        def proj0_dve(b):
            a = at[0]
            for m in range(4):
                nc.vector.wait_ge(a.qk, b * 4 + m + 1)
                nc.vector.tensor_scalar(rest0[:, m, :], PS[:, m, :], (HD0 ** -0.5 if m < 2 else 1.0), None,
                                        ALU.mult).then_inc(f0["f"], 1)
                nc.vector.wait_ge(f0["hi"], b * 4 + m + 1)
                nc.vector.tensor_tensor(rest0[:, m, :], rest0[:, m, :], split0[0][:, m, :],
                                        ALU.subtract).then_inc(f0["r"], 1)

        def proj0_pool(b):
            for m in range(4):
                nc.gpsimd.wait_ge(f0["mid"], b * 4 + m + 1)
                nc.gpsimd.tensor_tensor(split0[2][:, m, :], rest0[:, m, :], split0[1][:, m, :],
                                        ALU.subtract).then_inc(f0["lo"], 1)

        Q_PARTS, K_PARTS = (0, 0, 1, 1, 0, 2), (0, 1, 0, 1, 2, 0)

        def stacks0_sp(b):
            a = at[0]
            for part, s in enumerate(("hi", "mid", "lo")):
                hold(nc.sync, "sp", f0[s], (b + 1) * 4)
                nc.sync.dma_start(qk_parts[part].rearrange("(m p) l -> p m l", p=P), split0[part])\
                    .then_inc(f0["stored"], 16)
            hold(nc.sync, "sp", f0["stored"], (b + 1) * 48)
            for r in range(6):
                for stack, parts, base in ((q_stack, Q_PARTS, 0), (k_stack, K_PARTS, 2 * P)):
                    nc.sync.dma_start(stack[r * HD0:(r + 1) * HD0, :, :],
                                      qk_parts[parts[r], base:base + 2 * P, :].rearrange("(h d) l -> d h l", d=HD0))\
                        .then_inc(a.stack, 16)
            nc.sync.dma_start(k_stack[6 * HD0:6 * HD0 + 1, :, :],
                              pen_rows[:, bass.ds(b * L, L)].unsqueeze(1).broadcast_to([1, H, L])).then_inc(a.stack, 16)

        STACK0 = 13 * 16

        ff = {n: sem("ff_" + n) for n in ("h", "g", "y", "x", "b")}

        def ffn_pe(b):
            nc.tensor.wait_ge(ln[1].hT, (b + 1) * C)
            for f in range(FT):
                if f >= 4:
                    nc.tensor.wait_ge(ff["g"], b * FT + f - 3)
                for c in range(C):
                    mm = nc.tensor.matmul(PS[:, f % 4, :], w1[:, c, f * P:(f + 1) * P], hT[:, c, :],
                                          start=(c == 0), stop=(c == C - 1))
                mm.then_inc(ff["h"], 1)
            nc.tensor.wait_ge(ff["g"], (b + 1) * FT)
            for q in range(QT):
                for f in range(FT):
                    mm = nc.tensor.matmul(PS[:, 4 + q, 0:D], aT[:, f, q * P:(q + 1) * P], w2[:, f, :],
                                          start=(f == 0), stop=(f == FT - 1))
                mm.then_inc(ff["y"], 1)

        def ffn_act(b):
            for f in range(FT):
                nc.scalar.wait_ge(ff["h"], b * FT + f + 1)
                nc.scalar.activation(aT[:, f, :], PS[:, f % 4, :], ACT.Gelu_apprx_tanh,
                                     bias=col["L0_cond_b1"][:, f:f + 1]).then_inc(ff["g"], 1)

        def ffn_dve(b):
            for q in range(QT):
                xq = x[:, bass.ds(b * QT + q, 1), :].rearrange("p a d -> p (a d)")
                nc.vector.wait_ge(ff["y"], b * QT + q + 1)
                nc.vector.tensor_tensor(xq, PS[:, 4 + q, 0:D], xq, ALU.add).then_inc(ff["x"], 1)
                nc.vector.wait_ge(ff["x"], b * QT + q + 1)
                nc.vector.tensor_tensor(xq, xq, b2b[:, :], ALU.add).then_inc(ff["b"], 1)

        p1 = {n: sem("p1_" + n) for n in ("mm", "sq", "sum", "v8", "r8", "qn", "tr", "hi", "f", "lo")}
        NS = 4 * QT

        def where1(n):
            cc, q = n // QT, n % QT
            return cc // 2, (cc % 2) * (G8 // 2), q

        def proj1_pe(b):
            a = at[1]
            nc.tensor.wait_ge(ln[2].hT, (b + 1) * C)
            for n in range(NS + 2):
                if n < NS:
                    q = n % QT
                    if n >= 4:
                        nc.tensor.wait_ge(p1["qn"], b * NS + n - 3)
                    for c in range(C):
                        mm = nc.tensor.matmul(PS[:, n % 4, :], hT[:, c, q * P:(q + 1) * P],
                                              wqkv1[:, c, (n // QT) * CH:(n // QT + 1) * CH],
                                              start=(c == 0), stop=(c == C - 1))
                    mm.then_inc(p1["mm"], 1)
                if n >= 2:
                    m = n - 2
                    nc.tensor.wait_ge(p1["qn"], b * NS + m + 1)
                    if m >= 2:
                        nc.tensor.wait_ge(p1["f"], b * NS + m - 1)
                    for pr in range(G8 // 2):
                        mm = nc.tensor.transpose(PS[:, 4 + m % 2, pr * P:(pr + 1) * P],
                                                 qn1[m % 2][:, pr * P:(pr + 1) * P], ident[:, :])
                    mm.then_inc(p1["tr"], 1)
            for n in range(2 * QT):
                q, half = n // 2, n % 2
                if n >= 2:
                    nc.tensor.wait_ge(a.vs, b * 2 * QT + n - 1)
                for c in range(C):
                    mm = nc.tensor.matmul(PS[:, 6 + half, :], hT[:, c, q * P:(q + 1) * P],
                                          wqkv1[:, c, 2 * W1V + half * CH:2 * W1V + (half + 1) * CH],
                                          start=(c == 0), stop=(c == C - 1))
                mm.then_inc(a.v, 1)

        def proj1_act(b):
            a = at[1]
            for n in range(NS + 3):
                if n < NS:
                    nc.scalar.wait_ge(p1["mm"], b * NS + n + 1)
                    if n >= 2:
                        nc.scalar.wait_ge(p1["sum"], b * NS + n - 1)
                    nc.scalar.activation(sq1[n % 2], PS[:, n % 4, :], ACT.Square).then_inc(p1["sq"], 1)
                if n >= 3:
                    m = n - 3
                    w, pair, q = where1(m)
                    nc.scalar.wait_ge(p1["f"], b * NS + m + 1)
                    nc.scalar.activation(hi1[:, w, pair:pair + G8 // 2, q * P:(q + 1) * P],
                                         f1b[m % 2].rearrange("p (c l) -> p c l", l=P), ACT.Copy)\
                        .then_inc(p1["hi"], 1)
            for n in range(2 * QT):
                q, half = n // 2, n % 2
                nc.scalar.wait_ge(a.v, b * 2 * QT + n + 1)
                nc.scalar.activation(vals[1][:, q, half * CH:(half + 1) * CH], PS[:, 6 + half, :], ACT.Copy)\
                    .then_inc(a.vs, 1)

        def proj1_dve(b):
            for n in range(NS + 3):
                if n < NS:
                    r = n % 2
                    nc.vector.wait_ge(p1["sq"], b * NS + n + 1)
                    nc.vector.tensor_reduce(ssum[:, r, :], sq1[r].rearrange("p (h d) -> p h d", d=HD1),
                                            AX.X, ALU.add).then_inc(p1["sum"], 1)
                    nc.vector.wait_ge(p1["sum"], b * NS + n + 1)
                    if n >= 2:
                        nc.vector.wait_ge(p1["r8"], b * NS + n - 1)
                    nc.vector.tensor_scalar(v8[:, r, :], ssum[:, r, :], 1.0 / HD1, EPS, ALU.mult, ALU.add)\
                        .then_inc(p1["v8"], 1)
                if 1 <= n <= NS:
                    m = n - 1
                    r = m % 2
                    nc.vector.wait_ge(p1["r8"], b * NS + m + 1)
                    if m >= 2:
                        nc.vector.wait_ge(p1["tr"], b * NS + m - 1)
                    nc.vector.tensor_tensor(qn1[r].rearrange("p (h d) -> p h d", d=HD1),
                                            PS[:, m % 4, :].rearrange("p (h d) -> p h d", d=HD1),
                                            r8[:, r, :].unsqueeze(2).broadcast_to([P, G8, HD1]), ALU.mult)\
                        .then_inc(p1["qn"], 1)
                if n >= 3:
                    m = n - 3
                    w = where1(m)[0]
                    nc.vector.wait_ge(p1["tr"], b * NS + m + 1)
                    if m >= 2:
                        nc.vector.wait_ge(p1["lo"], b * NS + m - 1)
                    nc.vector.tensor_scalar(f1b[m % 2], PS[:, 4 + m % 2, :], qkf[:, 2 * w:2 * w + 1],
                                            qkf[:, 2 * w + 1:2 * w + 2], ALU.mult, ALU.add).then_inc(p1["f"], 1)

        def proj1_pool(b):
            for n in range(NS + 3):
                if n < NS:
                    nc.gpsimd.wait_ge(p1["v8"], b * NS + n + 1)
                    if n >= 2:
                        nc.gpsimd.wait_ge(p1["qn"], b * NS + n - 1)
                    nc.gpsimd.tensor_tensor(r8[:, n % 2, :], v8[:, n % 2, :], mhalf[:, 0:G8], ALU.pow)\
                        .then_inc(p1["r8"], 1)
                if n >= 3:
                    m = n - 3
                    w, pair, q = where1(m)
                    nc.gpsimd.wait_ge(p1["hi"], b * NS + m + 1)
                    nc.gpsimd.wait_ge(p1["f"], b * NS + m + 1)
                    nc.gpsimd.tensor_tensor(lo1[:, w, pair:pair + G8 // 2, q * P:(q + 1) * P],
                                            f1b[m % 2].rearrange("p (c l) -> p c l", l=P),
                                            hi1[:, w, pair:pair + G8 // 2, q * P:(q + 1) * P], ALU.subtract)\
                        .then_inc(p1["lo"], 1)

        def stacks1_sp(b):
            a = at[1]

            def place(stack, row, src, w):
                for odd in range(2):
                    nc.sync.dma_start(stack[row:row + HD1, odd:H:2, :],
                                      src[odd * HD1:(odd + 1) * HD1, w, :, :]).then_inc(a.stack, 16)

            hold(nc.sync, "sp", p1["lo"], b * NS + NS // 2)
            place(q16, 0, hi1, 0)
            place(q16, HD1, lo1, 0)
            hold(nc.sync, "sp", p1["lo"], b * NS + NS)
            for row in (0, HD1):
                place(k16, row, hi1, 1)
                place(kl_stack, row, lo1, 1)

        STACK1 = 12 * 16

        g = {n: sem("gate_" + n) for n in ("xT", "xTs", "mm", "max", "sub", "exp", "sum", "inv", "gate", "row",
                                           "stored")}

        def gate_pe(b):
            nc.tensor.wait_ge(at[1].xa, (b + 1) * QT)
            for c in range(C):
                for q in range(QT):
                    mm = nc.tensor.transpose(PS[:, c, q * P:(q + 1) * P], xs[:, q, c * P:(c + 1) * P], ident[:, :])
                mm.then_inc(g["xT"], 1)
            nc.tensor.wait_ge(g["xTs"], (b + 1) * C)
            for q in range(QT):
                for c in range(C):
                    mm = nc.tensor.matmul(PS[:, 6, q * E:(q + 1) * E], hT[:, c, q * P:(q + 1) * P], wgate[:, c, :],
                                          start=(c == 0), stop=(c == C - 1))
            mm.then_inc(g["mm"], 1)

        def gate_act(b):
            for c in range(C):
                nc.scalar.wait_ge(g["xT"], b * C + c + 1)
                nc.scalar.activation(hT[:, c, :], PS[:, c, :], ACT.Copy).then_inc(g["xTs"], 1)
            nc.scalar.wait_ge(g["sub"], b + 1)
            nc.scalar.activation(gexp[:, :, :], gexp[:, :, :], ACT.Exp).then_inc(g["exp"], 1)

        def gate_dve(b):
            logits = PS[:, 6, 0:QT * E].rearrange("p (q e) -> p q e", e=E)
            nc.vector.wait_ge(g["mm"], b + 1)
            nc.vector.tensor_reduce(gmax[:, :], logits, AX.X, ALU.max).then_inc(g["max"], 1)
            nc.vector.wait_ge(g["max"], b + 1)
            nc.vector.tensor_tensor(gexp[:, :, :], logits, gmax[:, :].unsqueeze(2).broadcast_to([P, QT, E]),
                                    ALU.subtract).then_inc(g["sub"], 1)
            nc.vector.wait_ge(g["exp"], b + 1)
            nc.vector.tensor_reduce(gsum[:, :], gexp[:, :, :], AX.X, ALU.add).then_inc(g["sum"], 1)
            nc.vector.wait_ge(g["sum"], b + 1)
            nc.vector.reciprocal(gmax[:, :], gsum[:, :]).then_inc(g["inv"], 1)
            nc.vector.wait_ge(g["inv"], b + 1)
            nc.vector.tensor_tensor(gates[:, bass.ds(b * QT, QT), :], gexp[:, :, :],
                                    gmax[:, :].unsqueeze(2).broadcast_to([P, QT, E]), ALU.mult)\
                .then_inc(g["gate"], 1)
            nc.vector.tensor_tensor(xn[:, :, D:RW], gexp[:, :, :],
                                    gmax[:, :].unsqueeze(2).broadcast_to([P, QT, E]), ALU.mult)\
                .then_inc(g["row"], 1)

        def gate_sp(b):
            tiles = out.rearrange("b (q p) d -> p (b q) d", p=P)
            hold(nc.sync, "sp", at[1].xa, (b + 1) * QT)
            nc.sync.dma_start(tiles[:, bass.ds(b * QT, QT), :], xs[:, :, :]).then_inc(g["stored"], 16)
            hold(nc.sync, "sp", ln[3].xn, (b + 1) * QT)
            hold(nc.sync, "sp", g["row"], b + 1)
            nc.sync.dma_start(rows.rearrange("(n p) w -> p n w", p=P)[:, bass.ds(b * QT, QT), :], xn[:, :, :])\
                .then_inc(g["stored"], 16)
            hold(nc.sync, "sp", g["stored"], (b + 2) * 32)

        def xtile(b, q):
            return x[:, bass.ds(b * QT + q, 1), :].rearrange("p a d -> p (a d)")


        ro = {n: sem("route_" + n) for n in ("b2", "consts", "pick", "spread", "gates", "rep", "cand", "count", "ok", "n", "more",
                                            "prefix", "above", "level", "need", "above_n", "level_n", "taken")}
        R_CONSTS = 5 * 16

        def route_pe():
            nc.tensor.wait_ge(ro["spread"], 1)
            for n in range(NT):
                mm = nc.tensor.matmul(PS[:, n // QT, (n % QT) * P:(n % QT + 1) * P],
                                      above_n[:, n * P:(n + 1) * P], ident[:, :],
                                      start=True, stop=True)
            mm.then_inc(ro["gates"], 1)
            nc.tensor.wait_ge(ro["consts"], R_CONSTS)
            with nc.tensor.Fori(0, ST) as k:
                nc.tensor.wait_ge(ro["ok"], k + 1)
                nc.tensor.matmul(PS[:, 7, 0:1], same[:, :], enough[:, :], start=True, stop=True)\
                    .then_inc(ro["n"], 1)

        def route_act():
            nc.scalar.wait_ge(ro["gates"], 1)
            nc.scalar.activation(gate_rep, PS[:, 0:QT, :].rearrange("p a b -> p (a b)"), ACT.Copy)\
                .then_inc(ro["rep"], 1)

        def route_dve():
            v = nc.vector
            v.wait_ge(g["gate"], B)
            v.tensor_copy(above_n.rearrange("p (n e l) -> p (n e) l", n=NT, e=E),
                          gates[:, :, :].rearrange("p n e -> p (n e)").unsqueeze(2).broadcast_to([P, NT * E, LANES]))\
                .then_inc(ro["spread"], 1)
            v.wait_ge(ro["consts"], R_CONSTS)
            v.tensor_copy(pick, pick_f).then_inc(ro["pick"], 1)
            v.memset(prefix[:, :], 0).then_inc(ro["prefix"], 1)
            v.wait_ge(ro["rep"], 1)
            with v.Fori(0, ST) as k:
                v.wait_ge(ro["prefix"], k + 1)
                v.tensor_tensor(cand[:, :], prefix[:, :], lanes[:, bass.ds(k, 1)], ALU.bitwise_or)\
                    .then_inc(ro["cand"], 1)
                v.wait_ge(ro["cand"], k + 1)
                v.tensor_scalar(level, gate_rep, cand[:, :].bitcast(fp32), None, ALU.is_ge, ALU.add,
                                accum_out=count[:, :]).then_inc(ro["count"], 1)
                v.wait_ge(ro["count"], k + 1)
                v.tensor_scalar(enough[:, :], count[:, :], CAP - 0.5, None, ALU.is_ge).then_inc(ro["ok"], 1)
                v.wait_ge(ro["n"], k + 1)
                v.tensor_scalar(more[:, :], PS[:, 7, 0:1], -1.0, steps[:, bass.ds(k, 1)], ALU.add, ALU.mult)\
                    .then_inc(ro["more"], 1)
                v.wait_ge(ro["more"], k + 1)
                v.tensor_tensor(prefix[:, :], prefix[:, :], more[:, :], ALU.bitwise_or).then_inc(ro["prefix"], 1)
            least = prefix[:, :].bitcast(fp32)
            v.wait_ge(ro["prefix"], ST + 1)
            v.tensor_scalar(above, gate_rep, least, None, ALU.is_gt, ALU.add, accum_out=count[:, :])\
                .then_inc(ro["above"], 1)
            v.tensor_scalar(level, gate_rep, least, None, ALU.is_equal).then_inc(ro["level"], 1)
            v.wait_ge(ro["above"], 1)
            v.tensor_scalar(need[:, :], count[:, :], -1.0, float(CAP), ALU.mult, ALU.add).then_inc(ro["need"], 1)
            v.tensor_tensor_scan(above_n, above, above, 0.0, ALU.add, ALU.max).then_inc(ro["above_n"], 1)
            v.wait_ge(ro["level"], 1)
            v.tensor_tensor_scan(level_n, level, level, 0.0, ALU.add, ALU.max).then_inc(ro["level_n"], 1)
            v.wait_ge(ro["level_n"], 1)
            v.wait_ge(ro["above_n"], 1)
            v.wait_ge(ro["need"], 1)
            v.scalar_tensor_tensor(out=taken_n, in0=level_n, scalar=need[:, 0:1], in1=above_n,
                                   op0=ALU.min, op1=ALU.add).then_inc(ro["taken"], 1)

        mo = {n: sem("moe_" + n) for n in ("w0", "w1", "taken", "idx_f", "idx", "xg0", "xg1", "tr", "gT", "h", "act", "y", "b",
                                          "yw", "add", "added")}
        FE = F1 // P

        def index_pe(e):
            if not (isinstance(e, int) and e == 0):
                hold(nc.tensor, "pe", mo["idx_f"], e * HALVES)
            for n in range(QT):
                mm = nc.tensor.matmul(PS[:, n, :], pick[:, bass.ds(e * P, P)], taken_n[:, n * CH:(n + 1) * CH],
                                      start=True, stop=True)
            mm.then_inc(mo["taken"], 1)

        def index_dve(e, ring_at):
            v = nc.vector
            v.wait_ge(mo["taken"], e + 1)
            if not (isinstance(e, int) and e == 0):
                v.wait_ge(mo["idx"], e)
            for h in range(HALVES):
                v.tensor_scalar((above, level)[h], PS[:, 0:QT, :].rearrange("p a b -> p (a b)"), slot[:, h:h + 1], None,
                                ALU.is_le, ALU.add, accum_out=idx_f[:, ring_at, h:h + 1]).then_inc(mo["idx_f"], 1)

        def index_out_dve(e, ring_at):
            v = nc.vector
            v.wait_ge(mo["idx_f"], (e + 1) * HALVES)
            if not (isinstance(e, int) and e < 2):
                v.wait_ge(mo["added"], e - 1)
            v.tensor_copy(idx[:, ring_at, :], idx_f[:, ring_at, :]).then_inc(mo["idx"], 1)

        def gather_pool(e, ring_at):
            hold(nc.gpsimd, "pool", mo["idx"], e + 1)
            for h in range(HALVES):
                nc.gpsimd.indirect_dma_start(
                    out=xg[:, ring_at, h, :], out_offset=None, in_=rows[:, :],
                    in_offset=bass.IndirectOffsetOnAxis(ap=idx[:, ring_at, h:h + 1], axis=0))\
                    .then_inc(mo[f"xg{ring_at}"], 16)

        def of_ring(e, ring_at):
            return e // 2 if isinstance(e, int) else (e - ring_at) // 2

        def turn_pe(e, ring_at):
            nc.tensor.wait_ge(mo[f"xg{ring_at}"], (of_ring(e, ring_at) + 1) * HALVES * 16)
            if not (isinstance(e, int) and e == 0):
                nc.tensor.wait_ge(mo["gT"], e * C)
            for c in range(C):
                for h in range(HALVES):
                    mm = nc.tensor.transpose(PS[:, 4, c * CAP + h * P:c * CAP + (h + 1) * P],
                                             xg[:, ring_at, h, c * P:(c + 1) * P], ident[:, :])
            mm.then_inc(mo["tr"], 1)

        def turn_act(e, ring_at):
            for c in range(C):
                nc.scalar.wait_ge(mo["tr"], e + 1)
                nc.scalar.activation(gT[:, ring_at, c, :], PS[:, 4, c * CAP:(c + 1) * CAP], ACT.Identity,
                                     bias=col["L1_cond_mlp_b"][:, c:c + 1], scale=col["L1_cond_mlp_g"][:, c:c + 1])\
                    .then_inc(mo["gT"], 1)

        def hidden_pe(e, ring_at):
            nc.tensor.wait_ge(mo["gT"], (e + 1) * C)
            nc.tensor.wait_ge(mo[f"w{ring_at}"], (of_ring(e, ring_at) + 1) * 32)
            for f in range(FE):
                if f % 2 == 0:
                    nc.tensor.wait_ge(mo["act"], e * FE + f - 2 + 4)
                for c in range(C):
                    mm = nc.tensor.matmul(PS[:, 5 + f // 2 % 2, f % 2 * CAP:(f % 2 + 1) * CAP],
                                          fc1[ring_at][:, c, f * P:(f + 1) * P], gT[:, ring_at, c, :],
                                          start=(c == 0), stop=(c == C - 1))
                if f % 2 == 1:
                    mm.then_inc(mo["h"], 1)

        def hidden_act(e, ring_at):
            for f in range(FE):
                hold(nc.scalar, "act", mo["h"], e * (FE // 2) + f // 2 + 1)
                nc.scalar.activation(yT[:, ring_at, f, :], PS[:, 5 + f // 2 % 2, f % 2 * CAP:(f % 2 + 1) * CAP],
                                     ACT.Gelu_apprx_tanh, bias=col["L1_cond_b1s"][:, bass.ds(e * FE + f, 1)])\
                    .then_inc(mo["act"], 1)

        def result_pe(e, ring_at, h):
            if h == 0:
                nc.tensor.wait_ge(mo["act"], (e + 1) * FE + 4)
                nc.tensor.wait_ge(mo["b"], (e + 1) * HALVES)
            for f in range(FE):
                mm = nc.tensor.matmul(PS[:, 7, h * D:(h + 1) * D], yT[:, ring_at, f, h * P:(h + 1) * P],
                                      fc2[ring_at][:, f, :], start=(f == 0), stop=(f == FE - 1))
            if h == HALVES - 1:
                mm.then_inc(mo["y"], 1)

        def result_dve(e, ring_at):
            v = nc.vector
            v.wait_ge(mo["y"], e + 1)
            for h in range(HALVES):
                v.tensor_tensor(yout[:, ring_at, h, :], PS[:, 7, h * D:(h + 1) * D], b2all[:, bass.ds(e * D, D)],
                                ALU.add).then_inc(mo["b"], 1)
            for h in range(HALVES):
                v.wait_ge(mo["b"], e * HALVES + h + 1 + HALVES)
                v.tensor_scalar(yout[:, ring_at, h, :], yout[:, ring_at, h, :],
                                xg[:, ring_at, h, bass.ds(D + e, 1)], None, ALU.mult).then_inc(mo["yw"], 1)

        def scatter_pool(e, ring_at):
            hold(nc.gpsimd, "pool", mo["yw"], (e + 1) * HALVES)
            for h in range(HALVES):
                nc.gpsimd.indirect_dma_start(
                    out=out.rearrange("b l d -> (b l) d"),
                    out_offset=bass.IndirectOffsetOnAxis(ap=idx[:, ring_at, h:h + 1], axis=0),
                    in_=yout[:, ring_at, h, :], in_offset=None, compute_op=ALU.add).then_inc(mo["add"], 16)
            nc.gpsimd.wait_ge(mo["add"], (e + 1) * 32)
            nc.gpsimd.sem_inc(mo["added"], 1)

        def expert_loop(eng, work):
            with eng.Fori(0, E // 2 - 1) as pair:
                work(2 * pair, 0, True, True)
                work(2 * pair + 1, 1, True, True)
            work(E - 2, 0, True, False)
            work(E - 1, 1, False, False)

        def experts_pe():
            index_pe(0)
            index_pe(1)
            turn_pe(0, 0)

            def work(e, r, one, two):
                hidden_pe(e, r)
                if two:
                    index_pe(e + 2)
                result_pe(e, r, 0)
                if one:
                    turn_pe(e + 1, 1 - r)
                result_pe(e, r, 1)

            expert_loop(nc.tensor, work)

        def experts_act():
            turn_act(0, 0)

            def work(e, r, one, two):
                hidden_act(e, r)
                if one:
                    turn_act(e + 1, 1 - r)

            expert_loop(nc.scalar, work)

        def experts_dve():
            for e in range(2):
                index_dve(e, e)
                index_out_dve(e, e)

            def work(e, r, one, two):
                if two:
                    index_dve(e + 2, r)
                result_dve(e, r)
                if two:
                    index_out_dve(e + 2, r)

            expert_loop(nc.vector, work)

        def experts_pool():
            gather_pool(0, 0)
            gather_pool(1, 1)

            def work(e, r, one, two):
                scatter_pool(e, r)
                if two:
                    gather_pool(e + 2, r)

            expert_loop(nc.gpsimd, work)

        def weights_sp(e, ring_at):
            nc.sync.dma_start(fc1[ring_at], t["L1_cond_fc1s"][bass.ds(e, 1)].rearrange("a (c p) f -> p (a c) f", p=P))\
                .then_inc(mo[f"w{ring_at}"], 16)
            nc.sync.dma_start(fc2[ring_at], t["L1_cond_fc2s"][bass.ds(e, 1)].rearrange("a (f p) d -> p (a f) d", p=P))\
                .then_inc(mo[f"w{ring_at}"], 16)

        def experts_sp():
            hold(nc.sync, "sp", at[1].s, B * H * QT)
            for e in range(2):
                weights_sp(e, e)
            with nc.sync.Fori(0, E // 2 - 1) as pair:
                for ring_at in range(2):
                    hold(nc.sync, "sp", mo["y"], 2 * pair + ring_at + 1)
                    weights_sp(2 * pair + ring_at + 2, ring_at)

        def centre_dve():
            nc.vector.wait_ge(s_wq1, 16)
            nc.vector.tensor_scalar(qkf[:, 0:2], qkg[:, 0:2], 0.5, None, ALU.mult).then_inc(w_centred, 1)
            nc.vector.tensor_scalar(qkf[:, 2:4], qkg[:, 2:4], 2.0 * HD1 ** -0.5, None, ALU.mult).then_inc(w_centred, 1)
            for c in range(C):
                wc = wqkv1[:, c, 0:2 * W1V].rearrange("p (h d) -> p h d", d=HD1)
                nc.vector.tensor_reduce(wmean[:, c, :], wc, AX.X, ALU.add).then_inc(s_mean, 1)
                nc.vector.wait_ge(s_mean, 2 * c + 1)
                nc.vector.tensor_scalar(wmean[:, c, :], wmean[:, c, :], 1.0 / HD1, None, ALU.mult).then_inc(s_mean, 1)
                nc.vector.wait_ge(s_mean, 2 * c + 2)
                nc.vector.tensor_tensor(wc, wc, wmean[:, c, :].unsqueeze(2).broadcast_to([P, 2 * H, HD1]),
                                  ALU.subtract).then_inc(w_centred, 2)

        def over_sequences(eng, work):
            with eng.Fori(0, B - 1) as b:
                work(b, True)
            work(B - 1, False)

        N_VEC = 7
        block = ctx.enter_context(nc.Block())

        @block.sync
        def _(sp):
            sp.sem_inc(g["stored"], 32)
            sp.dma_start(x[:, :, :], t["x"].rearrange("b (q p) d -> p (b q) d", p=P)).then_inc(s_x, 16)
            sp.dma_start(condT[:, :, :], t["condT"].rearrange("(c p) b -> p c b", p=P)).then_inc(s_vec, 16)
            sp.dma_start(wt, t["L0_cond_Wt"].rearrange("(c p) n -> p c n", p=P)).then_inc(s_vec, 16)
            sp.dma_start(wada, t["L1_cond_W_ada"].rearrange("(c p) n -> p c n", p=P)).then_inc(s_vec, 16)
            sp.dma_start(cols[:, :], t["cols"]).then_inc(s_vec, 16)
            sp.dma_start(b2b[:, :], t["L0_cond_b2"].partition_broadcast(P)).then_inc(s_vec, 16)
            sp.dma_start(tscale[:, :], t["L0_cond_torus_scale"].partition_broadcast(P)).then_inc(s_vec, 16)
            sp.dma_start(mask_u8[:, :], t["mask_BxS_bf1"].rearrange("(a b) l -> a (b l)", a=1)).then_inc(s_vec, 16)
            sp.dma_start(wqkv0, t["L0_cond_Wqkv"].rearrange("(c p) n -> p c n", p=P)).then_inc(s_w0, 16)
            sp.dma_start(dist[:, :].rearrange("p (q l) -> p q l", q=QT),
                         t["L0_cond_torus_dist"].rearrange("a (q p) l -> p (a q) l", p=P)).then_inc(s_w0, 16)
            sp.wait_ge(s_const, 4)
            for h in range(4):
                sp.dma_start(wout0[h * OW[0]:h * OW[0] + HD0, :, :],
                             t["L0_cond_Wout"].rearrange("(j h d) n -> h d j n", h=4, d=HD0)[h]).then_inc(s_w0, 16)
            sp.dma_start(w1, t["L0_cond_W1"].rearrange("(c p) n -> p c n", p=P)).then_inc(s_w0, 16)
            sp.dma_start(w2, t["L0_cond_W2"].rearrange("(c p) n -> p c n", p=P)).then_inc(s_w0, 16)
            sp.wait_ge(s_pen, 1)
            sp.dma_start(pen_rows, pen).then_inc(s_pen_row, 16)
            sp.wait_ge(s_pen_row, 16)
            with sp.Fori(0, B) as b:
                stacks0_sp(b)
            sp.wait_ge(at[0].o, B * JT0 + C1)
            sp.dma_start(wqkv1, t["L1_cond_Wqkv"].rearrange("(c p) n -> p c n", p=P)).then_inc(s_wq1, 16)
            for dst, name in ((lanes, "lanes"), (steps, "steps"), (same, "same"), (slot, "slot")):
                sp.dma_start(dst[:, :], t[name]).then_inc(ro["consts"], 16)
            stacks1_sp(0)

            def layer1(b, ahead):
                if ahead:
                    stacks1_sp(b + 1)
                gate_sp(b)

            over_sequences(sp, layer1)
            sp.dma_start(pick_f, t["pick"]).then_inc(ro["consts"], 16)
            experts_sp()

        @block.gpsimd
        def _(pool):
            pool.memset(ident[:, :], 0.0).then_inc(s_ident, 1)
            pool.memset(mhalf[:, :], -0.5).then_inc(s_const, 1)
            pool.memset(v_now[:, :], 0.0).then_inc(s_const, 1)
            credits(pool, "pool")
            pool.wait_ge(s_ident, 1)
            pool.affine_select(out=ident[:, :], in_=ident[:, :], compare_op=ALU.not_equal, fill=1.0,
                               base=0, pattern=[[-1, P]], channel_multiplier=1).then_inc(s_ident, 1)
            pool.dma_start(wgate[:, :, :], t["L1_cond_Wgate"].rearrange("(c p) n -> p c n", p=P)).then_inc(s_w1, 16)
            pool.dma_start(wout1[:, :, :], t["L1_cond_Wout"].rearrange("(c p) n -> p c n", p=P)).then_inc(s_w1, 16)
            pool.wait_ge(s_w0, 8 * 16)
            pool.wait_ge(s_const, 4)
            norm_pool(0, 0)
            proj0_pool(0)

            def layer0(b, ahead):
                attn_pool(0, b)
                if ahead:
                    norm_pool(0, b + 1)
                    proj0_pool(b + 1)
                norm_pool(1, b)

            over_sequences(pool, layer0)
            norm_pool(2, 0)
            proj1_pool(0)

            def layer1(b, ahead):
                attn_pool(1, b)
                if ahead:
                    norm_pool(2, b + 1)
                    proj1_pool(b + 1)
                norm_pool(3, b)

            over_sequences(pool, layer1)
            pool.wait_ge(at[1].pv, B * PAIRS + C2)
            pool.dma_start(b2all, t["L1_cond_b2s"].rearrange("e d -> (e d)").partition_broadcast(P))\
                .then_inc(ro["b2"], 16)
            pool.wait_ge(g["stored"], (B + 1) * 32)
            experts_pool()
            pool.wait_ge(mo["add"], E * 32)

        @block.scalar
        def _(act):
            credits(act, "act")
            act.wait_ge(s_vec, N_VEC * 16)
            act.activation(gelT[:, :, :], condT[:, :, :], ACT.Gelu_apprx_tanh).then_inc(cond_act, 1)
            act.activation(silT[:, :, :], condT[:, :, :], ACT.Silu).then_inc(cond_act, 1)
            act.wait_ge(cond_vec, 12)
            norm_act(0, 0)
            proj0_act(0)

            def layer0(b, ahead):
                attn_act(0, b)
                if ahead:
                    norm_act(0, b + 1)
                    proj0_act(b + 1)
                norm_act(1, b)
                ffn_act(b)

            over_sequences(act, layer0)
            norm_act(2, 0)
            proj1_act(0)

            def layer1(b, ahead):
                attn_act(1, b)
                if ahead:
                    norm_act(2, b + 1)
                    proj1_act(b + 1)
                gate_act(b)

            over_sequences(act, layer1)
            route_act()
            act.sem_inc(mo["act"], 4)
            experts_act()

        @block.tensor
        def _(pe):
            credits(pe, "pe")
            pe.wait_ge(s_ident, 2)
            pe.wait_ge(s_vec, N_VEC * 16)
            pe.wait_ge(cond_act, 2)
            for m in range(3 * C):
                w, act_in, off = (wt, gelT, m * P) if m < 2 * C else (wada, silT, (m - 2 * C) * P)
                for c in range(C):
                    mm = pe.matmul(PS[:, 7, m * B:(m + 1) * B], w[:, c, off:off + P], act_in[:, c, :],
                                   start=(c == 0), stop=(c == C - 1))
            mm.then_inc(cond_mm, 1)
            pe.wait_ge(s_w0, 8 * 16)
            pe.wait_ge(cond_vec, 12)
            norm_pe(0, 0)
            proj0_pe(0)

            def layer0(b, ahead):
                pe.wait_ge(at[0].stack, (b + 1) * STACK0)
                pe.wait_ge(at[0].vs, (b + 1) * QT)
                attn_pe(0, b)
                if ahead:
                    norm_pe(0, b + 1)
                out_pe(0, b)
                if ahead:
                    pe.wait_ge(at[0].xa, (b + 1) * QT)
                    proj0_pe(b + 1)
                norm_pe(1, b)
                ffn_pe(b)
                pe.wait_ge(ff["x"], (b + 1) * QT)

            over_sequences(pe, layer0)
            pe.wait_ge(s_w1, 2 * 16)
            pe.wait_ge(w_centred, 2 + 2 * C)
            norm_pe(2, 0)
            proj1_pe(0)
            pe.wait_ge(at[1].vs, 2 * QT)

            def layer1(b, ahead):
                pe.wait_ge(at[1].stack, (b + 1) * STACK1)
                attn_pe(1, b)
                if ahead:
                    norm_pe(2, b + 1)
                out_pe(1, b)
                if ahead:
                    pe.wait_ge(at[1].xa, (b + 1) * QT)
                    proj1_pe(b + 1)
                    pe.wait_ge(at[1].vs, (b + 2) * 2 * QT)
                gate_pe(b)

            over_sequences(pe, layer1)
            route_pe()
            pe.wait_ge(ro["taken"], 1)
            pe.wait_ge(ro["pick"], 1)
            pe.wait_ge(ro["rep"], 1)
            experts_pe()

        @block.vector
        def _(dve):
            credits(dve, "dve")
            dve.memset(q_stack[6 * HD0:6 * HD0 + 1, :, :], 1.0).then_inc(s_const, 1)
            dve.memset(wout0, 0.0).then_inc(s_const, 1)
            dve.wait_ge(s_vec, N_VEC * 16)
            dve.tensor_scalar(pen[:, :], mask_u8[:, :], 1.0, -NEG, ALU.subtract, ALU.mult).then_inc(s_pen, 1)
            dve.wait_ge(cond_mm, 1)
            modes = [(col["L0_cond_bt"][:, m:m + 1]) for m in range(2 * C)] + [col["L1_cond_b_ada"][:, c:c + 1] for c in range(C)]
            for m in range(3 * C):
                dve.tensor_scalar(tp[:, m, :], PS[:, 7, m * B:(m + 1) * B], modes[m],
                                  1.0 if m < C else 0.0, ALU.add, ALU.add).then_inc(cond_vec, 1)
            dve.wait_ge(cond_vec, 3 * C)
            for c in range(C):
                gc, bc = col["L0_cond_ln1_g"][:, c:c + 1], col["L0_cond_ln1_b"][:, c:c + 1]
                dve.tensor_scalar(gain[0][:, c, :], tp[:, c, :], gc, None, ALU.mult).then_inc(cond_vec, 1)
                dve.scalar_tensor_tensor(out=shift[0][:, c, :], in0=tp[:, c, :], scalar=bc, in1=tp[:, C + c, :],
                                         op0=ALU.mult, op1=ALU.add).then_inc(cond_vec, 1)
                dve.tensor_scalar(shift[2][:, c, :], tp[:, 2 * C + c, :], col["L1_cond_ln1_b"][:, c:c + 1], None,
                                  ALU.add).then_inc(cond_vec, 1)
            for c in range(C):
                for n, name in ((1, "L0_cond_ln2"), (2, "L1_cond_ln1")):
                    dve.tensor_scalar(gain[n][:, c, :], tp[:, c, :], 0.0, col[name + "_g"][:, c:c + 1],
                                      ALU.mult, ALU.add).then_inc(cond_vec, 1)
                dve.tensor_scalar(shift[1][:, c, :], tp[:, c, :], 0.0, col["L0_cond_ln2_b"][:, c:c + 1],
                                  ALU.mult, ALU.add).then_inc(cond_vec, 1)
            dve.wait_ge(s_x, 16)
            norm_dve(0, 0, xtile)
            proj0_dve(0)

            def layer0(b, ahead):
                attn_dve(0, b)
                if ahead:
                    norm_dve(0, b + 1, xtile)
                out_dve(0, b)
                if ahead:
                    proj0_dve(b + 1)
                hold(dve, "dve", at[0].xa, (b + 1) * QT)
                norm_dve(1, b, xtile)
                if not ahead:
                    centre_dve()
                ffn_dve(b)

            over_sequences(dve, layer0)
            dve.wait_ge(ff["b"], B * QT)
            norm_dve(2, 0, xtile)
            proj1_dve(0)

            def layer1(b, ahead):
                attn_dve(1, b)
                hold(dve, "dve", g["stored"], (b + 1) * 32)
                if ahead:
                    norm_dve(2, b + 1, xtile)
                out_dve(1, b)
                if ahead:
                    proj1_dve(b + 1)
                hold(dve, "dve", at[1].xa, (b + 1) * QT)
                norm_dve(3, b, lambda b, q: xs[:, q, :])
                gate_dve(b)

            over_sequences(dve, layer1)
            route_dve()
            dve.sem_inc(mo["b"], HALVES)
            dve.wait_ge(ro["b2"], 16)
            experts_dve()


FEATURE_COLS = [("L0_cond_ln1_g", 2), ("L0_cond_ln1_b", 2), ("L0_cond_ln2_g", 2), ("L0_cond_ln2_b", 2),
                ("L1_cond_ln1_g", 2), ("L1_cond_ln1_b", 2), ("L1_cond_mlp_g", 2), ("L1_cond_mlp_b", 2),
                ("L1_cond_b_ada", 2), ("L0_cond_bt", 4), ("L0_cond_b1", 8), ("L1_cond_b1s", 64)]
_PAIR_COLS = ["L1_cond_qn_g", "L1_cond_qn_b", "L1_cond_kn_g", "L1_cond_kn_b"]
_PLAIN = ["x", "mask_BxS_bf1", "L0_cond_torus_dist", "L0_cond_Wqkv", "L0_cond_Wout", "L0_cond_torus_scale",
          "L0_cond_W1", "L0_cond_W2", "L0_cond_b2", "L0_cond_Wt", "L1_cond_b2s"]
_TURNED = {"condT": "cond_1024", "L1_cond_W_ada": "L1_cond_W_ada", "L1_cond_Wqkv": "L1_cond_Wqkv",
           "L1_cond_Wout": "L1_cond_Wout", "L1_cond_Wgate": "L1_cond_Wgate", "L1_cond_fc1s": "L1_cond_fc1s",
           "L1_cond_fc2s": "L1_cond_fc2s"}


def kernel(**inputs):
    import numpy as _np
    import concourse.bacc as _bacc
    from concourse import mybir as _mybir
    from concourse.bass_utils import run_bass_kernel_spmd as _run

    nc = _bacc.Bacc("TRN2", target_bir_lowering=False, num_devices=1)
    laid = {n: _np.asarray(inputs[n]) for n in _PLAIN}
    laid.update({n: _np.swapaxes(_np.asarray(inputs[src]), -1, -2) for n, src in _TURNED.items()})
    laid["cols"] = _np.concatenate(
        [_np.asarray(inputs[n]).reshape(-1, 128).T for n, _ in FEATURE_COLS]
        + [_np.tile(_np.asarray(inputs[n]), 2)[:, None] for n in _PAIR_COLS], axis=1)
    part, ex = _np.arange(128), laid["L1_cond_b2s"].shape[0]
    lane, shifts = part % (128 // ex), 28 - 4 * _np.arange(8)
    laid["lanes"] = (_np.minimum(lane[:, None], _np.where(shifts == 28, 7, 15)) << shifts).astype(_np.int32)
    laid["steps"] = _np.broadcast_to((2.0 ** shifts).astype(_np.float32), (128, 8))
    laid["same"] = (part[:, None] // (128 // ex) == part // (128 // ex)).astype(_np.float32)
    laid["slot"] = (part[:, None] + 128 * _np.arange(2)).astype(_np.float32)
    laid["pick"] = _np.repeat((part[:, None] == (128 // ex) * _np.arange(ex)).astype(_np.float32), 128, axis=1)
    arrays, aps = {}, {}
    for name, a in laid.items():
        a = _np.ascontiguousarray(a)
        arrays[f"in_{name}"] = a
        aps[name] = nc.dram_tensor(f"in_{name}", a.shape, _mybir.dt.from_np(a.dtype), kind="ExternalInput").ap()
    out = nc.dram_tensor("out_0", laid["x"].shape, _mybir.dt.float32, kind="ExternalOutput").ap()
    cond_seq_kernel(nc, aps, out)
    r = _run(nc, [arrays], core_ids=[0])
    return r.results[0]["out_0"]
```

```python
import concourse.bass as bass
from concourse import mybir
from contextlib import ExitStack


def cond_seq_kernel(nc, t, out):
    fp32 = mybir.dt.float32
    fp16 = mybir.dt.float16
    bf16 = mybir.dt.bfloat16
    i32 = mybir.dt.int32
    u32 = mybir.dt.uint32
    u8 = mybir.dt.uint8
    ALU = mybir.AluOpType
    ACT = mybir.ActivationFunctionType
    AX = mybir.AxisListType

    B, L, D = t["x"].shape
    P = 128
    H = t["L0_cond_torus_scale"].shape[0]
    HD0 = D // H
    HD1 = 64
    C = D // P
    QT = L // P
    NT = B * QT
    F0 = t["L0_cond_W1"].shape[1]
    FT = F0 // P
    E, _, F1 = t["L1_cond_fc1s"].shape
    W1V = H * HD1
    JT = W1V // P
    EPS = 1e-5
    CAP = B * L // E
    HALVES = CAP // P
    PAIRS = H // 2
    CH = 512
    G8 = CH // HD1
    RW = D + E
    NEG = -1e30
    LANES = P // E

    ctx = ExitStack()
    with ctx:
        def sb(name, shape, dt=fp32):
            return ctx.enter_context(nc.sbuf_tensor(name, shape, dt))

        def sem(name):
            return ctx.enter_context(nc.semaphore(name))

        qk_parts = nc.dram_tensor("qk_parts", (3, 4 * P, L), bf16, kind="Internal").ap()
        pen_rows = nc.dram_tensor("pen_rows", (1, B * L), bf16, kind="Internal").ap()
        rows = nc.dram_tensor("routed_rows", (B * L, RW), fp32, kind="Internal").ap()

        x = sb("x", [P, NT, D])
        ident = sb("ident", [P, P])
        JT0 = H // 4
        w_sizes = [C * 3 * D, JT0 * D, C * F0, FT * D]
        w0buf = sb("w0buf", [P, sum(w_sizes)])
        w_at = [sum(w_sizes[:k]) for k in range(5)]
        wqkv0, wout0, w1, w2 = [w0buf[:, w_at[k]:w_at[k + 1]].rearrange("p (c n) -> p c n", c=c)
                                for k, c in enumerate((C, JT0, C, FT))]
        wq1buf = sb("wq1buf", [P, C * 3 * W1V])
        wqkv1 = wq1buf[:, :].rearrange("p (c n) -> p c n", c=C)
        wout1 = sb("wout1", [P, JT, D])
        wgate = sb("wgate", [P, C, E])
        hT = sb("hT", [P, C, L])
        xn = sb("xn", [P, QT, RW])
        q_stack = sb("q_stack", [P, H, L], bf16)
        k_stack = sb("k_stack", [P, H, L], bf16)
        kl_stack = sb("kl_stack", [P, H, L], fp16)
        vals_flat = sb("vals", [P, QT * W1V])
        obuf = sb("obuf", [P, QT * W1V])
        RB = QT * L
        ring = sb("ring", [P, 4 * RB])
        v_now = sb("v_now", [P, 4 * QT * HD1])

        q16 = q_stack[:, :, :].bitcast(fp16)
        k16 = k_stack[:, :, :].bitcast(fp16)
        vals = [vals_flat[:, 0:QT * w].rearrange("p (q w) -> p q w", q=QT) for w in (D, W1V)]
        dist = vals_flat[:, QT * W1V - QT * L:QT * W1V]
        xs = w0buf[:, 2 * RB:2 * RB + QT * D].rearrange("p (q d) -> p q d", q=QT)
        mask_u8 = obuf[0:1, 0:B * L // 4].bitcast(u8)
        pen = obuf[0:1, B * L // 4:B * L // 4 + B * L // 2].bitcast(bf16)
        bias_ring = kl_stack[:, :, :].rearrange("p h l -> p (h l)").bitcast(fp32)
        probs = [ring[:, r * RB:(r + 1) * RB] for r in (0, 1)]
        probsT = [[ring[:, 2 * RB:3 * RB], ring[:, 3 * RB:4 * RB], far[:, 0:RB], far[:, RB:2 * RB]]
                  for far in (wq1buf, w0buf)]
        sum_rep, sum_T = [[far[:, at_:at_ + CH] for far, at_ in ((wq1buf, 2 * RB + d), (w0buf, 2 * RB + QT * D + d))]
                          for d in (0, CH)]
        OW = (2 * HD0, HD1)
        v_heads = [v_now[:, 0:4 * QT * w].rearrange("p (h q w) -> p h q w", h=4, q=QT) for w in OW]
        split0 = [ring[:, r * RB // 2:(r + 1) * RB // 2].bitcast(bf16)
                  .rearrange("p (m l) -> p m l", m=4) for r in range(3)]
        rest0 = ring[:, 2 * RB:3 * RB].rearrange("p (m l) -> p m l", m=4)
        hi1 = ring[:, 0:2 * RB].bitcast(fp16).rearrange("p (w c l) -> p w c l", w=2, c=PAIRS)
        lo1 = ring[:, 2 * RB:4 * RB].bitcast(fp16).rearrange("p (w c l) -> p w c l", w=2, c=PAIRS)
        sq1 = [obuf[:, r * CH:(r + 1) * CH] for r in (0, 1)]
        qn1 = [obuf[:, r * CH:(r + 1) * CH] for r in (2, 3)]
        xT = obuf[:, 6 * CH:(6 + C) * CH].rearrange("p (c l) -> p c l", c=C)
        f1b = [obuf[:, r * CH:(r + 1) * CH] for r in (4, 5)]
        oT = obuf[:, 0:JT * L].rearrange("p (j l) -> p j l", j=JT)
        aT = obuf[:, 0:FT * L].rearrange("p (f l) -> p f l", f=FT)
        wt = ring[:, 0:C * 2 * D].rearrange("p (c n) -> p c n", c=C)
        wada = ring[:, C * 2 * D:C * 3 * D].rearrange("p (c n) -> p c n", c=C)

        negmax = sb("negmax", [P, 2, QT])
        rsum = sb("rsum", [P, 4, QT])
        rinv = sb("rinv", [P, 4, QT])
        scale_now = sb("scale_now", [P, 2])
        tscale = sb("tscale", [P, H])
        stats = sb("stats", [P, QT, 6])
        mv = sb("mv", [P, QT, 2])
        veps = sb("veps", [P, QT])
        rstd = sb("rstd", [P, QT])
        mhalf = sb("mhalf", [P, QT])
        eps = sb("eps", [P, 1])
        ssum = sb("ssum", [P, 2, G8])
        std8 = sb("std8", [P, 2, G8])
        rstd8 = sb("rstd8", [P, 2, G8])
        condT = sb("condT", [P, C, B])
        gelT = sb("gelT", [P, C, B])
        silT = sb("silT", [P, C, B])
        cols = sb("cols", [P, t["cols"].shape[1]])
        col, at_col = {}, 0
        for n, k in FEATURE_COLS:
            col[n] = cols[:, at_col:at_col + k]
            at_col += k
        qkg = cols[:, at_col:at_col + 4]
        qkf = sb("qkf", [P, 4])
        b2b = sb("b2b", [P, D])
        gain = {0: sb("gain0", [P, C, B]), 1: sb("gain1", [P, C, B]), 2: sb("gain2", [P, C, B])}
        shift = {0: sb("shift0", [P, C, B]), 1: sb("shift1", [P, C, B]), 2: sb("shift2", [P, C, B])}
        tp = sb("tp", [P, 3 * C, B])
        wmean = sb("wmean", [P, C, 2 * H])
        gates = sb("gates", [P, NT, E])
        gmax = sb("gmax", [P, QT])
        gsum = sb("gsum", [P, QT])
        gexp = sb("gexp", [P, QT, E])
        logits = sb("logits", [P, QT, E])

        ST = 32 // 4
        gate_rep = ring[:, 0:B * L]
        above = ring[:, B * L:3 * B * L // 2].bitcast(bf16)
        level = ring[:, 3 * B * L // 2:2 * B * L].bitcast(bf16)
        above_n = ring[:, 2 * B * L:3 * B * L]
        level_n = ring[:, 3 * B * L:4 * B * L]
        taken_n = obuf[:, 0:B * L // 2].bitcast(bf16)
        xg = obuf[:, B * L // 2:B * L // 2 + 2 * HALVES * RW].rearrange("p (r h w) -> p r h w", r=2, h=HALVES)
        b2all = vals_flat[:, 0:E * D]
        yout = vals_flat[:, E * D:E * D + 2 * HALVES * D].rearrange("p (r h d) -> p r h d", r=2, h=HALVES)
        gT = vals_flat[:, E * D + 2 * HALVES * D:E * D + 2 * HALVES * D + 2 * C * CAP]\
            .rearrange("p (r c s) -> p r c s", r=2, c=C)
        yT = kl_stack[:, :, :].rearrange("p h l -> p (h l)").bitcast(fp32)\
            .rearrange("p (r f s) -> p r f s", r=2, f=F1 // P)
        fc1, fc2 = [], []
        for buf in (q_stack, k_stack):
            flat = buf[:, :, :].rearrange("p h l -> p (h l)").bitcast(fp32)
            fc1.append(flat[:, 0:C * F1].rearrange("p (c f) -> p c f", c=C))
            fc2.append(flat[:, C * F1:2 * C * F1].rearrange("p (f d) -> p f d", d=D))
        pick_f = w0buf[:, 0:E * P]
        pick = w0buf[:, E * P:E * P + E * P // 2].bitcast(bf16)
        lanes = sb("lanes", [P, ST], i32)
        steps = sb("steps", [P, ST])
        same = sb("same", [P, P])
        slot = sb("slot", [P, HALVES])
        prefix = sb("prefix", [P, 1], i32)
        cand = sb("cand", [P, 1], i32)
        more = sb("more", [P, 1], i32)
        count = sb("count", [P, 1])
        enough = sb("enough", [P, 1])
        need = sb("need", [P, 1])
        idx_f = sb("idx_f", [P, 2, HALVES])
        idx = sb("idx", [P, 2, HALVES], u32)
        idx_out = sb("idx_out", [P, 2, HALVES], u32)

        PS = ctx.enter_context(nc.psum_tensor("PS", [P, 8, CH], fp32))

        s_wq0 = sem("s_wq0")
        s_mask = sem("s_mask")
        s_vec = sem("s_vec")
        s_w0 = sem("s_w0")
        s_w1 = sem("s_w1")
        s_ident = sem("s_ident")
        s_const = sem("s_const")
        s_pen = sem("s_pen")
        s_wq1 = sem("s_wq1")
        turn = {e: sem(f"turn_{e}") for e in ("pe", "act", "dve", "pool", "sp")}
        cond_act = sem("cond_act")
        cond_mm = sem("cond_mm")
        cond_vec = sem("cond_vec")
        w_centred = sem("w_centred")

        def hold(eng, key, s, val):
            eng.wait_ge(s, val)
            eng.sem_inc(turn[key], 1)

        class Norm:
            def __init__(self, name):
                self.stats = sem(name + "_stats")
                self.aggr = sem(name + "_aggr")
                self.veps = sem(name + "_veps")
                self.rstd = sem(name + "_rstd")
                self.xn = sem(name + "_xn")
                self.tr = sem(name + "_tr")
                self.hT = sem(name + "_hT")

        ln = [Norm("ln_a"), Norm("ln_b"), Norm("ln_c"), Norm("ln_d")]

        def norm_dve(n, b, src, width_off=0):
            s = ln[n]
            for q in range(QT):
                nc.vector.bn_stats(stats[:, q, :], src(b, q)).then_inc(s.stats, 1)
            for q in range(QT):
                hold(nc.vector, "dve", s.stats, b * QT + q + 1)
                nc.vector.bn_aggr(mv[:, q, :], stats[:, q, :]).then_inc(s.aggr, 1)
            nc.vector.wait_ge(s.aggr, b * QT + QT)
            nc.vector.tensor_scalar(veps[:, :], mv[:, :, 1], EPS, None, ALU.add).then_inc(s.veps, 1)
            nc.vector.wait_ge(s.rstd, b + 1)
            for q in range(QT):
                nc.vector.tensor_scalar(xn[:, q, 0:D], src(b, q), mv[:, q, 0:1], rstd[:, q:q + 1],
                                        ALU.subtract, ALU.mult).then_inc(s.xn, 1)

        def norm_pool(n, b):
            s = ln[n]
            nc.gpsimd.wait_ge(s.veps, b + 1)
            nc.gpsimd.tensor_tensor(rstd[:, :], veps[:, :], mhalf[:, 0:QT], ALU.pow).then_inc(s.rstd, 1)

        def norm_pe(n, b):
            s = ln[n]
            for c in range(C):
                for q in range(QT):
                    if c == 0:
                        nc.tensor.wait_ge(s.xn, b * QT + q + 1)
                    mm = nc.tensor.transpose(PS[:, c, q * P:(q + 1) * P], xn[:, q, c * P:(c + 1) * P], ident[:, :])
                mm.then_inc(s.tr, 1)

        def norm_act(n, b):
            s = ln[n]
            for c in range(C):
                hold(nc.scalar, "act", s.tr, b * C + c + 1)
                nc.scalar.activation(hT[:, c, :], PS[:, c, :], ACT.Identity, bias=shift[n][:, c, bass.ds(b, 1)],
                                     scale=gain[n][:, c, bass.ds(b, 1)]).then_inc(s.hT, 1)

        class Attn:
            def __init__(self, name):
                self.s = sem(name + "_scores")
                self.mx = sem(name + "_max")
                self.ex = sem(name + "_exp")
                self.t = sem(name + "_probsT")
                self.ea = sem(name + "_evac_act")
                self.ed = sem(name + "_evac_dve")
                self.pv = sem(name + "_pv")
                self.ri = sem(name + "_rinv")
                self.rep = sem(name + "_rep")
                self.reph = sem(name + "_rep_head")
                self.rt = sem(name + "_repT")
                self.re = sem(name + "_repT_sbuf")
                self.o = sem(name + "_out")
                self.vst = sem(name + "_v_head")
                if name == "at0":
                    self.bias = sem(name + "_bias")
                    self.scl = sem(name + "_scale")
                else:
                    self.stack_rest = sem(name + "_stack_rest")
                self.stack = sem(name + "_stack")
                self.qk = sem(name + "_qk")
                self.v = sem(name + "_v")
                self.vs = sem(name + "_v_sbuf")
                self.pr = sem(name + "_proj")
                self.xa = sem(name + "_x_added")

        at = [Attn("at0"), Attn("at1")]
        CS = 2 * QT
        CE = 1
        C2 = 2
        C1 = 1

        def credits(eng, which):
            for a in at:
                if which == "pe":
                    eng.sem_inc(a.t, CS)
                    eng.sem_inc(a.pv, C2)
                    eng.sem_inc(a.rt, C1)
                if which == "act":
                    eng.sem_inc(a.ex, CS)
                    eng.sem_inc(a.ea, CE)
                    eng.sem_inc(a.re, C1)
                if which == "dve":
                    eng.sem_inc(a.mx, CS)
                    eng.sem_inc(a.ed, CE)
                    eng.sem_inc(a.o, C1)
                    eng.sem_inc(a.ri, C2)
                if which == "pool":
                    eng.sem_inc(a.rep, C2)

        class Step:
            def __init__(self, k, b, g, j):
                t_ = 4 * g + j
                self.j, self.t = j, t_
                self.peeled = peeled = isinstance(g, int)
                self.scores = not peeled or t_ < H
                self.turned = not peeled or 1 <= t_ <= H
                self.n = b * H + t_
                self.slot = j
                self.last_slot = (j - 1) % 4
                half = lambda back: 2 * g + (j - back) // 2
                self.pair = b * PAIRS + half(0)
                self.last_pair = b * PAIRS + half(1)
                self.pv = (not peeled or 0 <= half(3 + (j % 2 == 0)) < PAIRS)
                self.pv_local = half(3 if j % 2 else 4)
                if peeled:
                    self.pv = 0 <= self.pv_local < PAIRS
                self.pv_pair = b * PAIRS + self.pv_local
                self.pv_kts = (0, 1) if j % 2 else (2, 3)
                self.pv_odd = ((j - (3 if j % 2 else 4)) // 2) % 2
                self.inv = j % 2 == 0 and (not peeled or 0 <= half(2) < PAIRS)
                self.inv_pair = b * PAIRS + half(2)
                self.inv_slot = (j - 2) % 4
                per = (H // 4, PAIRS)[k]
                if k == 0:
                    rt_local, nm_local = g - 1, g - 1
                    rt_here, nm_here = j == 2, j == 3
                else:
                    rt_local, nm_local = half(4), half(5)
                    rt_here, nm_here = j % 2 == 0, j % 2 == 1
                self.rt = rt_here and (not peeled or 0 <= rt_local < per)
                self.norm = nm_here and (not peeled or 0 <= nm_local < per)
                self.inv_tile = b * (H // 4) + g + (j - 2) // 4
                self.rt_tile, self.norm_tile, self.norm_local = b * per + rt_local, b * per + nm_local, nm_local
                self.rt_pairs = b * PAIRS + ((g - 1) * 2 + 2 if k == 0 else half(4) + 1)
                self.norm_pairs = b * PAIRS + ((g - 1) * 2 + 2 if k == 0 else half(5) + 1)
                self.pv_tile = b * per + (self.pv_local if k == 1 else
                                          (g + ((j - (3 if j % 2 else 4)) // 4)))

        def ordered(text):
            return [(w.rstrip("0123"), int(w[-1]) if w[-1].isdigit() else 0) for w in text.split()]

        def heads(eng, k, b, work):
            for j in range(4):
                work(Step(k, b, 0, j))
            with eng.Fori(1, H // 4) as g:
                for j in range(4):
                    work(Step(k, b, g, j))
            for j in range(4):
                work(Step(k, b, H // 4, j))

        PE_ORDER = [ordered("score0 score1 sums score2 score3 turn0 turn1 values0 turn2 turn3 values1"),
                    ordered("score0 score1 sums score2 turn0 turn1 score3 values0 turn2 turn3 values1")]
        ACT_ORDER = [ordered("exp0 copy0 exp1 sums copy2 exp2 exp3"),
                     ordered("exp0 copy0 exp1 sums copy2 exp2 exp3")]
        DVE_ORDER = [ordered("normalise max0 max1 inverse copy1 max2 max3 copy3")] * 2

        def attn_pe(k, b):
            a = at[k]

            def step(s):
                def score(q):
                    hold(nc.tensor, "pe", (a.mx, a.ex)[k], s.n * QT + q + 1 - QT + CS)
                    if k == 0:
                        R = 6 * HD0 + 1
                        nc.tensor.matmul(PS[:, q, :], q_stack[0:R, s.t, q * P:(q + 1) * P], k_stack[0:R, s.t, :],
                                         start=True, stop=True).then_inc(a.s, 1)
                    else:
                        nc.tensor.matmul(PS[:, q, :], q16[:, s.t, q * P:(q + 1) * P], k16[:, s.t, :],
                                         start=True, stop=False)
                        nc.tensor.matmul(PS[:, q, :], q16[:, s.t, q * P:(q + 1) * P], kl_stack[:, s.t, :],
                                         start=False, stop=True).then_inc(a.s, 1)

                def turn_probs(kt):
                    m = s.n - 1
                    if kt == 0:
                        nc.tensor.wait_ge(a.ex, m * QT + QT + CS)
                    nc.tensor.wait_ge((a.ea, a.ed)[kt % 2], m * (QT // 2) + kt // 2 + CE)
                    for qq in range(QT):
                        mm = nc.tensor.transpose(PS[:, 4 + kt % 2, qq * P:(qq + 1) * P],
                                                 probs[s.last_slot % 2][:, qq * L + kt * P:qq * L + (kt + 1) * P],
                                                 ident[:, :])
                    mm.then_inc(a.t, 1)

                def weigh_values(kt):
                    if kt == 0:
                        both = (s.pv_pair * 2 + 2) * (QT // 2) + CE
                        nc.tensor.wait_ge(a.ea, both)
                        nc.tensor.wait_ge(a.ed, both)
                        nc.tensor.wait_ge(a.vst, s.pv_pair * 2 + 2)
                        if k == 1 or not s.pv_odd:
                            nc.tensor.wait_ge(a.o, s.pv_tile + C1)
                    for h in range(2):
                        slot = 2 * s.pv_odd + h
                        row = (slot * OW[0], h * OW[1])[k]
                        mm = nc.tensor.matmul(PS[row:row + OW[k], 6, :], v_heads[k][:, slot, kt, :],
                                              probsT[k][slot][:, kt * L:(kt + 1) * L],
                                              start=(kt == 0), stop=(kt == QT - 1))
                    if kt == QT - 1:
                        mm.then_inc(a.pv, 1)

                def turn_sums():
                    nc.tensor.wait_ge(a.rep, s.rt_pairs + C2)
                    nc.tensor.wait_ge(a.re, s.rt_tile + C1)
                    for q in range(QT):
                        mm = nc.tensor.transpose(PS[:, 7, q * P:(q + 1) * P],
                                                 sum_rep[k][:, q * P:(q + 1) * P], ident[:, :])
                    mm.then_inc(a.rt, 1)

                if k == 1 and s.peeled and s.t == 3:
                    nc.tensor.wait_ge(a.stack_rest, (b + 1) * STACK1_REST)
                for what, n in PE_ORDER[k]:
                    if what == "score" and s.scores:
                        score(n)
                    elif what == "turn" and s.turned:
                        turn_probs(n)
                    elif what == "sums" and s.rt:
                        turn_sums()
                    elif what == "values" and s.pv:
                        weigh_values(s.pv_kts[n])

            heads(nc.tensor, k, b, step)

        def evac_probsT(eng, k, s, kt):
            a = at[k]
            if kt < 2:
                eng.wait_ge(a.pv, s.last_pair - 1 + C2)
            eng.wait_ge(a.t, (s.n - 1) * QT + kt + 1 + CS)
            dst, src = probsT[k][s.last_slot][:, kt * L:(kt + 1) * L], PS[:, 4 + kt % 2, :]
            if eng is nc.scalar:
                nc.scalar.activation(dst, src, ACT.Copy).then_inc(a.ea, 1)
            else:
                nc.vector.tensor_copy(dst, src).then_inc(a.ed, 1)

        def attn_act(k, b):
            a = at[k]

            def step(s):
                def exponentials(q):
                    if q == 0:
                        nc.scalar.wait_ge(a.ri, s.pair - 1 + C2)
                        if k == 1:
                            nc.scalar.wait_ge(a.t, (s.n - 1) * QT + CS)
                    if k == 1 and q == QT // 2 and s.peeled and s.t == 1:
                        nc.scalar.wait_ge(a.stack_rest, (b + 1) * STACK1_REST)
                    nc.scalar.wait_ge(a.mx, s.n * QT + q + 1 + CS)
                    p = probs[s.slot % 2][:, q * L:(q + 1) * L]
                    nc.scalar.activation(p, p if k == 0 else PS[:, q, :], ACT.Exp,
                                         bias=negmax[:, s.slot % 2, q:q + 1], scale=(-1.0, 1.0)[k],
                                         accum_out=rsum[:, s.slot, q:q + 1]).then_inc(a.ex, 1)

                def copy_sums():
                    nc.scalar.wait_ge(a.rt, s.rt_tile + 1 + C1)
                    nc.scalar.wait_ge(a.o, s.rt_tile + C1)
                    nc.scalar.activation(sum_T[k], PS[:, 7, :], ACT.Copy).then_inc(a.re, 1)

                for what, n in ACT_ORDER[k]:
                    if what == "exp" and s.scores:
                        exponentials(n)
                    elif what == "copy" and s.turned:
                        evac_probsT(nc.scalar, k, s, n)
                    elif what == "sums" and s.rt:
                        copy_sums()

            heads(nc.scalar, k, b, step)

        def attn_dve(k, b):
            a = at[k]

            def step(s):
                par = s.slot % 2

                def maximum(q):
                    if k == 0 and q == 0:
                        nc.vector.wait_ge(a.t, (s.n - 1) * QT + CS)
                        nc.vector.wait_ge(a.bias, s.n + 1)
                    nc.vector.wait_ge(a.ex, (s.n - 2) * QT + q + 1 + CS)
                    if k == 0:
                        hold(nc.vector, "dve", a.s, s.n * QT + q + 1)
                        nc.vector.tensor_tensor_reduce(probs[par][:, q * L:(q + 1) * L], PS[:, q, :],
                                                       bias_ring[:, par * RB + q * L:par * RB + (q + 1) * L],
                                                       -1.0, 3e38, ALU.add, ALU.min,
                                                       negmax[:, par, q:q + 1]).then_inc(a.mx, 1)
                    else:
                        nc.vector.wait_ge(a.s, s.n * QT + q + 1)
                        nc.vector.tensor_reduce(negmax[:, par, q:q + 1], PS[:, q, :], AX.X, ALU.max,
                                                negate=True).then_inc(a.mx, 1)

                def invert():
                    nc.vector.wait_ge(a.ex, (s.inv_pair + 1) * 2 * QT + CS)
                    nc.vector.wait_ge(a.rep, s.inv_pair - 1 + C2)
                    two = slice(s.inv_slot, s.inv_slot + 2)
                    nc.vector.reciprocal(rinv[:, two, :], rsum[:, two, :]).then_inc(a.ri, 1)

                def normalise():
                    nc.vector.wait_ge(a.re, s.norm_tile + 1 + C1)
                    nc.vector.wait_ge(a.pv, s.norm_pairs + C2)
                    nc.vector.tensor_tensor(oT[:, s.norm_local, :], PS[:, 6, :], sum_T[k], ALU.mult)\
                        .then_inc(a.o, 1)

                for what, n in DVE_ORDER[k]:
                    if what == "max" and s.scores:
                        maximum(n)
                    elif what == "copy" and s.turned:
                        evac_probsT(nc.vector, k, s, n)
                    elif what == "inverse" and s.inv:
                        invert()
                    elif what == "normalise" and s.norm:
                        normalise()

            heads(nc.vector, k, b, step)

        def attn_pool(k, b):
            a = at[k]
            w = (HD0, HD1)[k]

            def bias(i, par):
                n = b * H + i
                hold(nc.gpsimd, "pool", a.mx, (n - 1) * QT + CS)
                nc.gpsimd.tensor_copy(scale_now[:, par:par + 1], tscale[:, bass.ds(i, 1)]).then_inc(a.scl, 1)
                hold(nc.gpsimd, "pool", a.scl, n + 1)
                nc.gpsimd.tensor_scalar(bias_ring[:, par * RB:(par + 1) * RB], dist, scale_now[:, par:par + 1],
                                        -1.0, ALU.mult, ALU.mult).then_inc(a.bias, 1)

            def step(s):
                if k == 0 and s.scores:
                    if s.j == 0:
                        bias(s.t, 0)
                    if s.j < 3:
                        bias(s.t + 1, (s.j + 1) % 2)
                if s.turned:
                    hold(nc.gpsimd, "pool", a.pv, s.last_pair - 1 + C2)
                    nc.gpsimd.tensor_copy(v_heads[k][:, s.last_slot, :, 0:w],
                                          vals[k][:, :, bass.ds((s.t - 1) * w, w)]).then_inc(a.vst, 1)
                if s.inv:
                    hold(nc.gpsimd, "pool", a.ri, s.inv_pair + 1 + C2)
                    if k == 1:
                        hold(nc.gpsimd, "pool", a.rt, s.inv_pair + C1)
                    elif s.inv_slot == 0:
                        hold(nc.gpsimd, "pool", a.rt, s.inv_tile + C1)
                    per_tile = (4, 2)[k]
                    dst = sum_rep[k].rearrange("p (q h w) -> p q h w", q=QT, h=per_tile)
                    at_h = s.inv_slot if k == 0 else 0
                    for h in range(2):
                        nc.gpsimd.tensor_copy(dst[:, :, at_h + h, :],
                                              rinv[:, s.inv_slot + h, :].unsqueeze(2).broadcast_to([P, QT, OW[k]]))\
                            .then_inc(a.reph, 1)
                    hold(nc.gpsimd, "pool", a.reph, (s.inv_pair + 1) * 2)
                    nc.gpsimd.sem_inc(a.rep, 1)

            hold(nc.gpsimd, "pool", a.vs, (b + 1) * (QT, 2 * QT)[k])
            heads(nc.gpsimd, k, b, step)

        def out_pe(k, b):
            a = at[k]
            jt, w = ((JT0, wout0), (JT, wout1))[k]
            nc.tensor.wait_ge(a.o, (b + 1) * jt + C1)
            for q in range(QT):
                for j in range(jt):
                    mm = nc.tensor.matmul(PS[:, 2 + q, 0:D], oT[:, j, q * P:(q + 1) * P], w[:, j, :],
                                          start=(j == 0), stop=(j == jt - 1))
                mm.then_inc(a.pr, 1)

        def out_dve(k, b):
            a = at[k]
            for q in range(QT):
                nc.vector.wait_ge(a.pr, b * QT + q + 1)
                old = xtile(b, q)
                new = old if k == 0 else xs[:, q, :]
                nc.vector.tensor_tensor(new, PS[:, 2 + q, 0:D], old, ALU.add).then_inc(a.xa, 1)

        f0 = {n: sem("p0_" + n) for n in ("hi", "f", "r", "mid", "lo", "stored")}

        def proj0_pe(b):
            a = at[0]
            nc.tensor.wait_ge(ln[0].hT, (b + 1) * C)
            for m in range(4):
                for c in range(C):
                    mm = nc.tensor.matmul(PS[:, m, :], wqkv0[:, c, m * P:(m + 1) * P], hT[:, c, :],
                                          start=(c == 0), stop=(c == C - 1))
                mm.then_inc(a.qk, 1)
            for q in range(QT):
                for c in range(C):
                    mm = nc.tensor.matmul(PS[:, 4 + q, 0:D], hT[:, c, q * P:(q + 1) * P],
                                          wqkv0[:, c, 2 * D:3 * D], start=(c == 0), stop=(c == C - 1))
                mm.then_inc(a.v, 1)

        def proj0_high_act(b):
            for m in range(4):
                nc.scalar.wait_ge(f0["f"], b * 4 + m + 1)
                nc.scalar.activation(split0[0][:, m, :], rest0[:, m, :], ACT.Copy).then_inc(f0["hi"], 1)

        def proj0_rest_act(b):
            a = at[0]
            for m in range(4):
                nc.scalar.wait_ge(f0["r"], b * 4 + m + 1)
                nc.scalar.activation(split0[1][:, m, :], rest0[:, m, :], ACT.Copy).then_inc(f0["mid"], 1)
            for q in range(QT):
                nc.scalar.wait_ge(a.v, b * QT + q + 1)
                nc.scalar.activation(vals[0][:, q, :], PS[:, 4 + q, 0:D], ACT.Copy).then_inc(a.vs, 1)

        def proj0_dve(b):
            a = at[0]
            for m in range(4):
                nc.vector.wait_ge(a.qk, b * 4 + m + 1)
                nc.vector.tensor_scalar(rest0[:, m, :], PS[:, m, :], (HD0 ** -0.5 if m < 2 else 1.0), None,
                                        ALU.mult).then_inc(f0["f"], 1)
                nc.vector.wait_ge(f0["hi"], b * 4 + m + 1)
                nc.vector.tensor_tensor(rest0[:, m, :], rest0[:, m, :], split0[0][:, m, :],
                                        ALU.subtract).then_inc(f0["r"], 1)

        def proj0_pool(b):
            for m in range(4):
                nc.gpsimd.wait_ge(f0["mid"], b * 4 + m + 1)
                nc.gpsimd.tensor_tensor(split0[2][:, m, :], rest0[:, m, :], split0[1][:, m, :],
                                        ALU.subtract).then_inc(f0["lo"], 1)

        Q_PARTS, K_PARTS = (0, 0, 1, 1, 0, 2), (0, 1, 0, 1, 2, 0)

        def stacks0_sp(b):
            a = at[0]
            for part, s in enumerate(("hi", "mid", "lo")):
                hold(nc.sync, "sp", f0[s], (b + 1) * 4)
                nc.sync.dma_start(qk_parts[part].rearrange("(m p) l -> p m l", p=P), split0[part])\
                    .then_inc(f0["stored"], 16)
            hold(nc.sync, "sp", f0["stored"], (b + 1) * 48)
            for r in range(6):
                for stack, parts, base in ((q_stack, Q_PARTS, 0), (k_stack, K_PARTS, 2 * P)):
                    nc.sync.dma_start(stack[r * HD0:(r + 1) * HD0, :, :],
                                      qk_parts[parts[r], base:base + 2 * P, :].rearrange("(h d) l -> d h l", d=HD0))\
                        .then_inc(a.stack, 16)
            nc.sync.dma_start(k_stack[6 * HD0:6 * HD0 + 1, :, :],
                              pen_rows[:, bass.ds(b * L, L)].unsqueeze(1).broadcast_to([1, H, L])).then_inc(a.stack, 16)

        STACK0 = 13 * 16

        ff = {n: sem("ff_" + n) for n in ("h", "g", "y", "x", "b")}

        def ffn_pe(b):
            nc.tensor.wait_ge(ln[1].hT, (b + 1) * C)
            for f in range(FT):
                if f >= 4:
                    nc.tensor.wait_ge(ff["g"], b * FT + f - 3)
                for c in range(C):
                    mm = nc.tensor.matmul(PS[:, f % 4, :], w1[:, c, f * P:(f + 1) * P], hT[:, c, :],
                                          start=(c == 0), stop=(c == C - 1))
                mm.then_inc(ff["h"], 1)
            nc.tensor.wait_ge(ff["g"], (b + 1) * FT)
            for q in range(QT):
                for f in range(FT):
                    mm = nc.tensor.matmul(PS[:, 4 + q, 0:D], aT[:, f, q * P:(q + 1) * P], w2[:, f, :],
                                          start=(f == 0), stop=(f == FT - 1))
                mm.then_inc(ff["y"], 1)

        def ffn_act(b):
            for f in range(FT):
                nc.scalar.wait_ge(ff["h"], b * FT + f + 1)
                nc.scalar.activation(aT[:, f, :], PS[:, f % 4, :], ACT.Gelu_apprx_tanh,
                                     bias=col["L0_cond_b1"][:, f:f + 1]).then_inc(ff["g"], 1)

        def ffn_dve(b):
            for q in range(QT):
                xq = x[:, bass.ds(b * QT + q, 1), :].rearrange("p a d -> p (a d)")
                nc.vector.wait_ge(ff["y"], b * QT + q + 1)
                nc.vector.tensor_tensor(xq, PS[:, 4 + q, 0:D], xq, ALU.add).then_inc(ff["x"], 1)
                nc.vector.wait_ge(ff["x"], b * QT + q + 1)
                nc.vector.tensor_tensor(xq, xq, b2b[:, :], ALU.add).then_inc(ff["b"], 1)

        p1 = {n: sem("p1_" + n) for n in ("mm", "sq", "sum", "std", "rstd", "qn", "tr", "hi", "f", "lo")}
        NS = 4 * QT

        def where1(n):
            cc, q = n // QT, n % QT
            return cc // 2, (cc % 2) * (G8 // 2), q

        def proj1_pe(b):
            a = at[1]

            def values(n):
                q, half = n // 2, n % 2
                if n >= 2:
                    nc.tensor.wait_ge(a.vs, b * 2 * QT + n - 1)
                for c in range(C):
                    mm = nc.tensor.matmul(PS[:, 6 + half, :], hT[:, c, q * P:(q + 1) * P],
                                          wqkv1[:, c, 2 * W1V + half * CH:2 * W1V + (half + 1) * CH],
                                          start=(c == 0), stop=(c == C - 1))
                mm.then_inc(a.v, 1)

            nc.tensor.wait_ge(ln[2].hT, (b + 1) * C)
            for n in range(NS + 3):
                if n < NS:
                    q = n % QT
                    if n >= 4:
                        nc.tensor.wait_ge(p1["qn"], b * NS + n - 3)
                    for c in range(C):
                        mm = nc.tensor.matmul(PS[:, n % 4, :], hT[:, c, q * P:(q + 1) * P],
                                              wqkv1[:, c, (n // QT) * CH:(n // QT + 1) * CH],
                                              start=(c == 0), stop=(c == C - 1))
                    mm.then_inc(p1["mm"], 1)
                if n >= 3:
                    m = n - 3
                    nc.tensor.wait_ge(p1["qn"], b * NS + m + 1)
                    if m >= 2:
                        nc.tensor.wait_ge(p1["f"], b * NS + m - 1)
                    elif m == 1 and not (isinstance(b, int) and b == 0):
                        nc.tensor.wait_ge(g["logits"], b)
                    for pr in range(G8 // 2):
                        mm = nc.tensor.transpose(PS[:, 4 + m % 2, pr * P:(pr + 1) * P],
                                                 qn1[m % 2][:, pr * P:(pr + 1) * P], ident[:, :])
                    mm.then_inc(p1["tr"], 1)
                if n < NS and n % 4 == 3:
                    values(n // 4)
            for n in range(NS // 4, 2 * QT):
                values(n)

        def proj1_act(b):
            a = at[1]

            def values(v):
                q, half = v // 2, v % 2
                nc.scalar.wait_ge(a.v, b * 2 * QT + v + 1)
                nc.scalar.activation(vals[1][:, q, half * CH:(half + 1) * CH], PS[:, 6 + half, :], ACT.Copy)\
                    .then_inc(a.vs, 1)

            for n in range(NS + 4):
                if n < NS:
                    nc.scalar.wait_ge(p1["mm"], b * NS + n + 1)
                    if n >= 2:
                        nc.scalar.wait_ge(p1["sum"], b * NS + n - 1)
                    nc.scalar.activation(sq1[n % 2], PS[:, n % 4, :], ACT.Square).then_inc(p1["sq"], 1)
                if 1 <= n <= NS:
                    m = n - 1
                    nc.scalar.wait_ge(p1["sum"], b * NS + m + 1)
                    if m >= 2:
                        nc.scalar.wait_ge(p1["rstd"], b * NS + m - 1)
                    nc.scalar.activation(std8[:, m % 2, :], ssum[:, m % 2, :], ACT.Sqrt, bias=eps[:, :],
                                         scale=1.0 / HD1).then_inc(p1["std"], 1)
                if n >= 4:
                    m = n - 4
                    w, pair, q = where1(m)
                    nc.scalar.wait_ge(p1["f"], b * NS + m + 1)
                    nc.scalar.activation(hi1[:, w, pair:pair + G8 // 2, q * P:(q + 1) * P],
                                         f1b[m % 2].rearrange("p (c l) -> p c l", l=P), ACT.Copy)\
                        .then_inc(p1["hi"], 1)
                if n >= 4 and n % 4 == 0 and n <= NS:
                    values(n // 4 - 1)
            for v in range(NS // 4, 2 * QT):
                values(v)

        def proj1_dve(b):
            for n in range(NS + 3):
                if n < NS:
                    r = n % 2
                    nc.vector.wait_ge(p1["sq"], b * NS + n + 1)
                    if n >= 2:
                        nc.vector.wait_ge(p1["std"], b * NS + n - 1)
                    nc.vector.tensor_reduce(ssum[:, r, :], sq1[r].rearrange("p (h d) -> p h d", d=HD1),
                                            AX.X, ALU.add).then_inc(p1["sum"], 1)
                if 1 <= n <= NS:
                    m = n - 1
                    r = m % 2
                    nc.vector.wait_ge(p1["std"], b * NS + m + 1)
                    if m >= 2:
                        nc.vector.wait_ge(p1["qn"], b * NS + m - 1)
                    nc.vector.reciprocal(rstd8[:, r, :], std8[:, r, :]).then_inc(p1["rstd"], 1)
                    nc.vector.wait_ge(p1["rstd"], b * NS + m + 1)
                    if m >= 2:
                        nc.vector.wait_ge(p1["tr"], b * NS + m - 1)
                    nc.vector.tensor_tensor(qn1[r].rearrange("p (h d) -> p h d", d=HD1),
                                            PS[:, m % 4, :].rearrange("p (h d) -> p h d", d=HD1),
                                            rstd8[:, r, :].unsqueeze(2).broadcast_to([P, G8, HD1]), ALU.mult)\
                        .then_inc(p1["qn"], 1)
                if n >= 3:
                    m = n - 3
                    w = where1(m)[0]
                    nc.vector.wait_ge(p1["tr"], b * NS + m + 1)
                    if m >= 2:
                        nc.vector.wait_ge(p1["lo"], b * NS + m - 1)
                    nc.vector.tensor_scalar(f1b[m % 2], PS[:, 4 + m % 2, :], qkf[:, 2 * w:2 * w + 1],
                                            qkf[:, 2 * w + 1:2 * w + 2], ALU.mult, ALU.add).then_inc(p1["f"], 1)

        def proj1_pool(b):
            for m in range(NS):
                w, pair, q = where1(m)
                nc.gpsimd.wait_ge(p1["hi"], b * NS + m + 1)
                nc.gpsimd.wait_ge(p1["f"], b * NS + m + 1)
                nc.gpsimd.tensor_tensor(lo1[:, w, pair:pair + G8 // 2, q * P:(q + 1) * P],
                                        f1b[m % 2].rearrange("p (c l) -> p c l", l=P),
                                        hi1[:, w, pair:pair + G8 // 2, q * P:(q + 1) * P], ALU.subtract)\
                    .then_inc(p1["lo"], 1)

        def stacks1_sp(b):
            a = at[1]

            def place(stack, row, src, w, some, signal):
                for odd in range(2):
                    nc.sync.dma_start(stack[row:row + HD1, 2 * some.start + odd:2 * some.stop:2, :],
                                      src[odd * HD1:(odd + 1) * HD1, w, some, :]).then_inc(signal, 16)

            every, parts = slice(0, PAIRS), [slice(0, G8 // 2), slice(G8 // 2, PAIRS)]
            hold(nc.sync, "sp", p1["lo"], b * NS + NS // 2)
            place(q16, 0, hi1, 0, every, a.stack)
            place(q16, HD1, lo1, 0, every, a.stack)
            for n, (some, signal) in enumerate(zip(parts, (a.stack, a.stack_rest))):
                hold(nc.sync, "sp", p1["lo"], b * NS + (3 + n) * QT)
                for row in (0, HD1):
                    place(k16, row, hi1, 1, some, signal)
                    place(kl_stack, row, lo1, 1, some, signal)

        STACK1, STACK1_REST = 12 * 16, 8 * 16

        g = {n: sem("gate_" + n) for n in ("xT", "xTs", "mm", "logits", "max", "sub", "exp", "sum", "inv", "gate", "row",
                                           "stored")}

        def tokens_pe(b):
            nc.tensor.wait_ge(at[1].xa, (b + 1) * QT)
            for c in range(C):
                for q in range(QT):
                    mm = nc.tensor.transpose(PS[:, 6 + c, q * P:(q + 1) * P], xs[:, q, c * P:(c + 1) * P],
                                             ident[:, :])
                mm.then_inc(g["xT"], 1)

        def tokens_act(b):
            for c in range(C):
                nc.scalar.wait_ge(g["xT"], b * C + c + 1)
                nc.scalar.activation(xT[:, c, :], PS[:, 6 + c, :], ACT.Copy).then_inc(g["xTs"], 1)

        def gate_pe(b):
            nc.tensor.wait_ge(g["xTs"], (b + 1) * C)
            for q in range(QT):
                for c in range(C):
                    mm = nc.tensor.matmul(PS[:, 5, q * E:(q + 1) * E], xT[:, c, q * P:(q + 1) * P], wgate[:, c, :],
                                          start=(c == 0), stop=(c == C - 1))
            mm.then_inc(g["mm"], 1)

        def logits_act(b):
            nc.scalar.wait_ge(g["mm"], b + 1)
            nc.scalar.activation(logits[:, :, :], PS[:, 5, 0:QT * E].rearrange("p (q e) -> p q e", e=E), ACT.Copy)\
                .then_inc(g["logits"], 1)

        def gate_act(b):
            nc.scalar.wait_ge(g["sub"], b + 1)
            nc.scalar.activation(gexp[:, :, :], gexp[:, :, :], ACT.Exp).then_inc(g["exp"], 1)

        def gate_dve(b):
            nc.vector.wait_ge(g["logits"], b + 1)
            nc.vector.tensor_reduce(gmax[:, :], logits[:, :, :], AX.X, ALU.max).then_inc(g["max"], 1)
            nc.vector.wait_ge(g["max"], b + 1)
            nc.vector.tensor_tensor(gexp[:, :, :], logits[:, :, :], gmax[:, :].unsqueeze(2).broadcast_to([P, QT, E]),
                                    ALU.subtract).then_inc(g["sub"], 1)
            nc.vector.wait_ge(g["exp"], b + 1)
            nc.vector.tensor_reduce(gsum[:, :], gexp[:, :, :], AX.X, ALU.add).then_inc(g["sum"], 1)
            nc.vector.wait_ge(g["sum"], b + 1)
            nc.vector.reciprocal(gmax[:, :], gsum[:, :]).then_inc(g["inv"], 1)
            nc.vector.wait_ge(g["inv"], b + 1)
            nc.vector.tensor_tensor(gates[:, bass.ds(b * QT, QT), :], gexp[:, :, :],
                                    gmax[:, :].unsqueeze(2).broadcast_to([P, QT, E]), ALU.mult)\
                .then_inc(g["gate"], 1)
            nc.vector.tensor_tensor(xn[:, :, D:RW], gexp[:, :, :],
                                    gmax[:, :].unsqueeze(2).broadcast_to([P, QT, E]), ALU.mult)\
                .then_inc(g["row"], 1)

        def gate_sp(b):
            tiles = out.rearrange("b (q p) d -> p (b q) d", p=P)
            hold(nc.sync, "sp", at[1].xa, (b + 1) * QT)
            nc.sync.dma_start(tiles[:, bass.ds(b * QT, QT), :], xs[:, :, :]).then_inc(g["stored"], 16)
            hold(nc.sync, "sp", ln[3].xn, (b + 1) * QT)
            hold(nc.sync, "sp", g["row"], b + 1)
            nc.sync.dma_start(rows.rearrange("(n p) w -> p n w", p=P)[:, bass.ds(b * QT, QT), :], xn[:, :, :])\
                .then_inc(g["stored"], 16)
            hold(nc.sync, "sp", g["stored"], (b + 2) * 32)

        def xtile(b, q):
            return x[:, bass.ds(b * QT + q, 1), :].rearrange("p a d -> p (a d)")

        ro = {n: sem("route_" + n) for n in ("b2", "consts", "pick", "spread", "gates", "rep", "cand", "count", "ok", "n", "more",
                                            "prefix", "above", "level", "need", "above_n", "level_n", "taken")}
        R_CONSTS = 5 * 16

        def route_pe():
            nc.tensor.wait_ge(ro["spread"], 1)
            for n in range(NT):
                mm = nc.tensor.transpose(PS[:, n // QT, (n % QT) * P:(n % QT + 1) * P],
                                         above_n[:, n * P:(n + 1) * P], ident[:, :])
            mm.then_inc(ro["gates"], 1)
            nc.tensor.wait_ge(ro["consts"], R_CONSTS)
            with nc.tensor.Fori(0, ST // 2) as two:
                for k in (2 * two, 2 * two + 1):
                    nc.tensor.wait_ge(ro["ok"], k + 1)
                    nc.tensor.matmul(PS[:, 7, 0:1], same[:, :], enough[:, :], start=True, stop=True)\
                        .then_inc(ro["n"], 1)

        def route_act():
            nc.scalar.wait_ge(ro["gates"], 1)
            nc.scalar.activation(gate_rep, PS[:, 0:QT, :].rearrange("p a b -> p (a b)"), ACT.Copy)\
                .then_inc(ro["rep"], 1)

        def route_dve():
            v = nc.vector
            v.wait_ge(g["gate"], B)
            v.tensor_copy(above_n.rearrange("p (n e l) -> p (n e) l", n=NT, e=E),
                          gates[:, :, :].rearrange("p n e -> p (n e)").unsqueeze(2).broadcast_to([P, NT * E, LANES]))\
                .then_inc(ro["spread"], 1)
            v.wait_ge(ro["consts"], R_CONSTS)
            v.tensor_copy(pick, pick_f).then_inc(ro["pick"], 1)
            v.memset(prefix[:, :], 0).then_inc(ro["prefix"], 1)
            v.wait_ge(ro["rep"], 1)
            def search(k):
                v.wait_ge(ro["prefix"], k + 1)
                v.tensor_tensor(cand[:, :], prefix[:, :], lanes[:, bass.ds(k, 1)], ALU.bitwise_or)\
                    .then_inc(ro["cand"], 1)
                v.wait_ge(ro["cand"], k + 1)
                v.tensor_scalar(level, gate_rep, cand[:, :].bitcast(fp32), None, ALU.is_ge, ALU.add,
                                accum_out=count[:, :]).then_inc(ro["count"], 1)
                v.wait_ge(ro["count"], k + 1)
                v.tensor_scalar(enough[:, :], count[:, :], CAP - 0.5, None, ALU.is_ge).then_inc(ro["ok"], 1)
                v.wait_ge(ro["n"], k + 1)
                v.tensor_scalar(more[:, :], PS[:, 7, 0:1], -1.0, steps[:, bass.ds(k, 1)], ALU.add, ALU.mult)\
                    .then_inc(ro["more"], 1)
                v.wait_ge(ro["more"], k + 1)
                v.tensor_tensor(prefix[:, :], prefix[:, :], more[:, :], ALU.bitwise_or).then_inc(ro["prefix"], 1)

            with v.Fori(0, ST // 2) as two:
                search(2 * two)
                search(2 * two + 1)
            least = prefix[:, :].bitcast(fp32)
            v.wait_ge(ro["prefix"], ST + 1)
            v.tensor_scalar(above, gate_rep, least, None, ALU.is_gt).then_inc(ro["above"], 1)
            v.tensor_scalar(level, gate_rep, least, None, ALU.is_equal).then_inc(ro["level"], 1)
            v.wait_ge(ro["above"], 1)
            v.tensor_tensor_scan(above_n, above, above, 0.0, ALU.add, ALU.max).then_inc(ro["above_n"], 1)
            v.wait_ge(ro["level"], 1)
            v.tensor_tensor_scan(level_n, level, level, 0.0, ALU.add, ALU.max).then_inc(ro["level_n"], 1)
            v.wait_ge(ro["level_n"], 1)
            v.wait_ge(ro["above_n"], 1)
            v.tensor_scalar(need[:, :], above_n[:, B * L - 1:B * L], -1.0, float(CAP), ALU.mult, ALU.add)\
                .then_inc(ro["need"], 1)
            v.wait_ge(ro["need"], 1)
            v.scalar_tensor_tensor(out=taken_n, in0=level_n, scalar=need[:, 0:1], in1=above_n,
                                   op0=ALU.min, op1=ALU.add).then_inc(ro["taken"], 1)

        mo = {n: sem("moe_" + n) for n in ("w0", "w1", "taken", "idx_f", "idx", "xg0", "xg1", "kept", "tr", "gT", "h", "act", "y", "b",
                                          "yw", "add", "added")}
        FE = F1 // P

        def index_pe(e):
            if not (isinstance(e, int) and e == 0):
                hold(nc.tensor, "pe", mo["idx_f"], e * HALVES)
            for n in range(QT):
                mm = nc.tensor.matmul(PS[:, n, :], pick[:, bass.ds(e * P, P)], taken_n[:, n * CH:(n + 1) * CH],
                                      start=True, stop=True)
            mm.then_inc(mo["taken"], 1)

        def index_dve(e, ring_at):
            v = nc.vector
            v.wait_ge(mo["taken"], e + 1)
            if not (isinstance(e, int) and e == 0):
                v.wait_ge(mo["idx"], e)
            for h in range(HALVES):
                v.tensor_scalar((above, level)[h], PS[:, 0:QT, :].rearrange("p a b -> p (a b)"), slot[:, h:h + 1], None,
                                ALU.is_le, ALU.add, accum_out=idx_f[:, ring_at, h:h + 1]).then_inc(mo["idx_f"], 1)

        def index_out_dve(e, ring_at):
            v = nc.vector
            v.wait_ge(mo["idx_f"], (e + 1) * HALVES)
            if not (isinstance(e, int) and e < 2):
                v.wait_ge(mo["tr"], e - 1)
            v.tensor_copy(idx[:, ring_at, :], idx_f[:, ring_at, :]).then_inc(mo["idx"], 1)

        def keep_index_dve(e, ring_at):
            nc.vector.wait_ge(mo["added"], e + 1)
            nc.vector.tensor_copy(idx_out[:, ring_at, :], idx[:, ring_at, :]).then_inc(mo["kept"], 1)

        def gather_pool(e, ring_at):
            hold(nc.gpsimd, "pool", mo["idx"], e + 1)
            if not (isinstance(e, int) and e < 2):
                hold(nc.gpsimd, "pool", mo["yw"], (e - 1) * HALVES)
            for h in range(HALVES):
                nc.gpsimd.indirect_dma_start(
                    out=xg[:, ring_at, h, :], out_offset=None, in_=rows[:, :],
                    in_offset=bass.IndirectOffsetOnAxis(ap=idx[:, ring_at, h:h + 1], axis=0))\
                    .then_inc(mo[f"xg{ring_at}"], 16)

        def of_ring(e, ring_at):
            return e // 2 if isinstance(e, int) else (e - ring_at) // 2

        def turn_pe(e, ring_at):
            nc.tensor.wait_ge(mo[f"xg{ring_at}"], (of_ring(e, ring_at) + 1) * HALVES * 16)
            if not (isinstance(e, int) and e == 0):
                nc.tensor.wait_ge(mo["gT"], e * C)
            for c in range(C):
                for h in range(HALVES):
                    mm = nc.tensor.transpose(PS[:, 4, c * CAP + h * P:c * CAP + (h + 1) * P],
                                             xg[:, ring_at, h, c * P:(c + 1) * P], ident[:, :])
            mm.then_inc(mo["tr"], 1)

        def turn_act(e, ring_at):
            for c in range(C):
                nc.scalar.wait_ge(mo["tr"], e + 1)
                nc.scalar.activation(gT[:, ring_at, c, :], PS[:, 4, c * CAP:(c + 1) * CAP], ACT.Identity,
                                     bias=col["L1_cond_mlp_b"][:, c:c + 1], scale=col["L1_cond_mlp_g"][:, c:c + 1])\
                    .then_inc(mo["gT"], 1)

        def hidden_pe(e, ring_at):
            nc.tensor.wait_ge(mo["gT"], (e + 1) * C)
            nc.tensor.wait_ge(mo[f"w{ring_at}"], (of_ring(e, ring_at) + 1) * 32)
            for f in range(FE):
                if f % 2 == 0:
                    nc.tensor.wait_ge(mo["act"], e * FE + f - 2 + 4)
                for c in range(C):
                    mm = nc.tensor.matmul(PS[:, 5 + f // 2 % 2, f % 2 * CAP:(f % 2 + 1) * CAP],
                                          fc1[ring_at][:, c, f * P:(f + 1) * P], gT[:, ring_at, c, :],
                                          start=(c == 0), stop=(c == C - 1))
                if f % 2 == 1:
                    mm.then_inc(mo["h"], 1)

        def hidden_act(e, ring_at):
            for f in range(FE):
                hold(nc.scalar, "act", mo["h"], e * (FE // 2) + f // 2 + 1)
                nc.scalar.activation(yT[:, ring_at, f, :], PS[:, 5 + f // 2 % 2, f % 2 * CAP:(f % 2 + 1) * CAP],
                                     ACT.Gelu_apprx_tanh, bias=col["L1_cond_b1s"][:, bass.ds(e * FE + f, 1)])\
                    .then_inc(mo["act"], 1)

        def result_pe(e, ring_at, h):
            if h == 0:
                nc.tensor.wait_ge(mo["act"], (e + 1) * FE + 4)
                nc.tensor.wait_ge(mo["b"], (e + 1) * HALVES)
            for f in range(FE):
                mm = nc.tensor.matmul(PS[:, 7, h * D:(h + 1) * D], yT[:, ring_at, f, h * P:(h + 1) * P],
                                      fc2[ring_at][:, f, :], start=(f == 0), stop=(f == FE - 1))
            if h == HALVES - 1:
                mm.then_inc(mo["y"], 1)

        def result_dve(e, ring_at):
            v = nc.vector
            v.wait_ge(mo["y"], e + 1)
            for h in range(HALVES):
                v.tensor_tensor(yout[:, ring_at, h, :], PS[:, 7, h * D:(h + 1) * D], b2all[:, bass.ds(e * D, D)],
                                ALU.add).then_inc(mo["b"], 1)
            for h in range(HALVES):
                v.wait_ge(mo["b"], e * HALVES + h + 1 + HALVES)
                v.tensor_scalar(yout[:, ring_at, h, :], yout[:, ring_at, h, :],
                                xg[:, ring_at, h, bass.ds(D + e, 1)], None, ALU.mult).then_inc(mo["yw"], 1)

        def scatter_pool(e, ring_at):
            hold(nc.gpsimd, "pool", mo["kept"], e + 1)
            hold(nc.gpsimd, "pool", mo["yw"], (e + 1) * HALVES)
            for h in range(HALVES):
                nc.gpsimd.indirect_dma_start(
                    out=out.rearrange("b l d -> (b l) d"),
                    out_offset=bass.IndirectOffsetOnAxis(ap=idx_out[:, ring_at, h:h + 1], axis=0),
                    in_=yout[:, ring_at, h, :], in_offset=None, compute_op=ALU.add).then_inc(mo["add"], 16)
            nc.gpsimd.wait_ge(mo["add"], (e + 1) * 32)
            nc.gpsimd.sem_inc(mo["added"], 1)

        def expert_loop(eng, work):
            with eng.Fori(0, E // 2 - 1) as pair:
                work(2 * pair, 0, True, True)
                work(2 * pair + 1, 1, True, True)
            work(E - 2, 0, True, False)
            work(E - 1, 1, False, False)

        def experts_pe():
            index_pe(0)
            index_pe(1)
            turn_pe(0, 0)

            def work(e, r, one, two):
                hidden_pe(e, r)
                if two:
                    index_pe(e + 2)
                result_pe(e, r, 0)
                if one:
                    turn_pe(e + 1, 1 - r)
                result_pe(e, r, 1)

            expert_loop(nc.tensor, work)

        def experts_act():
            turn_act(0, 0)

            def work(e, r, one, two):
                hidden_act(e, r)
                if one:
                    turn_act(e + 1, 1 - r)

            expert_loop(nc.scalar, work)

        def experts_dve():
            for e in range(2):
                index_dve(e, e)
                index_out_dve(e, e)

            def work(e, r, one, two):
                keep_index_dve(e, r)
                if two:
                    index_dve(e + 2, r)
                    index_out_dve(e + 2, r)
                result_dve(e, r)

            expert_loop(nc.vector, work)

        def experts_pool():
            gather_pool(0, 0)
            gather_pool(1, 1)

            def work(e, r, one, two):
                if two:
                    gather_pool(e + 2, r)
                scatter_pool(e, r)

            expert_loop(nc.gpsimd, work)

        def weights_sp(e, ring_at):
            nc.sync.dma_start(fc1[ring_at], t["L1_cond_fc1s"][bass.ds(e, 1)].rearrange("a (c p) f -> p (a c) f", p=P))\
                .then_inc(mo[f"w{ring_at}"], 16)
            nc.sync.dma_start(fc2[ring_at], t["L1_cond_fc2s"][bass.ds(e, 1)].rearrange("a (f p) d -> p (a f) d", p=P))\
                .then_inc(mo[f"w{ring_at}"], 16)

        def experts_sp():
            hold(nc.sync, "sp", at[1].s, B * H * QT)
            for e in range(2):
                weights_sp(e, e)
            with nc.sync.Fori(0, E // 2 - 1) as pair:
                for ring_at in range(2):
                    hold(nc.sync, "sp", mo["y"], 2 * pair + ring_at + 1)
                    weights_sp(2 * pair + ring_at + 2, ring_at)

        def centre_dve():
            nc.vector.wait_ge(s_wq1, 16)
            nc.vector.tensor_scalar(qkf[:, 0:2], qkg[:, 0:2], 0.5, None, ALU.mult).then_inc(w_centred, 1)
            nc.vector.tensor_scalar(qkf[:, 2:4], qkg[:, 2:4], 2.0 * HD1 ** -0.5, None, ALU.mult).then_inc(w_centred, 1)
            for c in range(C):
                wc = wqkv1[:, c, 0:2 * W1V].rearrange("p (h d) -> p h d", d=HD1)
                nc.vector.tensor_reduce(wmean[:, c, :], wc, AX.X, ALU.add).then_inc(cond_vec, 1)
                nc.vector.wait_ge(cond_vec, 9 * C + 2 * c + 1)
                nc.vector.tensor_scalar(wmean[:, c, :], wmean[:, c, :], 1.0 / HD1, None, ALU.mult).then_inc(cond_vec, 1)
                nc.vector.wait_ge(cond_vec, 9 * C + 2 * c + 2)
                nc.vector.tensor_tensor(wc, wc, wmean[:, c, :].unsqueeze(2).broadcast_to([P, 2 * H, HD1]),
                                  ALU.subtract).then_inc(w_centred, 2)

        def over_sequences(eng, work):
            with eng.Fori(0, B - 1) as b:
                work(b, True)
            work(B - 1, False)

        N_VEC, N_W0 = 5, 10
        block = ctx.enter_context(nc.Block())

        @block.sync
        def _(sp):
            sp.sem_inc(g["stored"], 32)
            sp.dma_start(condT[:, :, :], t["condT"].rearrange("(c p) b -> p c b", p=P)).then_inc(s_vec, 16)
            sp.dma_start(wt, t["L0_cond_Wt"].rearrange("(c p) n -> p c n", p=P)).then_inc(s_vec, 16)
            sp.dma_start(wada, t["L1_cond_W_ada"].rearrange("(c p) n -> p c n", p=P)).then_inc(s_vec, 16)
            sp.dma_start(cols[:, :], t["cols"]).then_inc(s_vec, 16)
            x_tiles = t["x"].rearrange("b (q p) d -> p (b q) d", p=P)
            sp.dma_start(x[:, 0:QT, :], x_tiles[:, 0:QT, :]).then_inc(s_vec, 16)
            sp.dma_start(wqkv0, t["L0_cond_Wqkv"].rearrange("(c p) n -> p c n", p=P)).then_inc(s_wq0, 16)
            sp.dma_start(mask_u8[:, :], t["mask_BxS_bf1"].rearrange("(a b) l -> a (b l)", a=1)).then_inc(s_mask, 16)
            sp.dma_start(b2b[:, :], t["L0_cond_b2"].partition_broadcast(P)).then_inc(s_w0, 16)
            sp.dma_start(tscale[:, :], t["L0_cond_torus_scale"].partition_broadcast(P)).then_inc(s_w0, 16)
            sp.dma_start(dist[:, :].rearrange("p (q l) -> p q l", q=QT),
                         t["L0_cond_torus_dist"].rearrange("a (q p) l -> p (a q) l", p=P)).then_inc(s_w0, 16)
            sp.dma_start(x[:, QT:NT, :], x_tiles[:, QT:NT, :]).then_inc(s_w0, 16)
            sp.wait_ge(s_const, 5)
            for h in range(4):
                sp.dma_start(wout0[h * OW[0]:h * OW[0] + HD0, :, :],
                             t["L0_cond_Wout"].rearrange("(j h d) n -> h d j n", h=4, d=HD0)[h]).then_inc(s_w0, 16)
            sp.wait_ge(s_pen, 1)
            sp.dma_start(pen_rows, pen).then_inc(s_mask, 16)
            sp.dma_start(w1, t["L0_cond_W1"].rearrange("(c p) n -> p c n", p=P)).then_inc(s_w0, 16)
            sp.dma_start(w2, t["L0_cond_W2"].rearrange("(c p) n -> p c n", p=P)).then_inc(s_w0, 16)
            sp.wait_ge(s_mask, 2 * 16)
            with sp.Fori(0, B) as b:
                stacks0_sp(b)
            sp.wait_ge(at[0].o, B * JT0 + C1)
            sp.dma_start(wqkv1, t["L1_cond_Wqkv"].rearrange("(c p) n -> p c n", p=P)).then_inc(s_wq1, 16)
            for dst, name in ((lanes, "lanes"), (steps, "steps"), (same, "same"), (slot, "slot")):
                sp.dma_start(dst[:, :], t[name]).then_inc(ro["consts"], 16)
            stacks1_sp(0)

            def layer1(b, ahead):
                if ahead:
                    stacks1_sp(b + 1)
                gate_sp(b)

            over_sequences(sp, layer1)
            sp.dma_start(pick_f, t["pick"]).then_inc(ro["consts"], 16)
            experts_sp()

        @block.gpsimd
        def _(pool):
            pool.memset(ident[:, :], 0.0).then_inc(s_ident, 1)
            pool.memset(mhalf[:, :], -0.5).then_inc(s_const, 1)
            pool.memset(eps[:, :], EPS).then_inc(s_const, 1)
            pool.memset(v_now[:, :], 0.0).then_inc(s_const, 1)
            credits(pool, "pool")
            pool.wait_ge(s_ident, 1)
            pool.affine_select(out=ident[:, :], in_=ident[:, :], compare_op=ALU.not_equal, fill=1.0,
                               base=0, pattern=[[-1, P]], channel_multiplier=1).then_inc(s_ident, 1)
            pool.dma_start(wgate[:, :, :], t["L1_cond_Wgate"].rearrange("(c p) n -> p c n", p=P)).then_inc(s_w1, 16)
            pool.dma_start(wout1[:, :, :], t["L1_cond_Wout"].rearrange("(c p) n -> p c n", p=P)).then_inc(s_w1, 16)
            pool.wait_ge(s_const, 5)
            norm_pool(0, 0)
            proj0_pool(0)
            pool.wait_ge(s_w0, N_W0 * 16)

            def layer0(b, ahead):
                attn_pool(0, b)
                if ahead:
                    norm_pool(0, b + 1)
                norm_pool(1, b)
                if ahead:
                    proj0_pool(b + 1)

            over_sequences(pool, layer0)
            norm_pool(2, 0)
            proj1_pool(0)

            def layer1(b, ahead):
                attn_pool(1, b)
                if ahead:
                    norm_pool(2, b + 1)
                    proj1_pool(b + 1)
                norm_pool(3, b)

            over_sequences(pool, layer1)
            pool.sem_inc(mo["added"], 2)
            pool.wait_ge(at[1].pv, B * PAIRS + C2)
            pool.dma_start(b2all, t["L1_cond_b2s"].rearrange("e d -> (e d)").partition_broadcast(P))\
                .then_inc(ro["b2"], 16)
            pool.wait_ge(g["stored"], (B + 1) * 32)
            experts_pool()
            pool.wait_ge(mo["add"], E * 32)

        @block.scalar
        def _(act):
            credits(act, "act")
            act.wait_ge(s_vec, N_VEC * 16)
            act.wait_ge(s_const, 5)
            act.activation(gelT[:, :, :], condT[:, :, :], ACT.Gelu_apprx_tanh).then_inc(cond_act, 1)
            act.activation(silT[:, :, :], condT[:, :, :], ACT.Silu).then_inc(cond_act, 1)
            act.wait_ge(cond_vec, 12)
            norm_act(0, 0)
            proj0_high_act(0)
            proj0_rest_act(0)

            def layer0(b, ahead):
                attn_act(0, b)
                if ahead:
                    norm_act(0, b + 1)
                    proj0_high_act(b + 1)
                norm_act(1, b)
                if ahead:
                    proj0_rest_act(b + 1)
                ffn_act(b)

            over_sequences(act, layer0)
            norm_act(2, 0)
            proj1_act(0)

            def layer1(b, ahead):
                attn_act(1, b)
                tokens_act(b)
                if ahead:
                    norm_act(2, b + 1)
                logits_act(b)
                if ahead:
                    proj1_act(b + 1)
                gate_act(b)

            over_sequences(act, layer1)
            route_act()
            act.sem_inc(mo["act"], 4)
            experts_act()

        @block.tensor
        def _(pe):
            credits(pe, "pe")
            pe.wait_ge(s_ident, 2)
            pe.wait_ge(s_vec, N_VEC * 16)
            pe.wait_ge(cond_act, 2)
            for m in range(3 * C):
                w, act_in, off = (wt, gelT, m * P) if m < 2 * C else (wada, silT, (m - 2 * C) * P)
                for c in range(C):
                    mm = pe.matmul(PS[:, 7, m * B:(m + 1) * B], w[:, c, off:off + P], act_in[:, c, :],
                                   start=(c == 0), stop=(c == C - 1))
            mm.then_inc(cond_mm, 1)
            pe.wait_ge(cond_vec, 12)
            norm_pe(0, 0)
            pe.wait_ge(s_wq0, 16)
            proj0_pe(0)
            pe.wait_ge(s_w0, N_W0 * 16)

            def layer0(b, ahead):
                pe.wait_ge(at[0].stack, (b + 1) * STACK0)
                pe.wait_ge(at[0].vs, (b + 1) * QT)
                attn_pe(0, b)
                out_pe(0, b)
                if ahead:
                    norm_pe(0, b + 1)
                    pe.wait_ge(at[0].xa, (b + 1) * QT)
                    proj0_pe(b + 1)
                    pe.wait_ge(f0["f"], (b + 2) * 4)
                norm_pe(1, b)
                ffn_pe(b)
                pe.wait_ge(ff["x"], (b + 1) * QT)

            over_sequences(pe, layer0)
            pe.wait_ge(s_w1, 2 * 16)
            pe.wait_ge(w_centred, 2 + 2 * C)
            norm_pe(2, 0)
            proj1_pe(0)
            pe.wait_ge(at[1].vs, 2 * QT)

            def layer1(b, ahead):
                pe.wait_ge(at[1].stack, (b + 1) * STACK1)
                attn_pe(1, b)
                out_pe(1, b)
                tokens_pe(b)
                if ahead:
                    norm_pe(2, b + 1)
                gate_pe(b)
                if ahead:
                    proj1_pe(b + 1)
                    pe.wait_ge(at[1].vs, (b + 2) * 2 * QT)

            over_sequences(pe, layer1)
            route_pe()
            pe.wait_ge(ro["taken"], 1)
            pe.wait_ge(ro["pick"], 1)
            pe.wait_ge(ro["rep"], 1)
            experts_pe()

        @block.vector
        def _(dve):
            credits(dve, "dve")
            dve.memset(q_stack[6 * HD0:6 * HD0 + 1, :, :], 1.0).then_inc(s_const, 1)
            dve.memset(wout0, 0.0).then_inc(s_const, 1)
            dve.wait_ge(s_vec, N_VEC * 16)
            norm_dve(0, 0, xtile)
            dve.wait_ge(cond_mm, 1)
            modes = [(col["L0_cond_bt"][:, m:m + 1]) for m in range(2 * C)] + [col["L1_cond_b_ada"][:, c:c + 1] for c in range(C)]
            for m in range(3 * C):
                dve.tensor_scalar(tp[:, m, :], PS[:, 7, m * B:(m + 1) * B], modes[m],
                                  1.0 if m < C else 0.0, ALU.add, ALU.add).then_inc(cond_vec, 1)
            dve.wait_ge(cond_vec, 3 * C)
            for c in range(C):
                gc, bc = col["L0_cond_ln1_g"][:, c:c + 1], col["L0_cond_ln1_b"][:, c:c + 1]
                dve.tensor_scalar(gain[0][:, c, :], tp[:, c, :], gc, None, ALU.mult).then_inc(cond_vec, 1)
                dve.scalar_tensor_tensor(out=shift[0][:, c, :], in0=tp[:, c, :], scalar=bc, in1=tp[:, C + c, :],
                                         op0=ALU.mult, op1=ALU.add).then_inc(cond_vec, 1)
                dve.tensor_scalar(shift[2][:, c, :], tp[:, 2 * C + c, :], col["L1_cond_ln1_b"][:, c:c + 1], None,
                                  ALU.add).then_inc(cond_vec, 1)
            for c in range(C):
                for n, name in ((1, "L0_cond_ln2"), (2, "L1_cond_ln1")):
                    dve.tensor_scalar(gain[n][:, c, :], tp[:, c, :], 0.0, col[name + "_g"][:, c:c + 1],
                                      ALU.mult, ALU.add).then_inc(cond_vec, 1)
                dve.tensor_scalar(shift[1][:, c, :], tp[:, c, :], 0.0, col["L0_cond_ln2_b"][:, c:c + 1],
                                  ALU.mult, ALU.add).then_inc(cond_vec, 1)
            dve.wait_ge(s_mask, 16)
            dve.tensor_scalar(pen[:, :], mask_u8[:, :], 1.0, -NEG, ALU.subtract, ALU.mult).then_inc(s_pen, 1)
            proj0_dve(0)
            dve.wait_ge(s_w0, N_W0 * 16)

            def layer0(b, ahead):
                attn_dve(0, b)
                if ahead:
                    norm_dve(0, b + 1, xtile)
                out_dve(0, b)
                hold(dve, "dve", at[0].xa, (b + 1) * QT)
                if ahead:
                    hold(dve, "dve", ln[0].tr, (b + 2) * C)
                norm_dve(1, b, xtile)
                if ahead:
                    proj0_dve(b + 1)
                if not ahead:
                    centre_dve()
                ffn_dve(b)

            over_sequences(dve, layer0)
            dve.wait_ge(ff["b"], B * QT)
            norm_dve(2, 0, xtile)
            proj1_dve(0)

            def layer1(b, ahead):
                attn_dve(1, b)
                hold(dve, "dve", g["stored"], (b + 1) * 32)
                if ahead:
                    norm_dve(2, b + 1, xtile)
                out_dve(1, b)
                if ahead:
                    proj1_dve(b + 1)
                hold(dve, "dve", at[1].xa, (b + 1) * QT)
                norm_dve(3, b, lambda b, q: xs[:, q, :])
                gate_dve(b)

            over_sequences(dve, layer1)
            route_dve()
            dve.sem_inc(mo["b"], HALVES)
            dve.wait_ge(ro["b2"], 16)
            experts_dve()


FEATURE_COLS = [("L0_cond_ln1_g", 2), ("L0_cond_ln1_b", 2), ("L0_cond_ln2_g", 2), ("L0_cond_ln2_b", 2),
                ("L1_cond_ln1_g", 2), ("L1_cond_ln1_b", 2), ("L1_cond_mlp_g", 2), ("L1_cond_mlp_b", 2),
                ("L1_cond_b_ada", 2), ("L0_cond_bt", 4), ("L0_cond_b1", 8), ("L1_cond_b1s", 64)]
_PAIR_COLS = ["L1_cond_qn_g", "L1_cond_qn_b", "L1_cond_kn_g", "L1_cond_kn_b"]
_PLAIN = ["x", "mask_BxS_bf1", "L0_cond_torus_dist", "L0_cond_Wqkv", "L0_cond_Wout", "L0_cond_torus_scale",
          "L0_cond_W1", "L0_cond_W2", "L0_cond_b2", "L0_cond_Wt", "L1_cond_b2s"]
_TURNED = {"condT": "cond_1024", "L1_cond_W_ada": "L1_cond_W_ada", "L1_cond_Wqkv": "L1_cond_Wqkv",
           "L1_cond_Wout": "L1_cond_Wout", "L1_cond_Wgate": "L1_cond_Wgate", "L1_cond_fc1s": "L1_cond_fc1s",
           "L1_cond_fc2s": "L1_cond_fc2s"}


def kernel(**inputs):
    import numpy as _np
    import concourse.bacc as _bacc
    from concourse import mybir as _mybir
    from concourse.bass_utils import run_bass_kernel_spmd as _run

    nc = _bacc.Bacc("TRN2", target_bir_lowering=False, num_devices=1)
    laid = {n: _np.asarray(inputs[n]) for n in _PLAIN}
    laid.update({n: _np.swapaxes(_np.asarray(inputs[src]), -1, -2) for n, src in _TURNED.items()})
    laid["cols"] = _np.concatenate(
        [_np.asarray(inputs[n]).reshape(-1, 128).T for n, _ in FEATURE_COLS]
        + [_np.tile(_np.asarray(inputs[n]), 2)[:, None] for n in _PAIR_COLS], axis=1)
    part, ex = _np.arange(128), laid["L1_cond_b2s"].shape[0]
    lane, shifts = part % (128 // ex), 28 - 4 * _np.arange(8)
    laid["lanes"] = (_np.minimum(lane[:, None], _np.where(shifts == 28, 7, 15)) << shifts).astype(_np.int32)
    laid["steps"] = _np.broadcast_to((2.0 ** shifts).astype(_np.float32), (128, 8))
    laid["same"] = (part[:, None] // (128 // ex) == part // (128 // ex)).astype(_np.float32)
    laid["slot"] = (part[:, None] + 128 * _np.arange(2)).astype(_np.float32)
    laid["pick"] = _np.repeat((part[:, None] == (128 // ex) * _np.arange(ex)).astype(_np.float32), 128, axis=1)
    arrays, aps = {}, {}
    for name, a in laid.items():
        a = _np.ascontiguousarray(a)
        arrays[f"in_{name}"] = a
        aps[name] = nc.dram_tensor(f"in_{name}", a.shape, _mybir.dt.from_np(a.dtype), kind="ExternalInput").ap()
    out = nc.dram_tensor("out_0", laid["x"].shape, _mybir.dt.float32, kind="ExternalOutput").ap()
    cond_seq_kernel(nc, aps, out)
    r = _run(nc, [arrays], core_ids=[0])
    return r.results[0]["out_0"]
```
